# Optimizing a Trainium2 kernel written in Bass

```python
import numpy as np
import jax
import jax.numpy as jnp

def _softmax(x, axis=-1):
    return jax.nn.softmax(x, axis=axis)

def _gelu(x):
    return jax.nn.gelu(x, approximate=True)

def _silu(x):
    return jax.nn.silu(x)

def _sigmoid(x):
    return jax.nn.sigmoid(x)

def _layernorm(x, axis=-1, eps=1e-05):
    m = jnp.mean(x, axis=axis, keepdims=True)
    v = jnp.var(x, axis=axis, keepdims=True)
    return (x - m) / jnp.sqrt(v + eps)

def _scatter_add(tgt, idx, src, axis=0):
    return tgt.at[idx].add(src)

def _segment_sum(src, seg, n):
    return jax.ops.segment_sum(src, seg, n)
kernel_name = 'mk_macaron_d4_jaxref_r8_278f67'

def setup_inputs(seed: int=0):
    np.random.seed(seed)
    _w = jnp.asarray

    def _L0_attn_setup():
        import jax, jax.numpy as jnp
        import numpy as np
        B, T, D = (1, 128, 128)
        HQ, HKV, HK, HV = (16, 4, 64, 64)
        KW = 4
        N_CHEB = 2
        CHEB_DAMP = 0.25
        EPS = 1e-06

        def _gka_core(x, Wq, Wk, Wv, Wconv, Wa, Walpha, Wb, A_log, dt_bias, norm_w, Wo):
            Bx, Tx, _ = x.shape
            qkv = jnp.concatenate([x @ Wq, x @ Wk, x @ Wv], axis=-1)
            pad = jnp.pad(qkv, ((0, 0), (KW - 1, 0), (0, 0)))
            conv = sum((pad[:, i:i + Tx, :] * Wconv[:, i] for i in range(KW)))
            qkv = jax.nn.silu(conv)
            q, k, v = jnp.split(qkv, [HQ * HK, HQ * HK + HKV * HK], axis=-1)
            q = q.reshape(Bx, Tx, HQ, HK)
            k = k.reshape(Bx, Tx, HKV, HK)
            v = v.reshape(Bx, Tx, HKV, HV)
            g = -jnp.exp(A_log) * jax.nn.softplus(x @ Wa + dt_bias)
            alpha = jax.nn.sigmoid(x @ Walpha)
            beta = jax.nn.sigmoid(x @ Wb)
            v = v * beta[..., None]
            k = k / (jnp.linalg.norm(k, axis=-1, keepdims=True) + EPS)
            q = q * HK ** (-0.5)
            rep = HQ // HKV
            k = jnp.repeat(k, rep, axis=2)
            v = jnp.repeat(v, rep, axis=2)

            def step(carry, inp):
                Hkk, Hkv = carry
                qt, kt, vt, gt = inp
                d = jnp.exp(gt)[..., None, None]
                Hkk = d * Hkk + kt[..., :, None] * kt[..., None, :]
                Hkv = d * Hkv + kt[..., :, None] * vt[..., None, :]
                xq = qt
                for _ in range(N_CHEB):
                    xq = qt - CHEB_DAMP * jnp.einsum('bhk,bhkl->bhl', xq, Hkk)
                ot = jnp.einsum('bhk,bhkv->bhv', xq, Hkv)
                return ((Hkk, Hkv), ot)
            tm = lambda a: jnp.moveaxis(a, 1, 0)
            init = (jnp.zeros((Bx, HQ, HK, HK), jnp.float32), jnp.zeros((Bx, HQ, HK, HV), jnp.float32))
            _, o = jax.lax.scan(step, init, (tm(q), tm(k), tm(v), tm(g)))
            o = jnp.moveaxis(o, 0, 1)
            o = o * alpha[..., None]
            o = o * jax.lax.rsqrt(jnp.mean(o * o, axis=-1, keepdims=True) + EPS) * norm_w
            return o.reshape(Bx, Tx, HQ * HV) @ Wo
        key = jax.random.key(seed)
        ks = jax.random.split(key, 12)
        C = HQ * HK + HKV * HK + HKV * HV
        s = lambda d: 1.0 / np.sqrt(d)
        inp = {'x': jax.random.normal(ks[0], (B, T, D), jnp.float32), 'Wq': jax.random.normal(ks[1], (D, HQ * HK), jnp.float32) * s(D), 'Wk': jax.random.normal(ks[2], (D, HKV * HK), jnp.float32) * s(D), 'Wv': jax.random.normal(ks[3], (D, HKV * HV), jnp.float32) * s(D), 'Wconv': jax.random.normal(ks[4], (C, KW), jnp.float32) * 0.2, 'Wa': jax.random.normal(ks[5], (D, HQ), jnp.float32) * s(D), 'Walpha': jax.random.normal(ks[6], (D, HQ), jnp.float32) * s(D), 'Wb': jax.random.normal(ks[7], (D, HKV), jnp.float32) * s(D), 'A_log': jnp.log(jax.random.uniform(ks[8], (HQ,), jnp.float32, 1.0, 16.0)), 'dt_bias': jax.random.normal(ks[9], (HQ,), jnp.float32) * 0.5, 'norm_w': jnp.ones((HV,), jnp.float32), 'Wo': jax.random.normal(ks[10], (HQ * HV, D), jnp.float32) * s(HQ * HV)}
        return inp
    _L0_attn_in = _L0_attn_setup()

    def _L0_ffn_setup():
        import jax, jax.numpy as jnp
        import numpy as np
        B, S, D, E = (2, 256, 128, 8)
        key = jax.random.key(seed)
        ks = jax.random.split(key, 5)
        x = jax.random.normal(ks[0], (B, S, D), dtype=jnp.float32)
        router_w = jax.random.normal(ks[1], (E, D), dtype=jnp.float32) * 0.02
        router_b = jnp.zeros((E,), dtype=jnp.float32)
        expert_w = jax.random.normal(ks[2], (E, D, D), dtype=jnp.float32) * 0.02
        expert_b = jnp.zeros((E, D), dtype=jnp.float32)
        return {'x': x, 'router_w': router_w, 'router_b': router_b, 'expert_w': expert_w, 'expert_b': expert_b}
    _L0_ffn_in = _L0_ffn_setup()

    def _L1_attn_setup():
        import jax, jax.numpy as jnp
        import numpy as np
        FEATURE_DIM = 128
        NUM_HEADS = 16
        QKV_DIM = 128
        HEAD_DIM = QKV_DIM // NUM_HEADS
        key = jax.random.key(seed)
        ks = jax.random.split(key, 5)
        x = jax.random.normal(ks[0], (4, 256, FEATURE_DIM), dtype=jnp.float32)
        s_in = 1.0 / np.sqrt(FEATURE_DIM)
        s_out = 1.0 / np.sqrt(QKV_DIM)
        W_in = jax.random.uniform(ks[1], (FEATURE_DIM, 3 * QKV_DIM), jnp.float32, -s_in, s_in)
        b_in = jax.random.uniform(ks[2], (3 * QKV_DIM,), jnp.float32, -s_in, s_in)
        W_out = jax.random.uniform(ks[3], (QKV_DIM, FEATURE_DIM), jnp.float32, -s_out, s_out)
        b_out = jax.random.uniform(ks[4], (FEATURE_DIM,), jnp.float32, -s_out, s_out)
        return {'x': x, 'W_in': W_in, 'b_in': b_in, 'W_out': W_out, 'b_out': b_out}
    _L1_attn_in = _L1_attn_setup()

    def _L1_ffn_setup():
        import jax, jax.numpy as jnp
        import numpy as np
        B, T, D, E, H, K = (2, 256, 128, 8, 512, 2)
        key = jax.random.key(seed)
        ks = jax.random.split(key, 8)
        s = 0.02
        return {'x': jax.random.normal(ks[0], (B, T, D), jnp.float32), 'rw1': jax.random.normal(ks[1], (D, D), jnp.float32) * s, 'rb1': jnp.zeros((D,), jnp.float32), 'rw2': jax.random.normal(ks[2], (D, E), jnp.float32) * s, 'rb2': jnp.zeros((E,), jnp.float32), 'we1': jax.random.normal(ks[3], (E, D, H), jnp.float32) * s, 'be1': jnp.zeros((E, H), jnp.float32), 'we2': jax.random.normal(ks[4], (E, H, D), jnp.float32) * s, 'be2': jnp.zeros((E, D), jnp.float32)}
    _L1_ffn_in = _L1_ffn_setup()

    def _L2_attn_setup():
        import jax, jax.numpy as jnp
        import numpy as np
        MAX_DIST = 8
        GUIDANCE_WEIGHT = 0.4
        EPS_MAG = 1e-06
        EPS_COS = 1e-08
        EPS_WSUM = 1e-08
        key = jax.random.key(seed)
        k1, k2 = jax.random.split(key)
        embeddings = jax.random.normal(k1, (4, 256, 128), dtype=jnp.float32)
        guidance_trajectories = jax.random.normal(k2, (64, 128), dtype=jnp.float32)
        return {'embeddings': embeddings, 'guidance_trajectories': guidance_trajectories}
    _L2_attn_in = _L2_attn_setup()

    def _L2_ffn_setup():
        import jax, jax.numpy as jnp
        import numpy as np
        H = 128
        I = 512
        E = 8
        K = 2
        B, S = (2, 256)

        def _moe_linear(x, router_w, expert_w):
            n_exp = router_w.shape[0]
            logits = x @ router_w.T
            vals, idx = jax.lax.top_k(logits, K)
            probs = jax.nn.softmax(vals, axis=-1)
            onehot = jax.nn.one_hot(idx, n_exp, dtype=x.dtype)
            combine = jnp.einsum('tk,tke->te', probs, onehot)
            out = jnp.zeros((x.shape[0], expert_w.shape[1]), x.dtype)
            for e in range(n_exp):
                out = out + combine[:, e:e + 1] * (x @ expert_w[e].T)
            return out
        key = jax.random.key(seed)
        ks = jax.random.split(key, 7)
        init = lambda k, shape, fan_in: jax.random.normal(k, shape, jnp.float32) / np.float32(np.sqrt(fan_in))
        return {'x': jax.random.normal(ks[0], (B, S, H), jnp.float32), 'router_gate': init(ks[1], (E, H), H), 'w_gate': init(ks[2], (E, I, H), H), 'router_up': init(ks[3], (E, H), H), 'w_up': init(ks[4], (E, I, H), H), 'router_down': init(ks[5], (E, I), I), 'w_down': init(ks[6], (E, H, I), I)}
    _L2_ffn_in = _L2_ffn_setup()

    def _L3_attn_setup():
        import jax, jax.numpy as jnp
        import numpy as np
        B, T, D = (8, 512, 128)

        def _ssm_scan(a_bc, bx):

            def combine(e1, e2):
                a1, u1 = e1
                a2, u2 = e2
                return (a1 * a2, a2 * u1 + u2)
            _, y = jax.lax.associative_scan(combine, (a_bc, bx), axis=1)
            return y
        key = jax.random.key(seed)
        k_x, k_a, k_b, k_w, k_bo = jax.random.split(key, 5)
        x = jax.random.normal(k_x, (B, T, D), dtype=jnp.float32)
        a = jax.random.normal(k_a, (D,), dtype=jnp.float32) * 0.5
        b = jax.random.normal(k_b, (D,), dtype=jnp.float32)
        w_out = jax.random.normal(k_w, (D, D), dtype=jnp.float32) * (1.0 / np.sqrt(D))
        b_out = jax.random.normal(k_bo, (D,), dtype=jnp.float32) * 0.01
        return {'x': x, 'a': a, 'b': b, 'w_out': w_out, 'b_out': b_out}
    _L3_attn_in = _L3_attn_setup()

    def _L3_ffn_setup():
        import jax, jax.numpy as jnp
        import numpy as np
        HIDDEN = 128
        N_ROUTED = 16
        N_SHARED = 2
        TOP_K = 2
        MID_R = HIDDEN // 4
        MID_S = HIDDEN // 2
        key = jax.random.key(seed)
        ks = jax.random.split(key, 8)
        s = 0.02
        return {'x': jax.random.normal(ks[0], (2, 128, HIDDEN), dtype=jnp.float32), 'router_w': jax.random.normal(ks[1], (HIDDEN, N_ROUTED), dtype=jnp.float32) * s, 'wg_r': jax.random.normal(ks[2], (N_ROUTED, HIDDEN, MID_R), dtype=jnp.float32) * s, 'wu_r': jax.random.normal(ks[3], (N_ROUTED, HIDDEN, MID_R), dtype=jnp.float32) * s, 'wd_r': jax.random.normal(ks[4], (N_ROUTED, MID_R, HIDDEN), dtype=jnp.float32) * s, 'wg_s': jax.random.normal(ks[5], (N_SHARED, HIDDEN, MID_S), dtype=jnp.float32) * s, 'wu_s': jax.random.normal(ks[6], (N_SHARED, HIDDEN, MID_S), dtype=jnp.float32) * s, 'wd_s': jax.random.normal(ks[7], (N_SHARED, MID_S, HIDDEN), dtype=jnp.float32) * s}
    _L3_ffn_in = _L3_ffn_setup()
    _d = {'L0_attn_x': _L0_attn_in['x'], 'L0_attn_Wq': _L0_attn_in['Wq'], 'L0_attn_Wk': _L0_attn_in['Wk'], 'L0_attn_Wv': _L0_attn_in['Wv'], 'L0_attn_Wconv': _L0_attn_in['Wconv'], 'L0_attn_Wa': _L0_attn_in['Wa'], 'L0_attn_Walpha': _L0_attn_in['Walpha'], 'L0_attn_Wb': _L0_attn_in['Wb'], 'L0_attn_A_log': _L0_attn_in['A_log'], 'L0_attn_dt_bias': _L0_attn_in['dt_bias'], 'L0_attn_norm_w': _L0_attn_in['norm_w'], 'L0_attn_Wo': _L0_attn_in['Wo'], 'L0_ffn_router_w': _L0_ffn_in['router_w'], 'L0_ffn_router_b': _L0_ffn_in['router_b'], 'L0_ffn_expert_w': _L0_ffn_in['expert_w'], 'L0_ffn_expert_b': _L0_ffn_in['expert_b'], 'L1_attn_W_in': _L1_attn_in['W_in'], 'L1_attn_b_in': _L1_attn_in['b_in'], 'L1_attn_W_out': _L1_attn_in['W_out'], 'L1_attn_b_out': _L1_attn_in['b_out'], 'L1_ffn_rw1': _L1_ffn_in['rw1'], 'L1_ffn_rb1': _L1_ffn_in['rb1'], 'L1_ffn_rw2': _L1_ffn_in['rw2'], 'L1_ffn_rb2': _L1_ffn_in['rb2'], 'L1_ffn_we1': _L1_ffn_in['we1'], 'L1_ffn_be1': _L1_ffn_in['be1'], 'L1_ffn_we2': _L1_ffn_in['we2'], 'L1_ffn_be2': _L1_ffn_in['be2'], 'L2_attn_guidance_trajectories': _L2_attn_in['guidance_trajectories'], 'L2_ffn_router_gate': _L2_ffn_in['router_gate'], 'L2_ffn_w_gate': _L2_ffn_in['w_gate'], 'L2_ffn_router_up': _L2_ffn_in['router_up'], 'L2_ffn_w_up': _L2_ffn_in['w_up'], 'L2_ffn_router_down': _L2_ffn_in['router_down'], 'L2_ffn_w_down': _L2_ffn_in['w_down'], 'L3_attn_a': _L3_attn_in['a'], 'L3_attn_b': _L3_attn_in['b'], 'L3_attn_w_out': _L3_attn_in['w_out'], 'L3_attn_b_out': _L3_attn_in['b_out'], 'L3_ffn_router_w': _L3_ffn_in['router_w'], 'L3_ffn_wg_r': _L3_ffn_in['wg_r'], 'L3_ffn_wu_r': _L3_ffn_in['wu_r'], 'L3_ffn_wd_r': _L3_ffn_in['wd_r'], 'L3_ffn_wg_s': _L3_ffn_in['wg_s'], 'L3_ffn_wu_s': _L3_ffn_in['wu_s'], 'L3_ffn_wd_s': _L3_ffn_in['wd_s']}
    _x0 = _d['L0_attn_x']
    _d['L0_attn_x'] = jax.random.normal(jax.random.fold_in(jax.random.key(seed), 1), (1, 2048, 128), dtype=_x0.dtype)
    del _x0
    return _d

def reference(L0_attn_x, L0_attn_Wq, L0_attn_Wk, L0_attn_Wv, L0_attn_Wconv, L0_attn_Wa, L0_attn_Walpha, L0_attn_Wb, L0_attn_A_log, L0_attn_dt_bias, L0_attn_norm_w, L0_attn_Wo, L0_ffn_router_w, L0_ffn_router_b, L0_ffn_expert_w, L0_ffn_expert_b, L1_attn_W_in, L1_attn_b_in, L1_attn_W_out, L1_attn_b_out, L1_ffn_rw1, L1_ffn_rb1, L1_ffn_rw2, L1_ffn_rb2, L1_ffn_we1, L1_ffn_be1, L1_ffn_we2, L1_ffn_be2, L2_attn_guidance_trajectories, L2_ffn_router_gate, L2_ffn_w_gate, L2_ffn_router_up, L2_ffn_w_up, L2_ffn_router_down, L2_ffn_w_down, L3_attn_a, L3_attn_b, L3_attn_w_out, L3_attn_b_out, L3_ffn_router_w, L3_ffn_wg_r, L3_ffn_wu_r, L3_ffn_wd_r, L3_ffn_wg_s, L3_ffn_wu_s, L3_ffn_wd_s):

    def _L0_attn_ref(x, Wq, Wk, Wv, Wconv, Wa, Walpha, Wb, A_log, dt_bias, norm_w, Wo):
        import jax, jax.numpy as jnp
        import numpy as np
        B, T, D = (1, 128, 128)
        HQ, HKV, HK, HV = (16, 4, 64, 64)
        KW = 4
        N_CHEB = 2
        CHEB_DAMP = 0.25
        EPS = 1e-06

        def _gka_core(x, Wq, Wk, Wv, Wconv, Wa, Walpha, Wb, A_log, dt_bias, norm_w, Wo):
            Bx, Tx, _ = x.shape
            qkv = jnp.concatenate([x @ Wq, x @ Wk, x @ Wv], axis=-1)
            pad = jnp.pad(qkv, ((0, 0), (KW - 1, 0), (0, 0)))
            conv = sum((pad[:, i:i + Tx, :] * Wconv[:, i] for i in range(KW)))
            qkv = jax.nn.silu(conv)
            q, k, v = jnp.split(qkv, [HQ * HK, HQ * HK + HKV * HK], axis=-1)
            q = q.reshape(Bx, Tx, HQ, HK)
            k = k.reshape(Bx, Tx, HKV, HK)
            v = v.reshape(Bx, Tx, HKV, HV)
            g = -jnp.exp(A_log) * jax.nn.softplus(x @ Wa + dt_bias)
            alpha = jax.nn.sigmoid(x @ Walpha)
            beta = jax.nn.sigmoid(x @ Wb)
            v = v * beta[..., None]
            k = k / (jnp.linalg.norm(k, axis=-1, keepdims=True) + EPS)
            q = q * HK ** (-0.5)
            rep = HQ // HKV
            k = jnp.repeat(k, rep, axis=2)
            v = jnp.repeat(v, rep, axis=2)

            def step(carry, inp):
                Hkk, Hkv = carry
                qt, kt, vt, gt = inp
                d = jnp.exp(gt)[..., None, None]
                Hkk = d * Hkk + kt[..., :, None] * kt[..., None, :]
                Hkv = d * Hkv + kt[..., :, None] * vt[..., None, :]
                xq = qt
                for _ in range(N_CHEB):
                    xq = qt - CHEB_DAMP * jnp.einsum('bhk,bhkl->bhl', xq, Hkk)
                ot = jnp.einsum('bhk,bhkv->bhv', xq, Hkv)
                return ((Hkk, Hkv), ot)
            tm = lambda a: jnp.moveaxis(a, 1, 0)
            init = (jnp.zeros((Bx, HQ, HK, HK), jnp.float32), jnp.zeros((Bx, HQ, HK, HV), jnp.float32))
            _, o = jax.lax.scan(step, init, (tm(q), tm(k), tm(v), tm(g)))
            o = jnp.moveaxis(o, 0, 1)
            o = o * alpha[..., None]
            o = o * jax.lax.rsqrt(jnp.mean(o * o, axis=-1, keepdims=True) + EPS) * norm_w
            return o.reshape(Bx, Tx, HQ * HV) @ Wo
        return _gka_core(x, Wq, Wk, Wv, Wconv, Wa, Walpha, Wb, A_log, dt_bias, norm_w, Wo)

    def _L0_ffn_ref(x, router_w, router_b, expert_w, expert_b):
        import jax, jax.numpy as jnp
        import numpy as np
        B, S, D, E = (2, 256, 128, 8)
        logits = jnp.einsum('bsd,ed->bse', x, router_w) + router_b
        probs = jax.nn.softmax(logits, axis=-1)
        weights = jnp.max(probs, axis=-1)
        top1 = jnp.argmax(probs, axis=-1)
        y_all = jnp.einsum('bsd,eod->bseo', x, expert_w) + expert_b
        y = jnp.take_along_axis(y_all, top1[:, :, None, None], axis=2)[:, :, 0, :]
        out = y * weights[:, :, None]
        return out

    def _L1_attn_ref(x, W_in, b_in, W_out, b_out):
        import jax, jax.numpy as jnp
        import numpy as np
        FEATURE_DIM = 128
        NUM_HEADS = 16
        QKV_DIM = 128
        HEAD_DIM = QKV_DIM // NUM_HEADS
        N, L, C = x.shape
        scale = HEAD_DIM ** (-0.5)
        qkv = x @ W_in + b_in
        qkv = qkv.reshape(N, L, 3, NUM_HEADS, HEAD_DIM)
        qkv = jnp.transpose(qkv, (2, 0, 3, 1, 4))
        q, k, v = (qkv[0], qkv[1], qkv[2])
        attn = jnp.einsum('nhqd,nhkd->nhqk', q, k) * scale
        attn = jax.nn.softmax(attn, axis=-1)
        out = jnp.einsum('nhqk,nhkd->nhqd', attn, v)
        out = jnp.transpose(out, (0, 2, 1, 3)).reshape(N, L, QKV_DIM)
        return out @ W_out + b_out

    def _L1_ffn_ref(x, rw1, rb1, rw2, rb2, we1, be1, we2, be2):
        import jax, jax.numpy as jnp
        import numpy as np
        B, T, D, E, H, K = (2, 256, 128, 8, 512, 2)
        b, t, d = x.shape
        xt = x.reshape(b * t, d)
        n = xt.shape[0]
        logits = jax.nn.silu(xt @ rw1 + rb1) @ rw2 + rb2
        _, idx = jax.lax.top_k(logits, K)
        mask = jnp.zeros((n, E), bool).at[jnp.arange(n)[:, None], idx].set(True)
        w = jax.nn.softmax(jnp.where(mask, logits, -jnp.inf), axis=1)
        h = jax.nn.silu(jnp.einsum('nd,edh->enh', xt, we1) + be1[:, None, :])
        eo = jnp.einsum('enh,ehd->end', h, we2) + be2[:, None, :]
        y = xt + jnp.einsum('ne,end->nd', w, eo)
        return y.reshape(b, t, d)

    def _L2_attn_ref(embeddings, guidance_trajectories):
        import jax, jax.numpy as jnp
        import numpy as np
        MAX_DIST = 8
        GUIDANCE_WEIGHT = 0.4
        EPS_MAG = 1e-06
        EPS_COS = 1e-08
        EPS_WSUM = 1e-08
        B, S, D = embeddings.shape
        W = min(MAX_DIST, S - 1)
        diffs = embeddings[:, 1:, :] - embeddings[:, :-1, :]
        pos = jnp.arange(S)[:, None]
        k = jnp.arange(W)[None, :]
        idx = pos - W + k
        valid = (idx >= 0) & (pos >= 1)
        windows = diffs[:, jnp.clip(idx, 0, S - 2), :]
        w = jnp.minimum(pos, W)
        j = k - (W - w)
        lin = jnp.where(w > 1, 0.1 + 0.9 * j / jnp.maximum(w - 1, 1), 0.1)
        pos_weights = jnp.where(valid, lin, 0.0).astype(embeddings.dtype)
        mag = jnp.linalg.norm(windows, axis=-1, keepdims=True)
        is_valid_mag = mag > EPS_MAG
        normed = jnp.where(is_valid_mag, windows / jnp.where(is_valid_mag, mag, 1.0), 0.0)
        mag_weights = jnp.tanh(mag * 2.0)
        combined = pos_weights[None, :, :, None] * mag_weights
        g_norm = jnp.linalg.norm(guidance_trajectories, axis=-1)
        a_norm = jnp.linalg.norm(normed, axis=-1)
        dots = jnp.einsum('bswd,gd->bswg', normed, guidance_trajectories)
        sims = dots / (jnp.maximum(a_norm, EPS_COS)[..., None] * jnp.maximum(g_norm, EPS_COS))
        g_weights = jax.nn.softmax(sims * 2.0, axis=-1)
        influence = jnp.einsum('bswg,gd->bswd', g_weights, guidance_trajectories)
        blended = (1.0 - GUIDANCE_WEIGHT) * normed + GUIDANCE_WEIGHT * influence
        weight_sum = jnp.maximum(combined.sum(axis=2), EPS_WSUM)
        trajectories = (blended * combined).sum(axis=2) / weight_sum
        return trajectories

    def _L2_ffn_ref(x, router_gate, w_gate, router_up, w_up, router_down, w_down):
        import jax, jax.numpy as jnp
        import numpy as np
        H = 128
        I = 512
        E = 8
        K = 2
        B, S = (2, 256)

        def _moe_linear(x, router_w, expert_w):
            n_exp = router_w.shape[0]
            logits = x @ router_w.T
            vals, idx = jax.lax.top_k(logits, K)
            probs = jax.nn.softmax(vals, axis=-1)
            onehot = jax.nn.one_hot(idx, n_exp, dtype=x.dtype)
            combine = jnp.einsum('tk,tke->te', probs, onehot)
            out = jnp.zeros((x.shape[0], expert_w.shape[1]), x.dtype)
            for e in range(n_exp):
                out = out + combine[:, e:e + 1] * (x @ expert_w[e].T)
            return out
        b, s, h = x.shape
        xt = x.reshape(b * s, h)
        g = _moe_linear(xt, router_gate, w_gate)
        u = _moe_linear(xt, router_up, w_up)
        inter = jax.nn.silu(g) * u
        d = _moe_linear(inter, router_down, w_down)
        return d.reshape(b, s, h)

    def _L3_attn_ref(x, a, b, w_out, b_out):
        import jax, jax.numpy as jnp
        import numpy as np
        B, T, D = (8, 512, 128)

        def _ssm_scan(a_bc, bx):

            def combine(e1, e2):
                a1, u1 = e1
                a2, u2 = e2
                return (a1 * a2, a2 * u1 + u2)
            _, y = jax.lax.associative_scan(combine, (a_bc, bx), axis=1)
            return y
        ah = jnp.tanh(a)
        bx = b * x
        a_bc = jnp.broadcast_to(ah, x.shape)
        y = _ssm_scan(a_bc, bx)
        return jnp.einsum('btd,ed->bte', y, w_out) + b_out

    def _L3_ffn_ref(x, router_w, wg_r, wu_r, wd_r, wg_s, wu_s, wd_s):
        import jax, jax.numpy as jnp
        import numpy as np
        HIDDEN = 128
        N_ROUTED = 16
        N_SHARED = 2
        TOP_K = 2
        MID_R = HIDDEN // 4
        MID_S = HIDDEN // 2
        orig_shape = x.shape
        flat = x.reshape(-1, orig_shape[-1])
        gs = jnp.einsum('td,ndm->tnm', flat, wg_s)
        us = jnp.einsum('td,ndm->tnm', flat, wu_s)
        out = jnp.einsum('tnm,nmd->td', jax.nn.silu(gs) * us, wd_s)
        logits = (flat @ router_w).astype(jnp.float32)
        probs = jax.nn.softmax(logits, axis=-1)
        weights, indices = jax.lax.top_k(probs, TOP_K)
        weights = weights / (weights.sum(axis=-1, keepdims=True) + 1e-09)
        weights = weights.astype(x.dtype)
        comb = jnp.sum(jax.nn.one_hot(indices, N_ROUTED, dtype=x.dtype) * weights[..., None], axis=1)
        g = jnp.einsum('td,edm->tem', flat, wg_r)
        u = jnp.einsum('td,edm->tem', flat, wu_r)
        h = jax.nn.silu(g) * u
        h = h * comb[:, :, None]
        out = out + jnp.einsum('tem,emd->td', h, wd_r)
        return out.reshape(orig_shape)
    x = L0_attn_x
    x = x + 0.5 * _L0_ffn_ref(_layernorm(x, axis=-1), L0_ffn_router_w, L0_ffn_router_b, L0_ffn_expert_w, L0_ffn_expert_b)
    x = x + _L0_attn_ref(_layernorm(x, axis=-1), L0_attn_Wq, L0_attn_Wk, L0_attn_Wv, L0_attn_Wconv, L0_attn_Wa, L0_attn_Walpha, L0_attn_Wb, L0_attn_A_log, L0_attn_dt_bias, L0_attn_norm_w, L0_attn_Wo)
    x = x + 0.5 * _L0_ffn_ref(_layernorm(x, axis=-1), L0_ffn_router_w, L0_ffn_router_b, L0_ffn_expert_w, L0_ffn_expert_b)
    x = x + 0.5 * _L1_ffn_ref(_layernorm(x, axis=-1), L1_ffn_rw1, L1_ffn_rb1, L1_ffn_rw2, L1_ffn_rb2, L1_ffn_we1, L1_ffn_be1, L1_ffn_we2, L1_ffn_be2)
    x = x + _L1_attn_ref(_layernorm(x, axis=-1), L1_attn_W_in, L1_attn_b_in, L1_attn_W_out, L1_attn_b_out)
    x = x + 0.5 * _L1_ffn_ref(_layernorm(x, axis=-1), L1_ffn_rw1, L1_ffn_rb1, L1_ffn_rw2, L1_ffn_rb2, L1_ffn_we1, L1_ffn_be1, L1_ffn_we2, L1_ffn_be2)
    x = x + 0.5 * _L2_ffn_ref(_layernorm(x, axis=-1), L2_ffn_router_gate, L2_ffn_w_gate, L2_ffn_router_up, L2_ffn_w_up, L2_ffn_router_down, L2_ffn_w_down)
    x = x + _L2_attn_ref(_layernorm(x, axis=-1), L2_attn_guidance_trajectories)
    x = x + 0.5 * _L2_ffn_ref(_layernorm(x, axis=-1), L2_ffn_router_gate, L2_ffn_w_gate, L2_ffn_router_up, L2_ffn_w_up, L2_ffn_router_down, L2_ffn_w_down)
    x = x + 0.5 * _L3_ffn_ref(_layernorm(x, axis=-1), L3_ffn_router_w, L3_ffn_wg_r, L3_ffn_wu_r, L3_ffn_wd_r, L3_ffn_wg_s, L3_ffn_wu_s, L3_ffn_wd_s)
    x = x + _L3_attn_ref(_layernorm(x, axis=-1), L3_attn_a, L3_attn_b, L3_attn_w_out, L3_attn_b_out)
    x = x + 0.5 * _L3_ffn_ref(_layernorm(x, axis=-1), L3_ffn_router_w, L3_ffn_wg_r, L3_ffn_wu_r, L3_ffn_wd_r, L3_ffn_wg_s, L3_ffn_wu_s, L3_ffn_wd_s)
    return x

_drawn_inputs = setup_inputs


def setup_inputs(seed=0):
    import zlib

    import numpy as np

    out = dict(_drawn_inputs(seed))
    spreads = {'L0_attn_norm_w': (1.0, 0.2),
     'L0_ffn_router_b': (0.0, 0.1),
     'L0_ffn_expert_b': (0.0, 0.289),
     'L1_ffn_rb1': (0.0, 0.8),
     'L1_ffn_rb2': (0.0, 0.1),
     'L1_ffn_be1': (0.0, 0.422),
     'L1_ffn_be2': (0.0, 0.1)}
    factors = {'L1_attn_W_in': 2.915,
     'L1_ffn_rw1': 8.0,
     'L1_ffn_rw2': 8.0,
     'L3_attn_b_out': 8.0,
     'L3_ffn_router_w': 8.0,
     'L3_ffn_wg_r': 8.0,
     'L3_ffn_wu_r': 8.0,
     'L3_ffn_wd_r': 8.0,
     'L3_ffn_wg_s': 8.0,
     'L3_ffn_wu_s': 8.0,
     'L3_ffn_wd_s': 8.0}
    for name, (base, spread) in spreads.items():
        noise = np.random.default_rng([zlib.crc32(name.encode()), seed]).standard_normal(out[name].shape)
        drawn = base * np.exp(spread * noise) if base else spread * noise
        out[name] = jnp.asarray(drawn.astype(out[name].dtype))
    for name, factor in factors.items():
        out[name] = (out[name] * factor).astype(out[name].dtype)
    return out
```

```python
import numpy as np
import concourse.bass as bass
from concourse import mybir
from contextlib import ExitStack

F32 = mybir.dt.float32
BF16 = mybir.dt.bfloat16
ACT = mybir.ActivationFunctionType
ALU = mybir.AluOpType
AX = mybir.AxisListType

P = 128
D = 128
T = 2048
TB = 512
NB = T // TB
TPB = TB // P
LN_EPS = 1e-5
LEAD = 4


class Counter:

    def __init__(self, sem):
        self.sem, self.start = sem, LEAD

    def at(self, n):
        return n + (self.start + 1)


class Kit:

    def __init__(self, nc, stack):
        self.nc, self.stack = nc, stack
        self.counters = {n: Counter(stack.enter_context(nc.semaphore(n))) for n in COUNTERS}
        self.stage_tensors = 0
        psum = stack.enter_context(nc.psum_tensor("psum", [P, 8 * TB], F32))
        self.bank = [psum[:, b * TB:(b + 1) * TB] for b in range(8)]
        self.pair = [psum[:, b * TB:(b + 2) * TB] for b in (2, 4)]

    def sbuf(self, name, shape, dtype=F32):
        return self.stack.enter_context(self.nc.sbuf_tensor(name, shape, dtype))

    def counter(self, name):
        return self.counters[name]

    def fresh(self, name):
        self.stage_tensors += 1
        return f"{name}_{self.stage_tensors}"

    def passed(self, counts):
        for name, n in counts.items():
            self.counters[name].start += n


class Carve:

    def __init__(self, region):
        self.region, self.used = region, 0

    def __call__(self, name, shape, dtype=F32):
        n = int(np.prod(shape[1:])) // (1 if dtype == F32 else 2)
        flat = self.region[0:shape[0], self.used:self.used + n]
        self.used += n
        assert self.used <= self.region.shape[1], name
        if dtype != F32:
            flat = flat.bitcast(dtype)
        names = "abcdef"[:len(shape) - 1]
        sizes = dict(zip(names[1:], shape[2:]))
        return flat.rearrange(f"p ({' '.join(names)}) -> p {' '.join(names)}", **sizes) if len(names) > 1 else flat


class Norm:

    def __init__(self, k, st, xn, left=0, block_only=False):
        self.k, self.xn, self.left, self.block_only = k, xn, left, block_only
        self.square, self.sd = (st(nm, [P, TB]) for nm in ("ln_square", "ln_sd"))
        self.centred = k.counter("ln_centred")
        self.squared = k.counter("ln_squared")
        self.variance = k.counter("ln_variance")
        self.deviation = k.counter("ln_deviation")
        self.normed = k.counter("ln_normed")

    def passed(self):
        self.k.passed({n: NB for n in ("ln_centred", "ln_squared", "ln_variance", "ln_deviation", "ln_normed")})

    def pe_centre(self, pe, n):
        pe.wait_ge(self.normed.sem, self.normed.at(n - 1))
        pe.matmul(self.k.bank[0][:, :], self.k.centre[:, :], self.k.x[:, bass.ts(n, TB)],
                  start=True, stop=True).then_inc(self.centred.sem, 1)

    def act_square(self, act, n):
        act.wait_ge(self.centred.sem, self.centred.at(n))
        act.activation(self.square[:, :], self.k.bank[0][:, :], ACT.Square).then_inc(self.squared.sem, 1)

    def pe_variance(self, pe, n):
        pe.wait_ge(self.squared.sem, self.squared.at(n))
        pe.matmul(self.k.bank[1][:, :], self.k.mean[:, :], self.square[:, :],
                  start=True, stop=True).then_inc(self.variance.sem, 1)

    def act_deviation(self, act, n):
        act.wait_ge(self.variance.sem, self.variance.at(n))
        act.activation(self.sd[:, :], self.k.bank[1][:, :], ACT.Sqrt,
                       bias=self.k.ln_eps[:, :]).then_inc(self.deviation.sem, 1)

    def dve_norm(self, dve, n):
        dve.wait_ge(self.deviation.sem, self.deviation.at(n))
        dve.reciprocal(self.sd[:, :], self.sd[:, :])
        dve.drain()
        here = self.xn[:, :] if self.block_only else self.xn[:, bass.ds(n * TB + self.left, TB)]
        dve.tensor_tensor(here, self.k.bank[0][:, :], self.sd[:, :],
                          ALU.mult).then_inc(self.normed.sem, 1)


class Route:

    def __init__(self, k, st, name, experts, routers, topk, denominator, rows, bias=None):
        self.k, self.E, self.R, self.topk, self.denominator, self.bias = k, experts, routers, topk, denominator, bias
        self.rows = rows
        W = self.W = experts * routers
        G = self.G = TPB * routers
        self.logT = k.logT[name]
        self.tok = st(name + "_tok", [P, TPB, W])
        self.top = st(name + "_top", [P, G])
        self.shift = st(name + "_shift", [P, TPB, W])
        self.expo = st(name + "_expo", [P, TPB, W])
        self.cmp_ge = st(name + "_cmp_ge", [P, G * experts, experts])
        self.cmp_gt = st(name + "_cmp_gt", [P, G * experts, experts])
        self.rank = st(name + "_rank", [P, TPB, W])
        self.sum = st(name + "_sum", [P, 2, G])
        self.comb = st(name + "_comb", [P, TPB, W])
        self.rest = st(name + "_rest", [P, TPB, W])
        self.parts = k.parts[name]
        self.names = [name + "_" + s for s in ("logits", "logits_out", "by_token", "shifted", "exped", "weighed", "turned", "rows")]
        (self.logits, self.logits_out, self.by_token, self.shifted, self.exped, self.weighed,
         self.turned, self.rows_ready) = (k.counter(s) for s in self.names)

    def passed(self):
        self.k.passed({n: NB for n in self.names})

    def act_logits_out(self, act, n):
        act.wait_ge(self.logits.sem, self.logits.at(n))
        src = self.k.bank[1][0:self.W, :]
        if self.bias is None:
            act.activation(self.logT[0:self.W, :], src, ACT.Copy).then_inc(self.logits_out.sem, 1)
        else:
            act.activation(self.logT[0:self.W, :], src, ACT.Identity, bias=self.bias).then_inc(self.logits_out.sem, 1)

    def pe_by_token(self, pe, n):
        pe.wait_ge(self.logits_out.sem, self.logits_out.at(n))
        for j in range(TPB):
            mm = pe.transpose(self.k.bank[1][:, j * P:(j + 1) * P], self.logT[:, j * P:(j + 1) * P],
                              self.k.ident[:, :])
        mm.then_inc(self.by_token.sem, 1)

    def dve_weights(self, dve, n):
        k, E, G, W = self.k, self.E, self.G, self.W
        g = lambda t: t[:, :, :].rearrange("p j (r e) -> p (j r) e", e=E)
        over_e = lambda t: t.unsqueeze(2).to_broadcast([P, G, E])
        tok, shift, expo, rank, comb, rest = map(g, (self.tok, self.shift, self.expo, self.rank, self.comb, self.rest))
        dve.wait_ge(self.by_token.sem, self.by_token.at(n))
        dve.tensor_copy(self.tok[:, :, :], k.bank[1][:, :].rearrange("p (j w) -> p j w", w=P)[:, :, 0:W])
        dve.drain()
        dve.tensor_reduce(self.top[:, :], tok, AX.X, ALU.max)
        mine = tok.unsqueeze(3).to_broadcast([P, G, E, E])
        other = tok.unsqueeze(2).to_broadcast([P, G, E, E])
        ge = self.cmp_ge[:, :, :].rearrange("p (g e) f -> p g e f", e=E)
        gt = self.cmp_gt[:, :, :].rearrange("p (g e) f -> p g e f", e=E)
        dve.drain()
        dve.tensor_tensor(shift, tok, over_e(self.top[:, :]), ALU.subtract).then_inc(self.shifted.sem, 1)
        dve.tensor_tensor(ge, other, mine, ALU.is_ge)
        dve.tensor_tensor(gt, other, mine, ALU.is_gt)
        dve.drain()
        flat = lambda t: t[:, :, :].rearrange("p (g e) f -> p g (e f)", e=E)
        before = k.before[E][:, :].unsqueeze(1).to_broadcast([P, G, E * E])
        after = k.after[E][:, :].unsqueeze(1).to_broadcast([P, G, E * E])
        dve.tensor_tensor(flat(self.cmp_ge), flat(self.cmp_ge), before, ALU.mult)
        dve.tensor_tensor(flat(self.cmp_gt), flat(self.cmp_gt), after, ALU.mult)
        dve.drain()
        dve.tensor_tensor(self.cmp_ge[:, :, :], self.cmp_ge[:, :, :], self.cmp_gt[:, :, :], ALU.add)
        dve.drain()
        dve.tensor_reduce(rank, ge, AX.X, ALU.add)
        dve.drain()
        dve.wait_ge(self.exped.sem, self.exped.at(n))
        if self.denominator != "chosen":
            dve.tensor_reduce(self.sum[:, 1, :], expo, AX.X, ALU.add)
        dve.scalar_tensor_tensor(rest, rank, float(self.topk), expo, ALU.is_lt, ALU.mult)
        dve.drain()
        if self.denominator != "all":
            dve.tensor_reduce(self.sum[:, 0, :], rest, AX.X, ALU.add)
            dve.drain()
        total = self.sum[:, 1 if self.denominator == "all" else 0, :]
        if self.denominator == "chosen+1e-9":
            dve.scalar_tensor_tensor(total, self.sum[:, 1, :], 1e-9, total, ALU.mult, ALU.add)
            dve.drain()
        dve.reciprocal(total, total)
        dve.drain()
        dve.tensor_tensor(comb, rest, over_e(total), ALU.mult)
        for part in range(3):
            dve.drain()
            dve_src = self.comb if part == 0 else self.rest
            mine3 = self.parts[:, :, part * W:(part + 1) * W]
            last = dve.tensor_copy(mine3, dve_src[:, :, :])
            if part < 2:
                dve.drain()
                dve.tensor_tensor(self.rest[:, :, :], dve_src[:, :, :], mine3, ALU.subtract)
        last.then_inc(self.weighed.sem, 1)

    def act_exp(self, act, n):
        act.wait_ge(self.shifted.sem, self.shifted.at(n))
        act.activation(self.expo[:, :, :], self.shift[:, :, :], ACT.Exp).then_inc(self.exped.sem, 1)

    def pe_turn_back(self, pe, n):
        pe.wait_ge(self.weighed.sem, self.weighed.at(n))
        turned = self.k.bank[1][:, 0:TB // 2].bitcast(BF16)
        for j in range(TPB):
            mm = pe.transpose(turned[:, j * P:(j + 1) * P], self.parts[:, j, :], self.k.ident_bf[:, :])
        mm.then_inc(self.turned.sem, 1)

    def act_rows(self, act, n):
        act.wait_ge(self.turned.sem, self.turned.at(n))
        act.activation(self.rows[:, bass.ts(n, TB)], self.k.bank[1][:, 0:TB // 2].bitcast(BF16),
                       ACT.Copy).then_inc(self.rows_ready.sem, 1)


def load_meanwhile(k, block, loads):
    if loads:
        @block.sync
        def _(sp):
            for region, array in loads:
                sp.dma_start(region, array).then_inc(k.loaded, 16)
            k.loads += len(loads)
            sp.wait_ge(k.loaded, 16 * k.loads)


def top1_ffn(k, w, loads=()):
    nc, E = k.nc, 8
    with ExitStack() as s:
        st = lambda name, shape, dt=F32: s.enter_context(nc.sbuf_tensor(k.fresh(name), shape, dt))
        xn = st("xn", [P, T])
        rows = k.rows
        scaled = st("scaled", [P, 2, TB])
        norm = Norm(k, st, xn)
        route = Route(k, st, "route", E, 1, 1, "all", rows, bias=w["router_b"])
        spread, scale, used = (k.counter(x) for x in ("spread", "scaled", "expert_used"))
        y_ready, x_done = k.counter("y_ready"), k.counter("x_done")
        bank_y = k.bank[4]
        block = s.enter_context(nc.Block())
        load_meanwhile(k, block, loads)

        @block.tensor
        def _(pe):
            def logits(n):
                pe.wait_ge(norm.normed.sem, norm.normed.at(n))
                pe.matmul(k.bank[1][0:E, :], w["router"], xn[:, bass.ts(n, TB)],
                          start=True, stop=True).then_inc(route.logits.sem, 1)

            prep = [norm.pe_centre, norm.pe_variance, None, route.pe_by_token, None, route.pe_turn_back, None, None]

            def prepare(n, step):
                if step == 2:
                    logits(n)
                elif prep[step]:
                    prep[step](pe, n)

            def put_weights(n, e):
                pe.wait_ge(scale.sem, scale.at(n * E + e - 2))
                if e == 0:
                    pe.wait_ge(route.rows_ready.sem, route.rows_ready.at(n))
                pe.matmul(k.bank[2 + e % 2][:, :], k.selector[E][:, e, :], rows[:, bass.ts(n, TB)],
                          start=True, stop=True).then_inc(spread.sem, 1)

            def expert(n, e):
                if e == 0:
                    put_weights(n, 0)
                    pe.wait_ge(x_done.sem, x_done.at(n - 1))
                if e < E - 1:
                    put_weights(n, e + 1)
                pe.wait_ge(scale.sem, scale.at(n * E + e))
                pe.matmul(bank_y[:, :], w["expert_w"][:, e, :], scaled[:, e % 2, :],
                          start=(e == 0), stop=False).then_inc(used.sem, 1)
                if e == E - 1:
                    for part in range(3):
                        mm = pe.matmul(bank_y[:, :], k.expert_b_parts[:, part, :], rows[:, bass.ts(n, TB)],
                                       start=False, stop=(part == 2))
                    mm.then_inc(y_ready.sem, 1)

            for step in range(8):
                prepare(0, step)
            with pe.Fori(0, NB - 1) as n:
                for e in range(E):
                    expert(n, e)
                    prepare(n + 1, e)
            for e in range(E):
                expert(NB - 1, e)

        @block.scalar
        def _(act):
            def prepare(n):
                norm.act_square(act, n)
                norm.act_deviation(act, n)
                route.act_logits_out(act, n)
                route.act_exp(act, n)
                route.act_rows(act, n)

            with act.Fori(0, NB) as n:
                prepare(n)

        @block.vector
        def _(dve):
            def prepare(n, step):
                if step == 1:
                    norm.dve_norm(dve, n)
                elif step == 4:
                    route.dve_weights(dve, n)

            def expert(n, e):
                dve.wait_ge(spread.sem, spread.at(n * E + e))
                dve.wait_ge(used.sem, used.at(n * E + e - 2))
                dve.tensor_tensor(scaled[:, e % 2, :], xn[:, bass.ts(n, TB)], k.bank[2 + e % 2][:, :],
                                  ALU.mult).then_inc(scale.sem, 1)

            def add_to_x(n):
                dve.wait_ge(y_ready.sem, y_ready.at(n))
                xb = k.x[:, bass.ts(n, TB)]
                dve.scalar_tensor_tensor(xb, bank_y[:, :], 0.5, xb, ALU.mult, ALU.add).then_inc(x_done.sem, 1)

            for step in range(8):
                prepare(0, step)
            with dve.Fori(0, NB - 1) as n:
                for e in range(E):
                    expert(n, e)
                    prepare(n + 1, e)
                add_to_x(n)
            for e in range(E):
                expert(NB - 1, e)
            add_to_x(NB - 1)

    norm.passed()
    route.passed()
    k.passed({"spread": NB * E, "scaled": NB * E, "expert_used": NB * E, "y_ready": NB, "x_done": NB})


def top2_silu_ffn(k, w, loads=()):
    nc, E, C = k.nc, 8, 4
    with ExitStack() as s:
        st = lambda name, shape, dt=F32: s.enter_context(nc.sbuf_tensor(k.fresh(name), shape, dt))
        xn = st("xn", [P, T])
        rows = k.rows
        router_hidden = st("router_hidden", [P, TB])
        hidden = k.probs[:, :].rearrange("p (b c t) -> p b c t", b=2, c=C)
        weight = st("weight", [P, 2, TB])
        weighted = st("weighted", [P, TB])
        norm = Norm(k, st, xn)
        route = Route(k, st, "route", E, 1, 2, "chosen", rows, bias=w["rb2"])
        spread, spread_out = k.counter("spread"), k.counter("spread_out")
        r_pre, r_hid = k.counter("router_pre"), k.counter("router_hidden")
        pre, act_done = k.counter("hidden_pre"), k.counter("hidden_done")
        y_ready, x_done = k.counter("y_ready"), k.counter("x_done")
        block = s.enter_context(nc.Block())
        load_meanwhile(k, block, loads)

        @block.tensor
        def _(pe):
            def prepare(n, step):
                if step == 0:
                    norm.pe_centre(pe, n)
                elif step == 1:
                    norm.pe_variance(pe, n)
                elif step == 2:
                    pe.wait_ge(norm.normed.sem, norm.normed.at(n))
                    pe.matmul(k.bank[1][:, :], w["rw1"], xn[:, bass.ts(n, TB)],
                              start=True, stop=True).then_inc(r_pre.sem, 1)
                elif step == 3:
                    pe.wait_ge(r_hid.sem, r_hid.at(n))
                    pe.matmul(k.bank[1][0:E, :], w["rw2"], router_hidden[:, :],
                              start=True, stop=True).then_inc(route.logits.sem, 1)
                elif step == 4:
                    route.pe_by_token(pe, n)
                elif step == 6:
                    route.pe_turn_back(pe, n)

            def first_layer(n, e):
                for c in range(C):
                    i = n * (E * C) + (e * C + c)
                    pe.wait_ge(act_done.sem, act_done.at(i - 2))
                    pe.matmul(k.bank[4 + c % 2][:, :], w["we1"][:, e, c, :], xn[:, bass.ts(n, TB)],
                              start=True, stop=True).then_inc(pre.sem, 1)

            def second_layer(n, e):
                pe.wait_ge(spread_out.sem, spread_out.at(n * E + e - 1))
                if e == 0:
                    pe.wait_ge(route.rows_ready.sem, route.rows_ready.at(n))
                pe.matmul(k.bank[2][:, :], k.selector[E][:, e, :], rows[:, bass.ts(n, TB)],
                          start=True, stop=True).then_inc(spread.sem, 1)
                pe.wait_ge(x_done.sem, x_done.at(n * E + e - 2))
                for c in range(C):
                    pe.wait_ge(act_done.sem, act_done.at(n * (E * C) + (e * C + c)))
                    mm = pe.matmul(k.bank[6 + e % 2][:, :], w["we2"][:, e, c, :], hidden[:, e % 2, c, :],
                                   start=(c == 0), stop=(c == C - 1))
                mm.then_inc(y_ready.sem, 1)

            def expert(n, e):
                if e == 0:
                    first_layer(n, 0)
                if e < E - 1:
                    first_layer(n, e + 1)
                second_layer(n, e)

            for step in range(8):
                prepare(0, step)
            with pe.Fori(0, NB - 1) as n:
                for e in range(E):
                    expert(n, e)
                    prepare(n + 1, e)
            for e in range(E):
                expert(NB - 1, e)

        @block.scalar
        def _(act):
            def prepare(n, step):
                if step == 0:
                    norm.act_square(act, n)
                elif step == 1:
                    norm.act_deviation(act, n)
                elif step == 2:
                    act.wait_ge(r_pre.sem, r_pre.at(n))
                    act.activation(router_hidden[:, :], k.bank[1][:, :], ACT.Silu,
                                   bias=w["rb1"]).then_inc(r_hid.sem, 1)
                elif step == 3:
                    route.act_logits_out(act, n)
                elif step == 5:
                    route.act_exp(act, n)
                elif step == 6:
                    route.act_rows(act, n)

            def hidden_of(n, e):
                act.wait_ge(y_ready.sem, y_ready.at(n * E + e - 2))
                for c in range(C):
                    act.wait_ge(pre.sem, pre.at(n * (E * C) + (e * C + c)))
                    act.activation(hidden[:, e % 2, c, :], k.bank[4 + c % 2][:, :], ACT.Silu,
                                   bias=w["be1"][:, e * C + c:e * C + c + 1]).then_inc(act_done.sem, 1)

            def expert(n, e):
                if e == 0:
                    hidden_of(n, 0)
                if e < E - 1:
                    hidden_of(n, e + 1)
                act.wait_ge(spread.sem, spread.at(n * E + e))
                act.wait_ge(x_done.sem, x_done.at(n * E + e - 2))
                act.activation(weight[:, e % 2, :], k.bank[2][:, :], ACT.Copy).then_inc(spread_out.sem, 1)

            for step in range(8):
                prepare(0, step)
            with act.Fori(0, NB - 1) as n:
                for e in range(E):
                    expert(n, e)
                    prepare(n + 1, e)
            for e in range(E):
                expert(NB - 1, e)

        @block.vector
        def _(dve):
            def prepare(n, step):
                if step == 1:
                    norm.dve_norm(dve, n)
                elif step == 5:
                    route.dve_weights(dve, n)

            def expert(n, e):
                xb = k.x[:, bass.ts(n, TB)]
                if e == 0:
                    dve.scalar_tensor_tensor(xb, xn[:, bass.ts(n, TB)], 0.5, xb, ALU.mult, ALU.add)
                dve.drain()
                dve.wait_ge(y_ready.sem, y_ready.at(n * E + e))
                dve.wait_ge(spread_out.sem, spread_out.at(n * E + e))
                dve.scalar_tensor_tensor(weighted[:, :], k.bank[6 + e % 2][:, :], w["be2"][:, e:e + 1],
                                         weight[:, e % 2, :], ALU.add, ALU.mult)
                dve.drain()
                dve.scalar_tensor_tensor(xb, weighted[:, :], 0.5, xb, ALU.mult,
                                         ALU.add).then_inc(x_done.sem, 1)

            for step in range(8):
                prepare(0, step)
            with dve.Fori(0, NB - 1) as n:
                for e in range(E):
                    expert(n, e)
                    prepare(n + 1, e)
            for e in range(E):
                expert(NB - 1, e)

    norm.passed()
    route.passed()
    k.passed({"spread": NB * E, "spread_out": NB * E, "router_pre": NB, "router_hidden": NB,
              "hidden_pre": NB * E * C, "hidden_done": NB * E * C, "y_ready": NB * E, "x_done": NB * E})


def top2_linear_ffn(k, w, loads=()):
    nc, E, C = k.nc, 8, 4
    with ExitStack() as s:
        st = lambda name, shape, dt=F32: s.enter_context(nc.sbuf_tensor(k.fresh(name), shape, dt))
        xn = st("xn", [P, T])
        rows = k.rows
        down_rows = k.down_rows
        scaled = k.big_scaled
        gated = st("gated", [P, TB])
        inter = k.probs[:, :].rearrange("p (b c t) -> p b c t", b=2, c=C)
        weight = st("weight", [P, 2, TB])
        weighted = st("weighted", [P, TB])
        norm = Norm(k, st, xn)
        route = Route(k, st, "route", E, 2, 2, "chosen", rows)
        down_route = Route(k, st, "down_route", E, 1, 2, "chosen", down_rows)
        spread, scale = k.counter("spread"), k.counter("scaled")
        gate_ready, up_ready, gate_silu, inter_ready = (
            k.counter(x) for x in ("gate_ready", "up_ready", "gate_silu", "inter_ready"))
        down_spread, down_spread_out = k.counter("down_spread"), k.counter("down_spread_out")
        y_ready, x_done = k.counter("y_ready"), k.counter("x_done")
        block = s.enter_context(nc.Block())
        load_meanwhile(k, block, loads)

        def parity(n):
            return n % 2

        @block.tensor
        def _(pe):
            def prepare(n, step):
                if step == 0:
                    norm.pe_centre(pe, n)
                    pe.wait_ge(down_route.rows_ready.sem, down_route.rows_ready.at(n - 2))
                    norm.pe_variance(pe, n)
                elif step == 1:
                    pe.wait_ge(norm.normed.sem, norm.normed.at(n))
                    pe.matmul(k.bank[1][0:2 * E, :], w["router_gate_up"], xn[:, bass.ts(n, TB)],
                              start=True, stop=True).then_inc(route.logits.sem, 1)
                elif step == 2:
                    route.pe_by_token(pe, n)
                elif step == 3:
                    route.pe_turn_back(pe, n)

            def put_weights(n, i):
                pe.wait_ge(scale.sem, scale.at(n * (2 * E) + i - 2))
                if i == 0:
                    pe.wait_ge(route.rows_ready.sem, route.rows_ready.at(n))
                pe.matmul(k.bank[2 + i % 2][:, :], k.selector[2 * E][:, i, :], rows[:, bass.ts(n, TB)],
                          start=True, stop=True).then_inc(spread.sem, 1)

            def gate_up(n, prev, c):
                pe.wait_ge(scale.sem, scale.at(n * (2 * E) + (2 * E - 1)))
                pe.wait_ge(inter_ready.sem, inter_ready.at(n * C + c - 2))
                for e in range(E):
                    mm = pe.matmul(k.bank[4 + c % 2][:, :], w["gate"][:, e, c, :], scaled[:, e, :],
                                   start=(e == 0), stop=(e == E - 1))
                mm.then_inc(gate_ready.sem, 1)
                if c < 2 and prev is not None:
                    pe.wait_ge(x_done.sem, x_done.at(n * E - E - 1))
                for e in range(E):
                    mm = pe.matmul(k.bank[6 + c % 2][:, :], w["up"][:, e, c, :], scaled[:, E + e, :],
                                   start=(e == 0), stop=(e == E - 1))
                mm.then_inc(up_ready.sem, 1)

            def down(n, e):
                pe.wait_ge(down_spread_out.sem, down_spread_out.at(n * E + e - 1))
                if e == 0:
                    pe.wait_ge(down_route.rows_ready.sem, down_route.rows_ready.at(n))
                pe.matmul(k.bank[2][:, :], k.selector[E][:, e, :], down_rows[:, bass.ts(n, TB)],
                          start=True, stop=True).then_inc(down_spread.sem, 1)
                pe.wait_ge(x_done.sem, x_done.at(n * E + e - 2))
                for c in range(C):
                    mm = pe.matmul(k.bank[6 + e % 2][:, :], w["down"][:, e, c, :],
                                   inter[:, parity(n), c, :], start=(c == 0), stop=(c == C - 1))
                mm.then_inc(y_ready.sem, 1)

            def down_logits(n):
                pe.wait_ge(inter_ready.sem, inter_ready.at(n * C + (C - 1)))
                for c in range(C):
                    mm = pe.matmul(k.bank[1][0:E, :], w["router_down"][:, c, :], inter[:, parity(n), c, :],
                                   start=(c == 0), stop=(c == C - 1))
                mm.then_inc(down_route.logits.sem, 1)

            def down_prepare(n, step):
                if step == 0:
                    down_logits(n)
                elif step == 2:
                    down_route.pe_by_token(pe, n)
                elif step == 5:
                    down_route.pe_turn_back(pe, n)

            def body(n, prev, nxt):
                for c in range(C):
                    gate_up(n, prev, c)
                    if nxt is not None:
                        prepare(nxt, c)
                if nxt is not None:
                    pe.wait_ge(route.rows_ready.sem, route.rows_ready.at(nxt))
                for e in range(E):
                    if e in (0, 2, 5):
                        down_prepare(n, e)
                    if prev is not None:
                        down(prev, e)
                if nxt is not None:
                    if prev is not None:
                        pe.wait_ge(down_spread_out.sem, down_spread_out.at(prev * E + (E - 1)))
                    for i in range(2 * E):
                        put_weights(nxt, i)

            for step in range(4):
                prepare(0, step)
            for i in range(2 * E):
                put_weights(0, i)
            body(0, None, 1)
            with pe.Fori(1, NB - 1) as n:
                body(n, n - 1, n + 1)
            body(NB - 1, NB - 2, None)
            for e in range(E):
                down(NB - 1, e)

        @block.scalar
        def _(act):
            def prepare(n, step):
                if step == 0:
                    norm.act_square(act, n)
                    norm.act_deviation(act, n)
                elif step == 1:
                    route.act_logits_out(act, n)
                elif step == 2:
                    route.act_exp(act, n)
                elif step == 3:
                    route.act_rows(act, n)

            def gate_up(n, c):
                act.wait_ge(gate_ready.sem, gate_ready.at(n * C + c))
                act.wait_ge(inter_ready.sem, inter_ready.at(n * C + c - 1))
                act.activation(gated[:, :], k.bank[4 + c % 2][:, :], ACT.Silu).then_inc(gate_silu.sem, 1)

            def down(n, e):
                act.wait_ge(down_spread.sem, down_spread.at(n * E + e))
                act.wait_ge(x_done.sem, x_done.at(n * E + e - 2))
                act.activation(weight[:, e % 2, :], k.bank[2][:, :], ACT.Copy).then_inc(down_spread_out.sem, 1)

            def body(n, prev, nxt):
                for c in range(C):
                    gate_up(n, c)
                    if nxt is not None:
                        prepare(nxt, c)
                for e in range(E):
                    if e == 0:
                        down_route.act_logits_out(act, n)
                    elif e == 3:
                        down_route.act_exp(act, n)
                    elif e == 5:
                        down_route.act_rows(act, n)
                    if prev is not None:
                        down(prev, e)

            for step in range(4):
                prepare(0, step)
            body(0, None, 1)
            with act.Fori(1, NB - 1) as n:
                body(n, n - 1, n + 1)
            body(NB - 1, NB - 2, None)
            for e in range(E):
                down(NB - 1, e)

        @block.vector
        def _(dve):
            def prepare(n, step):
                if step == 0:
                    norm.dve_norm(dve, n)
                elif step == 2:
                    route.dve_weights(dve, n)

            def scale_inputs(n):
                dve.wait_ge(up_ready.sem, up_ready.at(n * C - 1))
                for i in range(2 * E):
                    dve.wait_ge(spread.sem, spread.at(n * (2 * E) + i))
                    dve.tensor_tensor(scaled[:, i, :], xn[:, bass.ts(n, TB)], k.bank[2 + i % 2][:, :],
                                      ALU.mult).then_inc(scale.sem, 1)

            def gate_up(n, prev, c):
                dve.wait_ge(gate_silu.sem, gate_silu.at(n * C + c))
                dve.wait_ge(up_ready.sem, up_ready.at(n * C + c))
                if prev is not None:
                    dve.wait_ge(y_ready.sem, y_ready.at(n * E - E - 1))
                dve.tensor_tensor(inter[:, parity(n), c, :], gated[:, :], k.bank[6 + c % 2][:, :],
                                  ALU.mult).then_inc(inter_ready.sem, 1)

            def down(n, e):
                xb = k.x[:, bass.ts(n, TB)]
                dve.drain()
                dve.wait_ge(y_ready.sem, y_ready.at(n * E + e))
                dve.wait_ge(down_spread_out.sem, down_spread_out.at(n * E + e))
                dve.tensor_tensor(weighted[:, :], k.bank[6 + e % 2][:, :], weight[:, e % 2, :], ALU.mult)
                dve.drain()
                dve.scalar_tensor_tensor(xb, weighted[:, :], 0.5, xb, ALU.mult, ALU.add).then_inc(x_done.sem, 1)

            def body(n, prev, nxt):
                for c in range(C):
                    gate_up(n, prev, c)
                    if nxt is not None:
                        prepare(nxt, c)
                for e in range(E):
                    if e == 3:
                        down_route.dve_weights(dve, n)
                    if prev is not None:
                        down(prev, e)
                if nxt is not None:
                    scale_inputs(nxt)

            for step in range(4):
                prepare(0, step)
            scale_inputs(0)
            body(0, None, 1)
            with dve.Fori(1, NB - 1) as n:
                body(n, n - 1, n + 1)
            body(NB - 1, NB - 2, None)
            for e in range(E):
                down(NB - 1, e)

    norm.passed()
    route.passed()
    down_route.passed()
    k.passed({"spread": NB * 2 * E, "scaled": NB * 2 * E, "gate_ready": NB * C, "up_ready": NB * C,
              "gate_silu": NB * C, "inter_ready": NB * C, "down_spread": NB * E, "down_spread_out": NB * E,
              "y_ready": NB * E, "x_done": NB * E})


def shared_routed_ffn(k, w, loads=()):
    nc, E, C = k.nc, 16, 4
    with ExitStack() as s:
        st = lambda name, shape, dt=F32: s.enter_context(nc.sbuf_tensor(k.fresh(name), shape, dt))
        xn = st("xn", [P, T])
        rows = k.rows
        gated = st("gated", [P, 2, TB])
        product = st("product", [P, TB])
        hidden = st("hidden", [P, 2, TB])
        norm = Norm(k, st, xn)
        route = Route(k, st, "wide_route", E, 1, 2, "chosen+1e-9", rows)
        spread = k.counter("spread")
        gate_ready, up_ready, gate_silu, inter_ready = (
            k.counter(x) for x in ("gate_ready", "up_ready", "gate_silu", "inter_ready"))
        used, y_ready, x_done = k.counter("expert_used"), k.counter("y_ready"), k.counter("x_done")
        bank_y = k.bank[3]
        C1 = C + 1
        block = s.enter_context(nc.Block())
        load_meanwhile(k, block, loads)

        @block.tensor
        def _(pe):
            def prepare(n, step):
                if step == 0:
                    norm.pe_centre(pe, n)
                elif step == 1:
                    norm.pe_variance(pe, n)
                elif step == 2:
                    pe.wait_ge(norm.normed.sem, norm.normed.at(n))
                    pe.matmul(k.bank[1][0:E, :], w["router"], xn[:, bass.ts(n, TB)],
                              start=True, stop=True).then_inc(route.logits.sem, 1)
                elif step == 3:
                    route.pe_by_token(pe, n)
                elif step == 4:
                    route.pe_turn_back(pe, n)

            def gate_up(n, c):
                i = n * C1 + c
                pe.wait_ge(inter_ready.sem, inter_ready.at(i - 1))
                if c == 0:
                    pe.wait_ge(route.rows_ready.sem, route.rows_ready.at(n))
                if c < C:
                    pe.matmul(k.bank[2][:, :], k.chunk_selector[:, c, :], rows[:, bass.ts(n, TB)],
                              start=True, stop=True).then_inc(spread.sem, 1)
                pe.matmul(k.bank[4 + c % 2][:, :], w["gate"][:, c, :], xn[:, bass.ts(n, TB)],
                          start=True, stop=True).then_inc(gate_ready.sem, 1)
                pe.matmul(k.bank[6 + c % 2][:, :], w["up"][:, c, :], xn[:, bass.ts(n, TB)],
                          start=True, stop=True).then_inc(up_ready.sem, 1)

            def down(n, c):
                pe.wait_ge(inter_ready.sem, inter_ready.at(n * C1 + c))
                if c == 0:
                    pe.wait_ge(x_done.sem, x_done.at(n - 1))
                mm = pe.matmul(bank_y[:, :], w["down"][:, c, :], hidden[:, c % 2, :],
                               start=(c == 0), stop=(c == C)).then_inc(used.sem, 1)
                return mm

            def chunk(n, c):
                gate_up(n, c)
                if c > 0:
                    down(n, c - 1)
                if c == C:
                    down(n, C)

            for step in range(C1):
                prepare(0, step)
            with pe.Fori(0, NB - 1) as n:
                for c in range(C1):
                    chunk(n, c)
                    prepare(n + 1, c)
            for c in range(C1):
                chunk(NB - 1, c)

        @block.scalar
        def _(act):
            def prepare(n, step):
                if step == 0:
                    norm.act_square(act, n)
                elif step == 1:
                    norm.act_deviation(act, n)
                elif step == 2:
                    route.act_logits_out(act, n)
                elif step == 3:
                    route.act_exp(act, n)
                elif step == 4:
                    route.act_rows(act, n)

            def chunk(n, c):
                i = n * C1 + c
                act.wait_ge(gate_ready.sem, gate_ready.at(i))
                act.wait_ge(inter_ready.sem, inter_ready.at(i - (1 if c == 0 else 2)))
                act.activation(gated[:, c % 2, :], k.bank[4 + c % 2][:, :], ACT.Silu).then_inc(gate_silu.sem, 1)

            for step in range(C1):
                prepare(0, step)
            with act.Fori(0, NB - 1) as n:
                for c in range(C1):
                    chunk(n, c)
                    prepare(n + 1, c)
            for c in range(C1):
                chunk(NB - 1, c)

        @block.vector
        def _(dve):
            def prepare(n, step):
                if step == 1:
                    norm.dve_norm(dve, n)
                elif step == 3:
                    route.dve_weights(dve, n)

            def chunk(n, c):
                i = n * C1 + c
                dve.wait_ge(gate_silu.sem, gate_silu.at(i))
                dve.wait_ge(up_ready.sem, up_ready.at(i))
                dve.wait_ge(used.sem, used.at(i - (1 if c == 0 else 2)))
                if c < C:
                    dve.tensor_tensor(product[:, :], gated[:, c % 2, :], k.bank[6 + c % 2][:, :], ALU.mult)
                    dve.drain()
                    dve.wait_ge(spread.sem, spread.at(n * C + c))
                    dve.tensor_tensor(hidden[:, c % 2, :], product[:, :], k.bank[2][:, :],
                                      ALU.mult).then_inc(inter_ready.sem, 1)
                else:
                    dve.tensor_tensor(hidden[:, c % 2, :], gated[:, c % 2, :], k.bank[6 + c % 2][:, :],
                                      ALU.mult).then_inc(inter_ready.sem, 1)

            def add_to_x(n):
                dve.wait_ge(used.sem, used.at(n * C1 + C))
                xb = k.x[:, bass.ts(n, TB)]
                dve.scalar_tensor_tensor(xb, bank_y[:, :], 0.5, xb, ALU.mult, ALU.add).then_inc(x_done.sem, 1)

            for step in range(C1):
                prepare(0, step)
            with dve.Fori(0, NB - 1) as n:
                for c in range(C1):
                    chunk(n, c)
                    prepare(n + 1, c)
                add_to_x(n)
            for c in range(C1):
                chunk(NB - 1, c)
            add_to_x(NB - 1)

    norm.passed()
    route.passed()
    k.passed({"spread": NB * C, "gate_ready": NB * C1, "up_ready": NB * C1, "gate_silu": NB * C1,
              "inter_ready": NB * C1, "expert_used": NB * C1, "x_done": NB})


def scan_attention(k, w):
    nc = k.nc
    with ExitStack() as s:
        st = Carve(k.big_upper)
        xn = st("xn", [P, T])
        driven = st("driven", [P, 2, TB])
        y = st("y", [P, T + 1])
        decay = st("decay", [P, 1])
        norm = Norm(k, st, xn)
        tanh_done, scanned = k.counter("scan_input"), k.counter("scanned")
        y_ready, x_done = k.counter("y_ready"), k.counter("x_done")
        block = s.enter_context(nc.Block())

        @block.tensor
        def _(pe):
            def project(n):
                pe.wait_ge(scanned.sem, scanned.at(n))
                pe.wait_ge(x_done.sem, x_done.at(n - 1))
                pe.matmul(k.bank[2][:, :], w["w_out"], y[:, bass.ds(n * TB + 1, TB)],
                          start=True, stop=True).then_inc(y_ready.sem, 1)

            norm.pe_centre(pe, 0)
            norm.pe_variance(pe, 0)
            with pe.Fori(0, NB - 1) as n:
                norm.pe_centre(pe, n + 1)
                norm.pe_variance(pe, n + 1)
                project(n)
            project(NB - 1)

        @block.scalar
        def _(act):
            act.activation(decay[:, :], w["a"], ACT.Tanh).then_inc(tanh_done.sem, 1)
            with act.Fori(0, NB) as n:
                norm.act_square(act, n)
                norm.act_deviation(act, n)

        @block.vector
        def _(dve):
            dve.memset(y[:, 0:1], 0.0)
            dve.wait_ge(tanh_done.sem, tanh_done.at(0))
            norm.dve_norm(dve, 0)

            def scan(n):
                dve.drain()
                dve.tensor_scalar(driven[:, 0, :], xn[:, bass.ts(n, TB)], w["b"], None, ALU.mult)
                dve.drain()
                dve.tensor_tensor_scan(y[:, bass.ds(n * TB + 1, TB)], decay[:, 0:1].to_broadcast([P, TB]),
                                       driven[:, 0, :], y[:, bass.ds(n * TB, 1)],
                                       ALU.mult, ALU.add).then_inc(scanned.sem, 1)

            def add_to_x(n):
                dve.wait_ge(y_ready.sem, y_ready.at(n))
                xb = k.x[:, bass.ts(n, TB)]
                dve.scalar_tensor_tensor(xb, k.bank[2][:, :], w["b_out"], xb, ALU.add,
                                         ALU.add).then_inc(x_done.sem, 1)

            with dve.Fori(0, NB - 1) as n:
                scan(n)
                norm.dve_norm(dve, n + 1)
                add_to_x(n)
            scan(NB - 1)
            add_to_x(NB - 1)

    norm.passed()
    k.passed({"scan_input": 1, "scanned": NB, "y_ready": NB, "x_done": NB})


def window_attention(k, w):
    nc, G = k.nc, 64
    H = WIN
    with ExitStack() as s:
        st = Carve(k.big_upper)
        xn = st("xn", [P, T + 1])
        diff = st("diff", [P, TB])
        square = st("square", [P, TB])
        size = st("size", [P, TB])
        inv = st("inv", [P, TB])
        unit = st("unit", [P, TB])
        unit_sq = st("unit_sq", [P, TB])
        unit_size = st("unit_size", [P, TB])
        direction = st("direction", [P, TB])
        expo = st("expo", [P, TB])
        total = st("total", [P, TB])
        value = st("value", [P, H + T])
        weight = st("weight", [P, H + T])
        wsum = st("wsum", [P, TB])
        early = st("early", [P, 2, WIN, WIN])
        early_sum = st("early_sum", [P, 2, WIN])
        gsq = st("gsq", [G, P])
        gscale = st("gscale", [G, 1])
        norm = Norm(k, Carve(k.probs), xn, left=1)
        names = ("win_diff", "win_square", "win_sum", "win_size", "win_unit", "win_unit_sq", "win_unit_sum",
                 "win_unit_size", "win_dir", "win_dots", "win_exp", "win_mix", "win_value", "win_out", "win_done")
        (s_diff, s_square, s_sum, s_size, s_unit, s_unit_sq, s_unit_sum, s_unit_size, s_dir, s_dots, s_exp,
         s_mix, s_value, s_out, s_done) = (k.counter(x) for x in names)
        block = s.enter_context(nc.Block())

        @block.gpsimd
        def _(pool):
            pool.memset(xn[:, 0:1], 0.0)
            pool.memset(value[:, 0:H], 0.0)
            pool.memset(weight[:, 0:H], 0.0)
            pool.memset(expo[:, :], 0.0)
            pool.drain().then_inc(s_diff.sem, 1)

        @block.tensor
        def _(pe):
            with pe.Fori(0, NB) as n:
                norm.pe_centre(pe, n)
                norm.pe_variance(pe, n)
                pe.wait_ge(s_square.sem, s_square.at(n))
                pe.matmul(k.bank[2][:, :], w["ones"], square[:, :], start=True, stop=True).then_inc(s_sum.sem, 1)
                pe.wait_ge(s_unit_sq.sem, s_unit_sq.at(n))
                pe.matmul(k.bank[3][:, :], w["ones"], unit_sq[:, :], start=True, stop=True).then_inc(s_unit_sum.sem, 1)
                pe.wait_ge(s_dir.sem, s_dir.at(n))
                pe.matmul(k.bank[4][0:G, :], w["guideT"], direction[:, :], start=True, stop=True).then_inc(s_dots.sem, 1)
                pe.wait_ge(s_exp.sem, s_exp.at(n + 1))
                pe.matmul(k.bank[5][:, :], w["ones"], expo[:, :], start=True, stop=True)
                pe.matmul(k.bank[6][:, :], w["guide"], expo[:, :], start=True, stop=True).then_inc(s_mix.sem, 1)
                pe.wait_ge(s_value.sem, s_value.at(n))
                for sh in range(WIN):
                    mm = pe.matmul(k.bank[7][:, :], w["ramp"][:, sh * P:(sh + 1) * P],
                                   value[:, bass.ds(n * TB + (H - sh), TB)],
                                   start=(sh == 0), stop=(sh == WIN - 1))
                mm.then_inc(s_out.sem, 1)

        @block.scalar
        def _(act):
            act.activation(gsq[:, :], w["guide_rows"], ACT.Square, accum_out=gscale[:, :])
            act.drain()
            act.activation(gscale[:, :], gscale[:, :], ACT.Sqrt)
            act.drain().then_inc(s_exp.sem, 1)
            with act.Fori(0, NB) as n:
                norm.act_square(act, n)
                norm.act_deviation(act, n)
                act.wait_ge(s_diff.sem, s_diff.at(n + 1))
                act.activation(square[:, :], diff[:, :], ACT.Square).then_inc(s_square.sem, 1)
                act.wait_ge(s_sum.sem, s_sum.at(n))
                act.activation(size[:, :], k.bank[2][:, :], ACT.Sqrt).then_inc(s_size.sem, 1)
                act.wait_ge(s_unit.sem, s_unit.at(n))
                act.activation(unit_sq[:, :], unit[:, :], ACT.Square).then_inc(s_unit_sq.sem, 1)
                act.wait_ge(s_unit_sum.sem, s_unit_sum.at(n))
                act.activation(unit_size[:, :], k.bank[3][:, :], ACT.Sqrt).then_inc(s_unit_size.sem, 1)
                act.activation(weight[:, bass.ds(n * TB + H, TB)], size[:, :], ACT.Tanh, scale=2.0)
                act.wait_ge(s_dots.sem, s_dots.at(n))
                act.activation(expo[0:G, :], k.bank[4][0:G, :], ACT.Exp, scale=gscale[:, :]).then_inc(s_exp.sem, 1)

        @block.vector
        def _(dve):
            dve.wait_ge(s_exp.sem, s_exp.at(0))
            dve.wait_ge(s_diff.sem, s_diff.at(0))
            dve.tensor_scalar(gscale[:, :], gscale[:, :], 1e-8, None, ALU.max)
            dve.drain()
            dve.reciprocal(gscale[:, :], gscale[:, :])
            dve.drain()
            dve.tensor_scalar(gscale[:, :], gscale[:, :], 2.0, None, ALU.mult)
            dve.drain()

            def body(n, first):
                here = bass.ds(n * TB + H, TB)
                norm.dve_norm(dve, n)
                dve.drain()
                dve.tensor_tensor(diff[:, :], xn[:, bass.ds(n * TB + 1, TB)], xn[:, bass.ds(n * TB, TB)],
                                  ALU.subtract).then_inc(s_diff.sem, 1)
                dve.wait_ge(s_size.sem, s_size.at(n))
                dve.tensor_scalar(inv[:, :], size[:, :], 1e-6, None, ALU.max)
                dve.drain()
                dve.reciprocal(inv[:, :], inv[:, :])
                dve.drain()
                dve.scalar_tensor_tensor(inv[:, :], size[:, :], 1e-6, inv[:, :], ALU.is_gt, ALU.mult)
                dve.drain()
                dve.tensor_tensor(unit[:, :], diff[:, :], inv[:, :], ALU.mult).then_inc(s_unit.sem, 1)
                dve.wait_ge(s_unit_size.sem, s_unit_size.at(n))
                dve.tensor_scalar(unit_size[:, :], unit_size[:, :], 1e-8, None, ALU.max)
                dve.drain()
                dve.reciprocal(unit_size[:, :], unit_size[:, :])
                dve.drain()
                dve.tensor_tensor(direction[:, :], unit[:, :], unit_size[:, :], ALU.mult).then_inc(s_dir.sem, 1)
                dve.wait_ge(s_mix.sem, s_mix.at(n))
                dve.reciprocal(total[:, :], k.bank[5][:, :])
                dve.drain()
                dve.tensor_tensor(total[:, :], k.bank[6][:, :], total[:, :], ALU.mult)
                dve.tensor_scalar(unit[:, :], unit[:, :], 0.6, None, ALU.mult)
                dve.drain()
                dve.scalar_tensor_tensor(total[:, :], total[:, :], 0.4, unit[:, :], ALU.mult, ALU.add)
                dve.drain()
                dve.tensor_tensor(value[:, here], total[:, :], weight[:, here], ALU.mult).then_inc(s_value.sem, 1)
                dve.tensor_scalar(wsum[:, :], weight[:, here], float(ramp(WIN - 1, WIN)), None, ALU.mult)
                for sh in range(1, WIN):
                    dve.drain()
                    dve.scalar_tensor_tensor(wsum[:, :], weight[:, bass.ds(n * TB + (H - sh), TB)],
                                             float(ramp(WIN - 1 - sh, WIN)), wsum[:, :], ALU.mult, ALU.add)
                dve.drain()
                dve.tensor_scalar(wsum[:, :], wsum[:, :], 1e-8, None, ALU.max)
                dve.drain()
                dve.reciprocal(wsum[:, :], wsum[:, :])
                dve.drain()
                dve.wait_ge(s_out.sem, s_out.at(n))
                dve.tensor_tensor(diff[:, :], k.bank[7][:, :], wsum[:, :], ALU.mult)
                dve.drain()
                if first:
                    table = w["first"].rearrange("p (a b) -> p a b", b=WIN)
                    for j, t in enumerate((value, weight)):
                        dve.tensor_tensor(early[:, j, :, :], t[:, H:H + WIN].unsqueeze(1).to_broadcast([P, WIN, WIN]),
                                          table, ALU.mult)
                    dve.drain()
                    dve.tensor_reduce(early_sum[:, :, :].rearrange("p j a -> p (j a)"),
                                      early[:, :, :, :].rearrange("p j a b -> p (j a) b"), AX.X, ALU.add)
                    dve.drain()
                    dve.tensor_scalar(early_sum[:, 1, :], early_sum[:, 1, :], 1e-8, None, ALU.max)
                    dve.drain()
                    dve.reciprocal(early_sum[:, 1, :], early_sum[:, 1, :])
                    dve.drain()
                    dve.tensor_tensor(diff[:, 0:WIN], early_sum[:, 0, :], early_sum[:, 1, :], ALU.mult)
                    dve.drain()
                xb = k.x[:, bass.ts(n, TB)]
                dve.tensor_tensor(xb, xb, diff[:, :], ALU.add).then_inc(s_done.sem, 1)

            body(0, True)
            with dve.Fori(1, NB) as n:
                body(n, False)

    norm.passed()
    k.passed({x: NB + (x in ("win_diff", "win_exp")) for x in names})


def softmax_attention(k, w, scratch):
    nc = k.nc
    HEADS, HD, GH = 16, 8, 4
    GROUPS, KT, QB = HEADS // GH, T // P, NB
    STEPS = GROUPS * QB
    SCALE = HD ** -0.5
    M_ROW = 96

    with ExitStack() as s:
        st = lambda name, shape, dt=F32: s.enter_context(nc.sbuf_tensor(k.fresh(name), shape, dt))
        xn = k.big_tail[:, 0:T]
        q_ops = k.big_low[:, 0:8192].bitcast(BF16).rearrange("p (b h t) -> p b h t", b=2, h=GH)
        v_group = k.big_low[:, 8192:8192 + KT * GH * 32].rearrange("p (t h m) -> p t h m", h=GH, m=32)
        k_ops = st("k_ops", [P, 2, GH, T], BF16)

        with ExitStack() as s1:
            st1 = Carve(k.probs[:, :])
            norm = Norm(k, st1, xn)
            parts = st1("qk_parts", [P, 2, 3, TB], BF16)
            whole = k.big_low[:, 8192:8192 + 4 * TB].rearrange("p (a t) -> p a t", a=4)
            pre, out, split, kept = (k.counter(x) for x in ("qk_pre", "qk_out", "qk_split", "qk_kept"))
            with nc.Block() as block:
                @block.gpsimd
                def _(pool):
                    pool.memset(q_ops[64:128, :, :, :], 0.0)
                    pool.memset(k_ops[64:128, :, :, :], 0.0)
                    pool.drain()
                    pool.memset(k_ops[M_ROW:M_ROW + 3, :, :, :], 1.0)

                @block.tensor
                def _(pe):
                    with pe.Fori(0, NB) as n:
                        norm.pe_centre(pe, n)
                        norm.pe_variance(pe, n)
                        pe.wait_ge(norm.normed.sem, norm.normed.at(n))
                        for j in range(2):
                            pe.wait_ge(out.sem, out.at(n * 2 + j - 2))
                            pe.matmul(k.bank[2 + j][:, :], w["qk"][:, j, :], xn[:, bass.ts(n, TB)],
                                      start=True, stop=True).then_inc(pre.sem, 1)

                @block.scalar
                def _(act):
                    with act.Fori(0, NB) as n:
                        norm.act_square(act, n)
                        norm.act_deviation(act, n)
                        for j in range(2):
                            act.wait_ge(pre.sem, pre.at(n * 2 + j))
                            act.wait_ge(split.sem, split.at(n * 2 + j - 2))
                            act.activation(whole[:, j, :], k.bank[2 + j][:, :], ACT.Identity,
                                           bias=w["qk_bias"][:, j:j + 1]).then_inc(out.sem, 1)

                @block.vector
                def _(dve):
                    with dve.Fori(0, NB) as n:
                        norm.dve_norm(dve, n)
                        for j in range(2):
                            dve.wait_ge(out.sem, out.at(n * 2 + j))
                            dve.wait_ge(kept.sem, n * 96 + kept.start)
                            left = whole[:, j, :]
                            for part in range(3):
                                last = dve.tensor_copy(parts[:, j, part, :], left)
                                dve.drain()
                                if part < 2:
                                    dve.tensor_tensor(whole[:, 2 + j, :], left, parts[:, j, part, :], ALU.subtract)
                                    dve.drain()
                                    left = whole[:, 2 + j, :]
                            dve.drain().then_inc(split.sem, 1)

                @block.sync
                def _(sp):
                    with sp.Fori(0, NB) as n:
                        for j in range(2):
                            sp.wait_ge(split.sem, split.at(n * 2 + j))
                            for part in range(3):
                                sp.dma_start(scratch[j, part, :, bass.ts(n, TB)],
                                             parts[:, j, part, :]).then_inc(kept.sem, 16)
                    sp.wait_ge(kept.sem, LEAD + NB * 6 * 16)

            norm.passed()
            k.passed({"qk_pre": 2 * NB, "qk_out": 2 * NB, "qk_split": 2 * NB})

        st = Carve(k.big_low[:, 8192 + KT * GH * 32:12500])
        highest = st("highest", [P, GH * TPB, 4])
        neg_max = st("neg_max", [P, GH * TPB])
        max_rest = st("max_rest", [P, GH * TPB])
        max_parts = st("max_parts", [P, P], BF16)
        max_rows = st("max_rows", [3 * GH * TPB, P], BF16)
        probs = k.probs[:, :].rearrange("p (b h t) -> p b h t", b=2, h=GH)
        sums = st("sums", [P, TB])
        recip = st("recip", [P, TB])
        w_out = st("w_out", [P, D])
        loaded, max_loaded = k.counter("operands_loaded"), k.counter("max_loaded")
        (row_scores, row_max, max_split, max_turned, max_out, scores, expd, summed, sums_out,
         spread, normalised, y_ready, x_done, v_pre, v_ready, w_ready) = (k.counter(x) for x in (
            "row_scores", "row_max", "max_split", "max_turned", "max_out", "scores", "exponentials", "summed",
            "sums_out", "sums_spread", "normalised", "y_ready", "x_done", "v_pre", "v_ready",
            "w_out_ready"))
        block = s.enter_context(nc.Block())
        ROWS_IN = 16 * 3 * GH
        LOADS = 18

        @block.sync
        def _(sp):
            def load_group(g, after):
                if after is not None:
                    sp.wait_ge(scores.sem, scores.at(after))
                if g > 0:
                    sp.wait_ge(loaded.sem, g * 16 * LOADS + loaded.start)
                for qp in range(3):
                    for kp in range(3):
                        r = (qp * 3 + kp) * HD
                        for j, ops, part in ((0, q_ops, qp), (1, k_ops, kp)):
                            src = scratch[j, part, bass.ds(g * (GH * HD), GH * HD), :]
                            sp.dma_start(ops[r:r + HD, g % 2, :, :],
                                         src.rearrange("(h d) t -> d h t", d=HD)).then_inc(loaded.sem, 16)

            def put_max(i):
                sp.wait_ge(max_out.sem, max_out.at(i))
                if i > 0:
                    sp.wait_ge(max_loaded.sem, i * ROWS_IN + max_loaded.start)
                g, qb = i // QB, i % QB
                for r in range(3 * GH):
                    part, h = r // GH, r % GH
                    sp.dma_start(q_ops[M_ROW + part:M_ROW + part + 1, g % 2, h, bass.ts(qb, TB)],
                                 max_rows[r * TPB:(r + 1) * TPB, :]).then_inc(max_loaded.sem, 16)

            load_group(0, None)
            load_group(1, None)
            for i in range(QB):
                put_max(i)
            load_group(2, QB * KT * 2 - 1)
            for i in range(QB, 2 * QB):
                put_max(i)
            load_group(3, 2 * QB * KT * 2 - 1)
            for i in range(2 * QB, STEPS):
                put_max(i)

        @block.gpsimd
        def _(pool):
            with pool.Fori(0, GROUPS) as g:
                pool.wait_ge(y_ready.sem, y_ready.at(g * QB - 1))
                pool.tensor_copy(w_out[:, :], w["out"][:, bass.ts(g, D)]).then_inc(w_ready.sem, 1)

        @block.tensor
        def _(pe):
            def row_unit(i, g, qb, u):
                h, qt = u // TPB, u % TPB
                for kb in range(4):
                    a = i * (16 * 4) + (u * 4 + kb)
                    pe.wait_ge(row_max.sem, row_max.at(a - 2))
                    pe.matmul(k.bank[kb % 2][:, :], q_ops[:, g % 2, h, bass.ds(qb * TB + qt * P, P)],
                              k_ops[:, g % 2, h, kb * TB:(kb + 1) * TB],
                              start=True, stop=True).then_inc(row_scores.sem, 1)

            def turn_max(i):
                pe.wait_ge(max_split.sem, max_split.at(i))
                pe.wait_ge(x_done.sem, x_done.at(i - 3))
                pe.wait_ge(v_ready.sem, v_ready.at(0))
                pe.transpose(k.bank[7][:, 0:P // 2].bitcast(BF16), max_parts[:, :],
                             k.ident_bf[:, :]).then_inc(max_turned.sem, 1)

            def score_pair(i, g, qb, kt, hp):
                b = i * (KT * 2) + (kt * 2 + hp)
                pe.wait_ge(expd.sem, expd.at(b - 2))
                for j in range(2):
                    mm = pe.matmul(k.bank[2 + 2 * hp + j][:, :], k_ops[:, g % 2, 2 * hp + j, kt * P:(kt + 1) * P],
                                   q_ops[:, g % 2, 2 * hp + j, bass.ts(qb, TB)], start=True, stop=True)
                mm.then_inc(scores.sem, 1)

            def sum_values(i, kt):
                pe.wait_ge(expd.sem, expd.at(i * (KT * 2) + (kt * 2 + 1)))
                if kt == 0:
                    pe.wait_ge(sums_out.sem, sums_out.at(i - 1))
                for h in range(GH):
                    mm = pe.matmul(k.bank[6][32 * h:32 * h + 32, :], v_group[:, kt, h, :],
                                   probs[:, kt % 2, h, :], start=(kt == 0), stop=(kt == KT - 1))
                mm.then_inc(summed.sem, 1)

            def spread_sums(i, turned):
                pe.wait_ge(sums_out.sem, sums_out.at(i))
                pe.wait_ge(x_done.sem, x_done.at(i - 1))
                if turned:
                    pe.wait_ge(max_out.sem, max_out.at(i + 2))
                pe.matmul(k.bank[7][:, :], w["spread"], sums[:, :], start=True, stop=True).then_inc(spread.sem, 1)

            def project(i, g):
                pe.wait_ge(normalised.sem, normalised.at(i))
                pe.wait_ge(w_ready.sem, w_ready.at(g))
                pe.matmul(k.bank[7][:, :], w_out[:, :], sums[:, :], start=True, stop=True).then_inc(y_ready.sem, 1)

            def values(g):
                pe.wait_ge(x_done.sem, x_done.at(g * QB - 2))
                for kt in range(KT):
                    mm = pe.matmul(k.bank[7][:, kt * 32:(kt + 1) * 32], xn[:, kt * P:(kt + 1) * P],
                                   w["v"][:, bass.ds(g * 32, 32)], start=True, stop=True)
                mm.then_inc(v_pre.sem, 1)

            def step(i, g, qb, ahead, turn, tail, before=None):
                pe.wait_ge(max_loaded.sem, i * ROWS_IN + (ROWS_IN + max_loaded.start))
                for hp in range(2):
                    score_pair(i, g, qb, 0, hp)
                for kt in range(KT):
                    if kt + 1 < KT:
                        for hp in range(2):
                            score_pair(i, g, qb, kt + 1, hp)
                    if ahead is not None:
                        row_unit(i + 2, *ahead, kt)
                    if kt == 0:
                        pe.wait_ge(v_ready.sem, v_ready.at(g))
                    sum_values(i, kt)
                    if kt == 1 and turn:
                        turn_max(i + 1)
                    if kt == 4 and tail:
                        spread_sums(i - 1, turn)
                    if kt == 8 and tail:
                        project(i - 1, g if before is None else before)

            def wait_operands(g):
                pe.wait_ge(loaded.sem, g * (16 * LOADS) + (16 * LOADS + loaded.start))

            wait_operands(0)
            values(0)
            for i in range(2):
                for u in range(16):
                    row_unit(i, 0, i, u)
                if i == 0:
                    turn_max(0)
            step(0, 0, 0, (0, 2), True, False)
            step(1, 0, 1, (0, 3), True, True)
            wait_operands(1)
            with pe.Fori(0, 2) as qb:
                step(qb + 2, 0, qb + 2, (1, qb), True, True)
            with pe.Fori(1, GROUPS - 1) as g:
                values(g)
                with pe.Fori(0, 2) as qb:
                    step(g * QB + qb, g, qb, (g, qb + 2), True, True, g - 1 + qb)
                with pe.Fori(0, 2) as qb:
                    wait_operands(g + 1)
                    step(g * QB + qb + 2, g, qb + 2, (g + 1, qb), True, True)
            g = GROUPS - 1
            values(g)
            with pe.Fori(0, 2) as qb:
                step(qb + g * QB, g, qb, (g, qb + 2), True, True, qb + (g - 1))
            step(STEPS - 2, g, 2, None, True, True)
            step(STEPS - 1, g, 3, None, False, True)
            pe.wait_ge(sums_out.sem, sums_out.at(STEPS - 1))
            pe.wait_ge(x_done.sem, x_done.at(STEPS - 2))
            pe.matmul(k.bank[7][:, :], w["spread"], sums[:, :], start=True, stop=True).then_inc(spread.sem, 1)
            project(STEPS - 1, GROUPS - 1)

        @block.scalar
        def _(act):
            def max_rows_out(i):
                act.wait_ge(max_turned.sem, max_turned.at(i))
                act.wait_ge(max_loaded.sem, i * ROWS_IN + max_loaded.start)
                act.activation(max_rows[:, :], k.bank[7][0:3 * GH * TPB, 0:P // 2].bitcast(BF16),
                               ACT.Copy).then_inc(max_out.sem, 1)

            def exponentials(i, kt, hp):
                b = i * (KT * 2) + (kt * 2 + hp)
                act.wait_ge(scores.sem, scores.at(b))
                act.wait_ge(summed.sem, summed.at(i * KT + kt - 2))
                both = k.pair[hp]
                act.activation(probs[:, kt % 2, 2 * hp:2 * hp + 2, :].rearrange("p h q -> p (h q)"), both,
                               ACT.Exp, scale=SCALE).then_inc(expd.sem, 1)

            def step(i, turn):
                for kt in range(KT):
                    for hp in range(2):
                        exponentials(i, kt, hp)
                    if kt == 2 and turn:
                        max_rows_out(i + 1)
                act.wait_ge(summed.sem, summed.at(i * KT + (KT - 1)))
                act.wait_ge(y_ready.sem, y_ready.at(i - 1))
                act.activation(sums[:, :], k.bank[6][:, :], ACT.Copy).then_inc(sums_out.sem, 1)

            max_rows_out(0)
            with act.Fori(0, STEPS - 1) as i:
                step(i, True)
            step(STEPS - 1, False)

        @block.vector
        def _(dve):
            def row_unit(i, u):
                for kb in range(4):
                    dve.wait_ge(row_scores.sem, row_scores.at(i * 64 + (u * 4 + kb)))
                    dve.tensor_reduce(highest[:, u, kb:kb + 1], k.bank[kb % 2][:, :], AX.X,
                                      ALU.max).then_inc(row_max.sem, 1)

            def split_max(i):
                dve.drain()
                dve.tensor_reduce(neg_max[:, :], highest[:, :, :], AX.X, ALU.max, negate=True)
                dve.drain()
                n = GH * TPB
                dve.wait_ge(max_turned.sem, max_turned.at(i - 1))
                left = neg_max[:, :]
                for part in range(3):
                    dve.tensor_copy(max_parts[:, part * n:(part + 1) * n], left)
                    dve.drain()
                    if part < 2:
                        dve.tensor_tensor(max_rest[:, :], left, max_parts[:, part * n:(part + 1) * n], ALU.subtract)
                        dve.drain()
                        left = max_rest[:, :]
                dve.drain().then_inc(max_split.sem, 1)

            def values(g):
                dve.wait_ge(v_pre.sem, v_pre.at(g))
                dve.wait_ge(summed.sem, summed.at(g * (QB * KT) - 1))
                dve.tensor_tensor(v_group[:, :, :, 0:HD],
                                  k.bank[7][:, :].rearrange("p (t h d) -> p t h d", h=GH, d=HD),
                                  w["v_bias"][:, bass.ds(g * 32, 32)].rearrange("p (h d) -> p h d", d=HD)
                                  .unsqueeze(1).to_broadcast([P, KT, GH, HD]), ALU.add).then_inc(v_ready.sem, 1)

            def normalise(i):
                dve.wait_ge(spread.sem, spread.at(i))
                dve.reciprocal(recip[:, :], k.bank[7][:, :])
                dve.drain()
                dve.tensor_tensor(sums[:, :], sums[:, :], recip[:, :], ALU.mult).then_inc(normalised.sem, 1)

            def add_to_x(i):
                dve.wait_ge(y_ready.sem, y_ready.at(i))
                xb = k.x[:, bass.ts(i % QB, TB)]
                dve.tensor_tensor(xb, k.bank[7][:, :], xb, ALU.add).then_inc(x_done.sem, 1)

            def step(i, ahead, tail):
                for kt in range(KT):
                    if ahead:
                        row_unit(i + 2, kt)
                    if kt == 5 and tail:
                        normalise(i - 1)
                    if kt == 9 and tail:
                        add_to_x(i - 1)
                if ahead:
                    split_max(i + 2)

            dve.memset(v_group[:, :, :, :], 0.0)
            dve.memset(max_parts[:, :], 0.0)
            dve.drain()
            dve.memset(v_group[:, :, :, HD:HD + 1], 1.0)
            dve.drain()
            values(0)
            for i in range(2):
                for u in range(16):
                    row_unit(i, u)
                split_max(i)
            step(0, True, False)
            with dve.Fori(1, QB) as i:
                step(i, True, True)
            with dve.Fori(1, GROUPS - 1) as g:
                values(g)
                with dve.Fori(0, QB) as qb:
                    step(g * QB + qb, True, True)
            g = GROUPS - 1
            values(g)
            with dve.Fori(g * QB, g * QB + 2) as i:
                step(i, True, True)
            step(STEPS - 2, False, True)
            step(STEPS - 1, False, True)
            normalise(STEPS - 1)
            add_to_x(STEPS - 1)
            dve.drain()
            dve.tensor_scalar(k.x[:, :], k.x[:, :], w["out_bias"], None, ALU.add)

    k.counters["qk_kept"].start += NB * 96
    k.counters["operands_loaded"].start += GROUPS * 16 * LOADS
    k.counters["max_loaded"].start += STEPS * ROWS_IN
    k.passed({"row_scores": STEPS * 64, "row_max": STEPS * 64, "max_split": STEPS, "max_turned": STEPS,
              "max_out": STEPS, "scores": STEPS * KT * 2, "exponentials": STEPS * KT * 2, "summed": STEPS * KT,
              "sums_out": STEPS, "sums_spread": STEPS, "normalised": STEPS,
              "y_ready": STEPS, "x_done": STEPS, "v_pre": GROUPS, "v_ready": GROUPS, "w_out_ready": GROUPS})


CH = 128
NCH = T // CH


def gated_kernel_attention(k, w, scratch):
    project_and_convolve(k, w, scratch)
    run_chunks(k, w, scratch)


def gate_columns(table):
    return {"g": table[..., 0:16], "alpha": table[..., 16:32], "beta": table[..., 32:36],
            "inv_k": table[..., 36:40], "alpha_sq": table[..., 40:56]}


GATES = 56


def project_and_convolve(k, w, scratch):
    nc = k.nc
    TILES, KTILE = 12, 8
    st = Carve(k.big_high)
    xn = st("xn", [P, TB])
    norm = Norm(k, st, xn, block_only=True)
    pre = st("pre", [P, 2, 3 + TB])
    acc = st("acc", [P, 2, TB])
    out = st("out", [P, 4, TB])
    halo = st("halo", [P, TILES, 4])
    k_sq = st("k_sq", [P, 2, TB])
    z = st("z", [P, NCH, 36])
    k_sum = st("k_sum", [P, NCH, 4])
    tmp = st("tmp", [P, NCH, 16])
    decay_rate = st("decay_rate", [P, 16])
    table = k.gates
    made, copied, convolved = (k.counter(n) for n in ("gka_made", "gka_copied", "gka_convolved"))
    kept = [k.counter(f"gka_kept_{b}") for b in range(4)]
    silu, squared, gates_made, gates_out = (k.counter(n) for n in ("gka_silu", "gka_k_squared", "gka_gates_made", "gka_gates_out"))
    act_step, dve_step = k.counter("gka_act_step"), k.counter("gka_dve_step")

    with nc.Block() as block:
        @block.tensor
        def _(pe):
            def chunk_gates(n):
                pe.wait_ge(gates_out.sem, gates_out.at(n - 1))
                for j in range(TPB):
                    pe.matmul(k.bank[4][:, j * 36:(j + 1) * 36], xn[:, j * P:(j + 1) * P], w["gates"],
                              start=True, stop=True)
                pe.wait_ge(squared.sem, squared.at(n * 2 + 1))
                for j in range(TPB):
                    for p in range(2):
                        mm = pe.matmul(k.bank[5][:, j * 4 + 2 * p:j * 4 + 2 * p + 2], k_sq[:, p, j * P:(j + 1) * P],
                                       w["half"], start=True, stop=True)
                mm.then_inc(gates_made.sem, 1)

            with pe.Fori(0, NB) as n:
                norm.pe_centre(pe, n)
                norm.pe_variance(pe, n)
                pe.wait_ge(norm.normed.sem, norm.normed.at(n))
                for j in range(TILES):
                    pe.wait_ge(copied.sem, copied.at(n * TILES + j - 2))
                    pe.matmul(k.bank[2 + j % 2][:, :], w["proj"][:, j, :], xn[:, :],
                              start=True, stop=True).then_inc(made.sem, 1)
                chunk_gates(n)

        @block.scalar
        def _(act):
            def copy(n, j):
                act.wait_ge(made.sem, made.at(n * TILES + j))
                act.wait_ge(convolved.sem, convolved.at(n * TILES + j - 2))
                act.activation(pre[:, j % 2, 3:3 + TB], k.bank[2 + j % 2][:, :], ACT.Copy)
                act.wait_ge(silu.sem, silu.at(n * TILES + j - 2))
                act.activation(acc[:, j % 2, :], k.bank[2 + j % 2][:, :], ACT.Copy,
                               scale=w["conv"][:, 4 * j + 3:4 * j + 4]).then_inc(copied.sem, 1)

            def finish(n, j):
                act.wait_ge(convolved.sem, convolved.at(n * TILES + j))
                act.wait_ge(kept[j % 4].sem, n * (16 * TILES // 4) + (16 * (j // 4) + kept[j % 4].start))
                if j == KTILE + 2:
                    act.wait_ge(squared.sem, squared.at(n * 2 + 1))
                act.activation(out[:, j % 4, :], acc[:, j % 2, :], ACT.Silu).then_inc(silu.sem, 1)

            with act.Fori(0, NB) as n:
                norm.act_square(act, n)
                norm.act_deviation(act, n)
                for j in range(TILES):
                    copy(n, j)
                    if j > 0:
                        finish(n, j - 1)
                finish(n, TILES - 1)
            act.wait_ge(dve_step.sem, dve_step.at(0))
            act.activation(k_sum[:, :, :], k_sum[:, :, :], ACT.Sqrt).then_inc(act_step.sem, 1)
            act.activation(decay_rate[:, :], w["A_log"], ACT.Exp)
            act.activation(z[:, :, 16:36], z[:, :, 16:36], ACT.Exp, scale=-1.0)
            act.activation(tmp[:, :, :], tmp[:, :, :], ACT.Exp, scale=-1.0)
            act.drain()
            act.activation(tmp[:, :, :], tmp[:, :, :], ACT.Ln, bias=w["one"]).then_inc(act_step.sem, 1)

        @block.gpsimd
        def _(pool):
            with pool.Fori(0, NB) as n:
                for p in range(2):
                    j = KTILE + p
                    pool.wait_ge(silu.sem, silu.at(n * TILES + j))
                    pool.wait_ge(gates_made.sem, gates_made.at(n - 1))
                    pool.tensor_tensor(k_sq[:, p, :], out[:, j % 4, :], out[:, j % 4, :],
                                       ALU.mult).then_inc(squared.sem, 1)

        @block.vector
        def _(dve):
            dve.memset(halo[:, :, :], 0.0)
            dve.drain()

            with dve.Fori(0, NB) as n:
                dve.wait_ge(gates_made.sem, gates_made.at(n - 1))
                norm.dve_norm(dve, n)
                for j in range(TILES):
                    b = j % 2
                    dve.wait_ge(copied.sem, copied.at(n * TILES + j))
                    dve.tensor_copy(pre[:, b, 0:3], halo[:, j, 0:3])
                    dve.drain()
                    for i in range(3):
                        dve.scalar_tensor_tensor(acc[:, b, :], pre[:, b, i:i + TB], w["conv"][:, 4 * j + i:4 * j + i + 1],
                                                 acc[:, b, :], ALU.mult, ALU.add)
                        dve.drain()
                    dve.tensor_copy(halo[:, j, 0:3], pre[:, b, TB:TB + 3])
                    dve.drain().then_inc(convolved.sem, 1)
                dve.wait_ge(gates_made.sem, gates_made.at(n))
                dve.tensor_scalar(z[:, bass.ts(n, TPB), :], k.bank[4][:, 0:TPB * 36].rearrange("p (c z) -> p c z", z=36),
                                  0.0, None, ALU.add)
                dve.tensor_scalar(k_sum[:, bass.ts(n, TPB), :], k.bank[5][:, 0:TPB * 4].rearrange("p (c z) -> p c z", z=4),
                                  0.0, None, ALU.add).then_inc(gates_out.sem, 1)
            dve.drain()
            za, t = z[:, :, 0:16], gate_columns(table)
            over = lambda a, m: a.unsqueeze(1).to_broadcast([P, NCH, m])
            dve.tensor_tensor(za, za, over(w["dt_bias"], 16), ALU.add)
            dve.drain()
            dve.scalar_tensor_tensor(tmp[:, :, :], za, -1.0, za, ALU.mult, ALU.max)
            dve.drain().then_inc(dve_step.sem, 1)
            dve.wait_ge(act_step.sem, act_step.at(1))
            dve.scalar_tensor_tensor(tmp[:, :, :], za, 0.0, tmp[:, :, :], ALU.max, ALU.add)
            dve.tensor_scalar(k_sum[:, :, :], k_sum[:, :, :], 1e-6, None, ALU.add)
            dve.tensor_scalar(z[:, :, 16:36], z[:, :, 16:36], 1.0, 1e30, ALU.add, ALU.min)
            dve.drain()
            dve.scalar_tensor_tensor(t["g"], tmp[:, :, :], -1.0, over(decay_rate[:, :], 16), ALU.mult, ALU.mult)
            dve.reciprocal(t["inv_k"], k_sum[:, :, :])
            dve.reciprocal(z[:, :, 16:36], z[:, :, 16:36])
            dve.drain()
            dve.tensor_scalar(t["alpha"], z[:, :, 16:32], 0.125, None, ALU.mult)
            dve.tensor_copy(t["beta"], z[:, :, 32:36])
            dve.drain()
            dve.tensor_tensor(t["alpha_sq"], t["alpha"], t["alpha"], ALU.mult)
            dve.drain()
            dve.tensor_scalar(t["alpha_sq"], t["alpha_sq"], 1.0 / 64, None, ALU.mult)

        @block.sync
        def _(sp):
            with sp.Fori(0, NB) as n:
                for j in range(TILES):
                    sp.wait_ge(silu.sem, silu.at(n * TILES + j))
                    sp.dma_start(scratch[bass.ts(n, TPB), :, j, :].rearrange("c p t -> p c t"),
                                 out[:, j % 4, :].rearrange("p (c t) -> p c t", t=CH)).then_inc(kept[j % 4].sem, 16)
            for b in range(4):
                sp.wait_ge(kept[b].sem, 16 * NB * TILES // 4 + kept[b].start)

    norm.passed()
    k.passed({"gka_made": NB * TILES, "gka_copied": NB * TILES, "gka_convolved": NB * TILES, "gka_silu": NB * TILES,
              **{f"gka_kept_{b}": 16 * NB * TILES // 4 for b in range(4)}, "gka_k_squared": NB * 2, "gka_gates_made": NB, "gka_gates_out": NB,
              "gka_act_step": 2, "gka_dve_step": 1})


def run_chunks(k, w, scratch):
    nc = k.nc
    G, R, HD, PAIRS = 4, 4, 64, 2
    st = Carve(k.big_high)
    qkv = [st(f"qkv{b}", [P, 12, CH]) for b in range(2)]
    gates = [st(f"gates{b}", [P, GATES]) for b in range(2)]
    k_pad = [st(f"k_pad{b}", [P, 2, PAIRS, CH]) for b in range(2)]
    kv = [st(f"kv{b}", [P, PAIRS, 2, 2, HD]) for b in range(2)]
    since = [st(f"since{b}", [P, PAIRS, R, CH]) for b in range(2)]
    decay = [k.probs[:, b * 2048:(b + 1) * 2048].rearrange("p (g r t) -> p g r t", g=G, r=R) for b in range(2)]
    until = [st(f"until{b}", [P, G, R]) for b in range(2)]
    g_masked = st("g_masked", [P, G, R, CH])
    kd = st("kd", [P, PAIRS, R, 2, HD])
    scores = st("scores", [P, G, R, CH])
    x_new = st("x_new", [P, PAIRS, R, CH])
    x_since = st("x_since", [P, PAIRS, R, CH])
    state = st("state", [P, PAIRS, R, 2, 2, HD])
    o = st("o", [P, PAIRS, R, 2, HD])
    o_sq = st("o_sq", [P, PAIRS, R, 2, HD])
    o_sum = st("o_sum", [P, PAIRS, R, 2])
    o_var = st("o_var", [P, PAIRS, R, 2])
    oT = st("oT", [P, PAIRS * R, CH])
    names = ("gka_loaded", "gka_gates", "gka_g_masked", "gka_decay_made", "gka_decay_out", "gka_turned", "gka_kv",
             "gka_k_pad", "gka_kd", "gka_scores", "gka_masked", "gka_u", "gka_x", "gka_x_since", "gka_o_out",
             "gka_state_made", "gka_state", "gka_o_var", "gka_o_sd", "gka_o_scaled", "gka_o_turned",
             "gka_oT", "gka_y", "gka_x_done")
    (loaded, gates_here, g_ready, decay_made, decay_out, turned, kv_ready, k_pad_ready, kd_ready, scored, masked,
     u_made, x_ready, since_ready, o_out, state_made, state_ready, var_ready, sd_ready, o_scaled, o_turned, oT_ready,
     y_ready, x_done) = (k.counter(n) for n in names)
    flat = lambda t: t.rearrange("p r t -> p (r t)")
    PREP = 7

    def reused(c):
        return not isinstance(c, int) or c >= 2

    def each_chunk(eng, prologue, chunk, epilogue):
        prologue()
        chunk(0, 0, True, False)
        with eng.Fori(0, (NCH - 2) // 2) as i:
            chunk(i * 2 + 1, 1, True, True)
            chunk(i * 2 + 2, 0, True, True)
        chunk(NCH - 1, 1, False, True)
        epilogue()

    with nc.Block() as block:
        @block.sync
        def _(sp):
            def load(c, b):
                sp.dma_start(qkv[b][:, :, :], scratch[bass.ds(c, 1), :, :, :].rearrange("c p j t -> p (c j) t")
                             ).then_inc(loaded.sem, 16)

            load(0, 0)

            def chunk(c, b, nxt, prev):
                if nxt:
                    sp.wait_ge(u_made.sem, u_made.at(c * 6 - 1))
                    sp.wait_ge(loaded.sem, c * 16 + (16 + loaded.start))
                    load(c + 1, 1 - b)

            each_chunk(sp, lambda: None, chunk, lambda: None)

        @block.tensor
        def _(pe):
            def made(c, i):
                return decay_made.at(c * PREP + i)

            def prep(c, b, i):
                bank = k.bank[i % 2]
                if i < 4:
                    if i == 0:
                        pe.wait_ge(kv_ready.sem, kv_ready.at(c - 1))
                    pe.wait_ge(decay_out.sem, decay_out.at(c * PREP + (i - 1 if i == 1 else i - 2)))
                    pe.wait_ge(g_ready.sem, g_ready.at(c * G + i))
                    pe.matmul(bank[:, :], w["later"], flat(g_masked[:, i, :, :]), start=True, stop=False)
                    pe.matmul(bank[:, :], k.ident_bf[:, :], k.mask_bf[:, :], start=False,
                              stop=True).then_inc(decay_made.sem, 1)
                elif i < 6:
                    p = i - 4
                    pe.wait_ge(decay_out.sem, decay_out.at(c * PREP + i - 2))
                    for half in range(2):
                        mm = pe.matmul(bank[64 * half:64 * half + 64, :], w["ones"][:, 0:64],
                                       flat(g_masked[:, 2 * p + half, :, :]), start=True, stop=True)
                    mm.then_inc(decay_made.sem, 1)
                elif i == 6:
                    pe.wait_ge(loaded.sem, c * 16 + (16 + loaded.start))
                    pe.wait_ge(decay_out.sem, decay_out.at(c * PREP + 4))
                    for j in range(4):
                        mm = pe.transpose(bank[:, j * P:(j + 1) * P], qkv[b][:, 8 + j, :], k.ident[:, :])
                    mm.then_inc(turned.sem, 1)
                else:
                    pe.wait_ge(decay_out.sem, decay_out.at(c * PREP + 5))
                    pe.matmul(bank[:, 0:16], w["later"], gates[b][:, 0:16], start=True, stop=True).then_inc(decay_made.sem, 1)

            def score(c, b, u):
                if u == 0:
                    pe.wait_ge(k_pad_ready.sem, k_pad_ready.at(c))
                for g in range(G):
                    p, half = g // 2, g % 2
                    if u > 0 and half == 0:
                        pe.wait_ge(x_ready.sem, x_ready.at(c * 4 + (2 * (u - 1) + p)))
                    pe.wait_ge(masked.sem, masked.at(c * 12 + (u * 4 + g - 2)))
                    x = qkv[b][:, 4 * p:4 * p + 4, :] if u == 0 else x_new[:, p, :, :]
                    pe.matmul(k.bank[2 + half][:, :], k_pad[b][:, half, p, :], flat(x),
                              start=True, stop=True).then_inc(scored.sem, 1)

            def product(c, b, u):
                for p in range(PAIRS):
                    if u == 0:
                        pe.wait_ge(state_ready.sem, state_ready.at(c * 4 - 1))
                        pe.wait_ge(o_out.sem, o_out.at(c * 2 + p - 2))
                        pe.wait_ge(kv_ready.sem, kv_ready.at(c))
                    pe.wait_ge(since_ready.sem, since_ready.at(c * 6 + (2 * u + p)))
                    for r in range(R):
                        pe.matmul(k.bank[4 + p][:, r * CH:(r + 1) * CH], state[:, p, r, 0, :, :].rearrange("p h f -> p (h f)"),
                                  x_since[:, p, r, :], start=(r == 0), stop=False)
                    for half in range(2):
                        g = 2 * p + half
                        pe.wait_ge(masked.sem, masked.at(c * 12 + (u * 4 + g)))
                        mm = pe.matmul(k.bank[4 + p][64 * half:64 * half + 64, :], kv[b][:, p, 0, half, :],
                                       flat(scores[:, g, :, :]), start=False, stop=True)
                    mm.then_inc(u_made.sem, 1)

            def output(c, b):
                for p in range(PAIRS):
                    pe.wait_ge(since_ready.sem, since_ready.at(c * 6 + (4 + p)))
                    pe.wait_ge(masked.sem, masked.at(c * 12 + (8 + 2 * p + 1)))
                    for r in range(R):
                        cols = k.bank[4 + p][:, r * CH:(r + 1) * CH]
                        pe.matmul(cols, x_since[:, p, r, :], state[:, p, r, 1, :, :].rearrange("p h f -> p (h f)"),
                                  start=(r == 0), stop=False)
                        for half in range(2):
                            mm = pe.matmul(cols[:, 64 * half:64 * half + 64], scores[:, 2 * p + half, r, :],
                                           kv[b][:, p, 1, half, :], start=False,
                                           stop=(r == R - 1 and half == 1))
                    mm.then_inc(u_made.sem, 1)

            def new_state(c, b):
                for i in range(4):
                    if i == 0:
                        pe.wait_ge(kd_ready.sem, kd_ready.at(c * 2))
                        pe.wait_ge(x_done.sem, x_done.at(c - 1))
                    elif i == 2:
                        pe.wait_ge(kd_ready.sem, kd_ready.at(c * 2 + 1))
                    if i == 1:
                        pe.wait_ge(oT_ready.sem, oT_ready.at(c * 2 - 1))
                    if i > 1:
                        pe.wait_ge(state_ready.sem, state_ready.at(c * 4 + (i - 2)))
                    for j in range(2):
                        p, r = i // 2, 2 * (i % 2) + j
                        mm = pe.matmul(k.bank[6 + i % 2][:, j * 256:(j + 1) * 256],
                                       kd[:, p, r, :, :].rearrange("p h f -> p (h f)"),
                                       kv[b][:, p, :, :, :].rearrange("p v h f -> p (v h f)"), start=True, stop=True)
                    mm.then_inc(state_made.sem, 1)

            def turn_o(c):
                pe.wait_ge(o_scaled.sem, o_scaled.at(c))
                pe.wait_ge(state_ready.sem, state_ready.at(c * 4 + 3))
                for p in range(PAIRS):
                    for r in range(R):
                        mm = pe.transpose(k.bank[6 + p][:, r * CH:(r + 1) * CH], o[:, p, r, :, :].rearrange("p h f -> p (h f)"),
                                          k.ident[:, :])
                    mm.then_inc(o_turned.sem, 1)

            def project(c):
                pe.wait_ge(oT_ready.sem, oT_ready.at(c * 2 + 1))
                for i in range(8):
                    mm = pe.matmul(k.bank[6][:, 0:CH], w["out"][:, i, :], oT[:, i, :], start=(i == 0), stop=(i == 7))
                mm.then_inc(y_ready.sem, 1)

            def chunk(c, b, nxt, prev):
                score(c, b, 0)
                product(c, b, 0)
                score(c, b, 1)
                if nxt:
                    prep(c + 1, 1 - b, 0)
                    prep(c + 1, 1 - b, 1)
                product(c, b, 1)
                score(c, b, 2)
                if nxt:
                    for i in range(2, 6):
                        prep(c + 1, 1 - b, i)
                if prev:
                    turn_o(c - 1)
                if nxt:
                    prep(c + 1, 1 - b, 6)
                output(c, b)
                if nxt:
                    prep(c + 1, 1 - b, 7)
                if prev:
                    project(c - 1)
                new_state(c, b)

            def prologue():
                for i in range(8):
                    prep(0, 0, i)

            def epilogue():
                turn_o(NCH - 1)
                project(NCH - 1)

            each_chunk(pe, prologue, chunk, epilogue)

        @block.scalar
        def _(act):
            def prep_copies(c, b):
                if reused(c):
                    act.wait_ge(u_made.sem, u_made.at(c * 6 - 7))
                    act.wait_ge(decay_made.sem, decay_made.at(c * PREP - PREP - 1))
                act.activation(gates[b][:, :], k.gates[:, bass.ds(c, 1), :].rearrange("p c z -> p (c z)"), ACT.Copy).then_inc(gates_here.sem, 1)
                act.wait_ge(loaded.sem, c * 16 + (16 + loaded.start))
                for half in range(2):
                    last = act.activation(k_pad[b][:, half, :, :], qkv[b][:, 8:10, :], ACT.Copy, scale=w["half"][:, half:half + 1])
                last.then_inc(k_pad_ready.sem, 1)

            def prep(c, b, i):
                act.wait_ge(decay_made.sem, decay_made.at(c * PREP + i))
                if i == 0 and reused(c):
                    act.wait_ge(state_ready.sem, state_ready.at(c * 4 - 5))
                bank = k.bank[i % 2]
                if i < 4:
                    act.activation(flat(decay[b][:, i, :, :]), bank[:, :], ACT.Exp).then_inc(decay_out.sem, 1)
                elif i < 6:
                    act.activation(flat(since[b][:, i - 4, :, :]), bank[:, :], ACT.Exp).then_inc(decay_out.sem, 1)
                else:
                    act.activation(until[b][:, :, :].rearrange("p g r -> p (g r)"), k.bank[1][:, 0:16],
                                   ACT.Exp).then_inc(decay_out.sem, 1)

            def o_copies(c):
                act.wait_ge(o_turned.sem, o_turned.at(c * 2 - 1))
                for p in range(PAIRS):
                    act.wait_ge(u_made.sem, u_made.at(c * 6 + (4 + p)))
                    fl = lambda t: t[:, p, :, :, :].rearrange("p r h f -> p (r h f)")
                    act.activation(fl(o_sq), k.bank[4 + p][:, :], ACT.Square)
                    act.activation(fl(o), k.bank[4 + p][:, :], ACT.Copy).then_inc(o_out.sem, 1)

            def deviation(c):
                act.wait_ge(var_ready.sem, var_ready.at(c))
                act.activation(o_var[:, :, :, :], o_var[:, :, :, :], ACT.Sqrt).then_inc(sd_ready.sem, 1)

            def oT_copies(c):
                act.wait_ge(y_ready.sem, y_ready.at(c - 1))
                for p in range(PAIRS):
                    act.wait_ge(o_turned.sem, o_turned.at(c * 2 + p))
                    act.activation(flat(oT[:, 4 * p:4 * p + 4, :]), k.bank[6 + p][:, :], ACT.Copy,
                                   scale=w["norm_w"]).then_inc(oT_ready.sem, 1)

            def chunk(c, b, nxt, prev):
                if nxt:
                    prep_copies(c + 1, 1 - b)
                if prev:
                    deviation(c - 1)
                if nxt:
                    for i in range(6):
                        prep(c + 1, 1 - b, i)
                if prev:
                    oT_copies(c - 1)
                if nxt:
                    prep(c + 1, 1 - b, 6)
                o_copies(c)

            def prologue():
                prep_copies(0, 0)
                for i in range(7):
                    prep(0, 0, i)

            def epilogue():
                deviation(NCH - 1)
                oT_copies(NCH - 1)

            each_chunk(act, prologue, chunk, epilogue)

        @block.gpsimd
        def _(pool):
            def mask_g(c, b, gs):
                if gs[0] == 0:
                    pool.wait_ge(gates_here.sem, gates_here.at(c))
                for g in gs:
                    pool.wait_ge(decay_made.sem, decay_made.at(c * PREP - 2))
                    pool.tensor_tensor(g_masked[:, g, :, :], gates[b][:, 4 * g:4 * g + 4].unsqueeze(2).to_broadcast([P, R, CH]),
                                       w["upto"].unsqueeze(1).to_broadcast([P, R, CH]), ALU.mult).then_inc(g_ready.sem, 1)

            def scale_x(c, b, u):
                for p in range(PAIRS):
                    if u == 0:
                        pool.wait_ge(decay_out.sem, decay_out.at(c * PREP + 5))
                        pool.wait_ge(loaded.sem, c * 16 + (16 + loaded.start))
                        x = qkv[b][:, 4 * p:4 * p + 4, :]
                    else:
                        pool.wait_ge(x_ready.sem, x_ready.at(c * 4 + (2 * (u - 1) + p)))
                        x = x_new[:, p, :, :]
                    pool.wait_ge(u_made.sem, u_made.at(c * 6 + (2 * u + p - 2)))
                    pool.tensor_tensor(x_since[:, p, :, :], x, since[b][:, p, :, :], ALU.mult).then_inc(since_ready.sem, 1)

            def keys_until(c, b):
                pool.wait_ge(kv_ready.sem, kv_ready.at(c))
                pool.wait_ge(decay_out.sem, decay_out.at(c * PREP + 6))
                for p in range(PAIRS):
                    pool.wait_ge(state_made.sem, state_made.at(c * 4 - 1))
                    keys = kv[b][:, p, 0, :, :].unsqueeze(1).to_broadcast([P, R, 2, HD])
                    by = until[b][:, 2 * p:2 * p + 2, :].rearrange("p h r -> p r h").unsqueeze(3).to_broadcast([P, R, 2, HD])
                    pool.tensor_tensor(kd[:, p, :, :, :], keys, by, ALU.mult).then_inc(kd_ready.sem, 1)

            def chunk(c, b, nxt, prev):
                scale_x(c, b, 0)
                if nxt:
                    mask_g(c + 1, 1 - b, (0, 1))
                scale_x(c, b, 1)
                if nxt:
                    mask_g(c + 1, 1 - b, (2, 3))
                scale_x(c, b, 2)
                keys_until(c, b)

            each_chunk(pool, lambda: mask_g(0, 0, (0, 1, 2, 3)), chunk, lambda: None)

        @block.vector
        def _(dve):
            def mask_scores(c, b, u):
                for g in range(G):
                    dve.wait_ge(scored.sem, scored.at(c * 12 + (u * 4 + g)))
                    if u == 0 and g == 0:
                        dve.wait_ge(decay_out.sem, decay_out.at(c * PREP + 3))
                        dve.wait_ge(gates_here.sem, gates_here.at(c))
                    dve.wait_ge(u_made.sem, u_made.at(c * 6 + (2 * u + g // 2 - 2)))
                    dve.scalar_tensor_tensor(flat(scores[:, g, :, :]), k.bank[2 + g % 2][:, :], gates[b][:, 36 + g:37 + g],
                                             flat(decay[b][:, g, :, :]), ALU.mult, ALU.mult).then_inc(masked.sem, 1)

            def next_x(c, b, u):
                for p in range(PAIRS):
                    dve.wait_ge(u_made.sem, u_made.at(c * 6 + (2 * u + p)))
                    dve.scalar_tensor_tensor(flat(x_new[:, p, :, :]), k.bank[4 + p][:, :], -0.25,
                                             flat(qkv[b][:, 4 * p:4 * p + 4, :]), ALU.mult, ALU.add).then_inc(x_ready.sem, 1)

            def keys_values(c, b):
                dve.wait_ge(turned.sem, turned.at(c))
                dve.wait_ge(gates_here.sem, gates_here.at(c))
                if reused(c):
                    dve.wait_ge(state_made.sem, state_made.at(c * 4 - 5))
                cols = k.bank[0][:, :].rearrange("p (v q f) -> p v q f", v=2, f=HD)
                for v, col in ((0, 36), (1, 32)):
                    for p in range(PAIRS):
                        last = dve.tensor_tensor(kv[b][:, p, v, :, :], cols[:, v, 2 * p:2 * p + 2, :],
                                                 gates[b][:, col + 2 * p:col + 2 * p + 2].unsqueeze(2).to_broadcast([P, 2, HD]),
                                                 ALU.mult)
                last.then_inc(kv_ready.sem, 1)

            def update_state(c, b):
                for i in range(4):
                    dve.wait_ge(state_made.sem, state_made.at(c * 4 + i))
                    for j in range(2):
                        p, r = i // 2, 2 * (i % 2) + j
                        add = k.bank[6 + i % 2][:, j * 256:(j + 1) * 256].rearrange("p (v h f) -> p v h f", v=2, h=2)
                        for half in range(2):
                            rows = slice(64 * half, 64 * half + 64)
                            last = dve.scalar_tensor_tensor(state[rows, p, r, :, half, :], state[rows, p, r, :, half, :],
                                                            since[b][rows, p, r, CH - 1:CH], add[rows, :, half, :],
                                                            ALU.mult, ALU.add)
                    last.then_inc(state_ready.sem, 1)

            def variance(c):
                dve.wait_ge(o_out.sem, o_out.at(c * 2 + 1))
                dve.tensor_reduce(o_sum[:, :, :, :].rearrange("p a r h -> p (a r h)"),
                                  o_sq[:, :, :, :, :].rearrange("p a r h f -> p (a r h) f"), AX.X, ALU.add)
                dve.drain()
                t = gate_columns(k.gates[:, bass.ds(c, 1), :])
                for p in range(PAIRS):
                    a = t["alpha_sq"][:, :, 8 * p:8 * p + 8].rearrange("p c (h r) -> p r (c h)", h=2)
                    dve.tensor_tensor(o_var[:, p, :, :], o_sum[:, p, :, :], a, ALU.mult)
                dve.drain()
                dve.tensor_scalar(o_var[:, :, :, :], o_var[:, :, :, :], 1e-6, None, ALU.add).then_inc(var_ready.sem, 1)

            def scale_o(c):
                dve.wait_ge(sd_ready.sem, sd_ready.at(c))
                dve.reciprocal(o_var[:, :, :, :], o_var[:, :, :, :])
                dve.drain()
                t = gate_columns(k.gates[:, bass.ds(c, 1), :])
                for p in range(PAIRS):
                    a = t["alpha"][:, :, 8 * p:8 * p + 8].rearrange("p c (h r) -> p r (c h)", h=2)
                    dve.tensor_tensor(o_var[:, p, :, :], o_var[:, p, :, :], a, ALU.mult)
                dve.drain()
                every = "p a r h f -> p (a r h) f"
                dve.tensor_tensor(o[:, :, :, :, :].rearrange(every), o[:, :, :, :, :].rearrange(every),
                                  o_var[:, :, :, :].rearrange("p a r h -> p (a r h)").unsqueeze(2).to_broadcast([P, 16, HD]),
                                  ALU.mult).then_inc(o_scaled.sem, 1)

            def add_to_x(c):
                dve.wait_ge(y_ready.sem, y_ready.at(c))
                xb = k.x[:, bass.ts(c, CH)]
                dve.tensor_tensor(xb, k.bank[6][:, 0:CH], xb, ALU.add).then_inc(x_done.sem, 1)

            def chunk(c, b, nxt, prev):
                mask_scores(c, b, 0)
                next_x(c, b, 0)
                if prev:
                    variance(c - 1)
                mask_scores(c, b, 1)
                if prev:
                    scale_o(c - 1)
                next_x(c, b, 1)
                mask_scores(c, b, 2)
                if nxt:
                    keys_values(c + 1, 1 - b)
                if prev:
                    add_to_x(c - 1)
                update_state(c, b)

            def prologue():
                dve.memset(state[:, :, :, :, :, :], 0.0)
                dve.drain()
                keys_values(0, 0)

            def epilogue():
                variance(NCH - 1)
                scale_o(NCH - 1)
                add_to_x(NCH - 1)

            each_chunk(dve, prologue, chunk, epilogue)

    k.passed({"gka_loaded": 16 * NCH, "gka_gates": NCH, "gka_g_masked": NCH * G, "gka_decay_made": NCH * PREP,
              "gka_decay_out": NCH * PREP, "gka_turned": NCH, "gka_kv": NCH, "gka_k_pad": NCH, "gka_kd": NCH * 2,
              "gka_scores": NCH * 12, "gka_masked": NCH * 12, "gka_u": NCH * 6, "gka_x": NCH * 4,
              "gka_x_since": NCH * 6, "gka_o_out": NCH * 2, "gka_state_made": NCH * 4, "gka_state": NCH * 4,
              "gka_o_var": NCH, "gka_o_sd": NCH, "gka_o_scaled": NCH, "gka_o_turned": NCH * 2,
              "gka_oT": NCH * 2, "gka_y": NCH, "gka_x_done": NCH})


ROUTE_STEPS = ("logits", "logits_out", "by_token", "shifted", "exped", "weighed", "turned", "rows")
COUNTERS = (
    ["ln_centred", "ln_squared", "ln_variance", "ln_deviation", "ln_normed"]
    + [f"{r}_{x}" for r in ("route", "down_route", "wide_route") for x in ROUTE_STEPS]
    + ["spread", "spread_out", "scaled", "expert_used", "y_ready", "x_done", "router_pre", "router_hidden",
       "hidden_pre", "hidden_done", "gate_ready", "up_ready", "gate_silu", "inter_ready", "down_spread",
       "down_spread_out", "scan_input", "scanned", "win_diff", "win_square", "win_sum", "win_size", "win_unit",
       "win_unit_sq", "win_unit_sum", "win_unit_size", "win_dir", "win_dots", "win_exp", "win_mix", "win_value", "win_out",
       "win_done", "qk_pre", "qk_out", "qk_split", "qk_kept", "operands_loaded", "max_loaded",
            "row_scores", "row_max", "max_split", "max_turned", "max_out", "scores", "exponentials", "summed",
            "sums_out", "sums_spread", "normalised", "v_pre", "v_ready",
            "w_out_ready"]
    + ["gka_" + x for x in (
        "made", "copied", "convolved", "kept_0", "kept_1", "kept_2", "kept_3", "silu", "k_squared", "gates_made", "gates_out", "act_step", "dve_step",
        "loaded", "gates", "g_masked", "decay_made", "decay_out", "turned", "kv", "k_pad", "kd", "scores", "masked",
        "u", "x", "x_since", "o_out", "state_made", "state", "o_var", "o_sd", "o_scaled", "o_turned", "oT", "y", "x_done")]
)


WIN = 8


def ramp(j, w):
    return 0.1 + 0.9 * j / (w - 1) if w > 1 else 0.1


def first_weight(p, m):
    return ramp(m - 1, p) if 1 <= m <= p else 0.0


def pieces(**a):
    t = lambda x, *axes: np.transpose(x, axes)
    f = np.float32
    eye = np.eye(P, dtype=f)

    def selector(width, groups, of):
        s = np.zeros((3 * width, groups, P), f)
        for part in range(3):
            for e in range(width):
                for grp in range(groups):
                    for m in range(P):
                        if of(grp, m) == e:
                            s[part * width + e, grp, m] = 1
        return np.concatenate([s.reshape(3 * width, groups * P), np.zeros((P - 3 * width, groups * P), f)], 0)

    def order(E, keep):
        return np.tile(np.array([[keep(j, e) for j in range(E)] for e in range(E)], f).reshape(1, E * E), (P, 1))

    out = {
        "const": {
            "centre": eye - f(1 / D), "mean": np.full((P, P), 1 / D, f), "ident": eye,
            "ln_eps": np.full((P, 1), LN_EPS, f),
            "before8": order(8, lambda j, e: j < e), "after8": order(8, lambda j, e: j > e),
            "before16": order(16, lambda j, e: j < e), "after16": order(16, lambda j, e: j > e),
        },
        "select": {
            "selector8": selector(8, 8, lambda g, m: g), "selector16": selector(16, 16, lambda g, m: g),
            "chunk_selector": selector(16, 4, lambda g, m: 4 * g + m // 32),
            "mask": np.tile(np.tril(np.full((P, P), -29952, f), -1), (1, 4)),
        },
        "L0": {
            "expert_w": t(a["L0_ffn_expert_w"], 2, 0, 1).reshape(D, -1),
            "router": a["L0_ffn_router_w"].T, "router_b": a["L0_ffn_router_b"][:, None],
            "expert_b": np.concatenate([a["L0_ffn_expert_b"]] * 3 + [np.zeros((P - 24, D), f)], 0),
        },
        "L1": {
            "rw1": a["L1_ffn_rw1"], "rb1": a["L1_ffn_rb1"][:, None], "rw2": a["L1_ffn_rw2"],
            "rb2": a["L1_ffn_rb2"][:, None],
            "be1": t(a["L1_ffn_be1"].reshape(8, 4, P), 2, 0, 1).reshape(P, -1),
            "be2": a["L1_ffn_be2"].T,
            "we1": t(a["L1_ffn_we1"], 1, 0, 2).reshape(D, -1),
            "we2": t(a["L1_ffn_we2"].reshape(8, 4, P, D), 2, 0, 1, 3).reshape(P, -1),
        },
        "L2": {
            "router_gate_up": np.concatenate([a["L2_ffn_router_gate"].T, a["L2_ffn_router_up"].T], 1),
            "router_down": t(a["L2_ffn_router_down"].reshape(8, 4, P), 2, 1, 0).reshape(P, -1),
            "gate": t(a["L2_ffn_w_gate"], 2, 0, 1).reshape(D, -1),
            "up": t(a["L2_ffn_w_up"], 2, 0, 1).reshape(D, -1),
            "down": t(a["L2_ffn_w_down"].reshape(8, D, 4, P), 3, 0, 2, 1).reshape(P, -1),
        },
        "L3": {
            "router": a["L3_ffn_router_w"],
            "gate": np.concatenate([t(a["L3_ffn_wg_r"], 1, 0, 2).reshape(D, -1), t(a["L3_ffn_wg_s"], 1, 0, 2).reshape(D, -1)], 1),
            "up": np.concatenate([t(a["L3_ffn_wu_r"], 1, 0, 2).reshape(D, -1), t(a["L3_ffn_wu_s"], 1, 0, 2).reshape(D, -1)], 1),
            "down": np.concatenate([t(a["L3_ffn_wd_r"].reshape(4, P, D), 1, 0, 2).reshape(P, -1), a["L3_ffn_wd_s"].reshape(P, D)], 1),
        },
        "A3": {
            "w_out": a["L3_attn_w_out"].T, "a": a["L3_attn_a"][:, None], "b": a["L3_attn_b"][:, None],
            "b_out": a["L3_attn_b_out"][:, None],
        },
        "A0": {
            "proj": np.concatenate([a["L0_attn_Wq"][:, tile_features()], a["L0_attn_Wk"], a["L0_attn_Wv"]], 1),
            "conv": t(a["L0_attn_Wconv"][np.concatenate([tile_features(), np.arange(1024, 1536)])].reshape(12, P, 4),
                      1, 0, 2).reshape(P, -1),
            "gates": np.concatenate([a["L0_attn_Wa"], a["L0_attn_Walpha"], a["L0_attn_Wb"]], 1),
            "out": t(a["L0_attn_Wo"][tile_features()].reshape(8, P, D), 1, 0, 2).reshape(P, -1),
            "norm_w": np.tile(a["L0_attn_norm_w"], 2)[:, None],
            "A_log": np.tile(a["L0_attn_A_log"][None], (P, 1)), "dt_bias": np.tile(a["L0_attn_dt_bias"][None], (P, 1)),
            "one": np.ones((P, 1), f), "ones": np.ones((P, 64), f),
            "half": np.repeat(np.eye(2, dtype=f), 64, 0),
            "later": np.tril(np.ones((P, P), f), -1), "upto": np.triu(np.ones((P, P), f)),
        },
        "A1": {
            "qk": a["L1_attn_W_in"][:, 0:256],
            "qk_bias": a["L1_attn_b_in"][0:256].reshape(2, P).T,
            "v": a["L1_attn_W_in"][:, 256:384],
            "v_bias": np.tile(a["L1_attn_b_in"][None, 256:384], (P, 1)),
            "out": np.concatenate([np.concatenate([a["L1_attn_W_out"].reshape(4, 4, 8, D), np.zeros((4, 4, 24, D), f)], 2)
                                   .reshape(4, P, D)[g] for g in range(4)], 1),
            "out_bias": a["L1_attn_b_out"][:, None],
            "spread": np.array([[float(r == m // 32 * 32 + 8) for m in range(P)] for r in range(P)], f),
        },
        "A2": {
            "guide": np.concatenate([a["L2_attn_guidance_trajectories"], np.zeros((P - 64, D), f)], 0),
            "guide_rows": a["L2_attn_guidance_trajectories"], "guideT": a["L2_attn_guidance_trajectories"].T,
            "ones": np.ones((P, P), f),
            "ramp": np.concatenate([eye * f(ramp(WIN - 1 - s, WIN)) for s in range(WIN)], 1),
            "first": np.tile(np.array([[first_weight(p, m) for m in range(WIN)] for p in range(WIN)], f).reshape(1, -1), (P, 1)),
        },
    }
    return out


def tile_features():
    return np.concatenate([np.arange(64) + 64 * (8 * p + 4 * half + r)
                           for p in range(2) for r in range(4) for half in range(2)])


def packed(group):
    where, at = {}, 0
    for name, p in group.items():
        where[name] = (p.shape[0], at, at + p.shape[1])
        at += p.shape[1]
    whole = np.zeros((P, at), np.float32)
    for name, p in group.items():
        rows, a, b = where[name]
        whole[0:rows, a:b] = p
    return whole, where


STAGES = (
    ("L0", ("A0",)), ("A0", ()), ("L0", ("L1", "A1")),
    ("L1", ()), ("A1", ()), ("L1", ("L2", "A2")),
    ("L2", ("L3",)), ("A2", ()), ("L2", ("A3",)),
    ("L3", ()), ("A3", ()), ("L3", ()),
)


def build(nc, dram, where, x_in, x_out, stages=STAGES):
    with ExitStack() as stack:
        k = Kit(nc, stack)
        resident = {g: k.sbuf("w_" + g, list(dram[g].shape)) for g in ("const", "L0")}
        width = {g: dram[g].shape[1] for g in dram}
        first = k.sbuf("w_A0_or_L3_A3", [P, max(width["A0"], width["L3"] + width["A3"])])
        second = k.sbuf("w_gates_or_A1_or_A2", [P, max(NCH * GATES, width["A1"], width["A2"])])
        resident.update(A0=first[:, 0:width["A0"]], L3=first[:, 0:width["L3"]],
                        A3=first[:, width["L3"]:width["L3"] + width["A3"]],
                        A1=second[:, 0:width["A1"]], A2=second[:, 0:width["A2"]])
        big = k.sbuf("big", [P, 24576])
        resident["L2"] = big[:, 0:dram["L2"].shape[1]]
        resident["L1"] = big[:, 12500:12500 + dram["L1"].shape[1]]

        def piece(group, name):
            rows, a, b = where[group][name]
            t = resident[group]
            return t[0:rows, a:b]

        k.big_scaled = big[:, 12500:12500 + 16 * TB].rearrange("p (i t) -> p i t", t=TB)
        k.big_low = big[:, 0:12500]
        k.big_upper = big[:, 12500:24576]
        k.big_high = big[:, 0:24576]
        k.mask_bf = k.sbuf("mask_bf", [P, TB], BF16)
        k.gates = second[:, 0:NCH * GATES].rearrange("p (c z) -> p c z", z=GATES)
        k.big_tail = big[:, 21000:24576]
        k.probs = k.sbuf("probs", [P, 8 * TB])
        k.x = k.sbuf("x", [P, T])
        k.centre, k.mean, k.ident, k.ln_eps = (piece("const", n) for n in ("centre", "mean", "ident", "ln_eps"))
        k.before = {E: piece("const", f"before{E}") for E in (8, 16)}
        k.after = {E: piece("const", f"after{E}") for E in (8, 16)}
        k.ident_bf = k.sbuf("ident_bf", [P, P], BF16)
        sel8 = k.sbuf("selector8_bf", [P, 8 * P], BF16)
        sel16 = k.sbuf("selector16_bf", [P, 16 * P], BF16)
        selc = k.sbuf("chunk_selector_bf", [P, 4 * P], BF16)
        k.selector = {8: sel8[:, :].rearrange("r (e m) -> r e m", m=P), 16: sel16[:, :].rearrange("r (e m) -> r e m", m=P)}
        k.chunk_selector = selc[:, :].rearrange("r (e m) -> r e m", m=P)
        k.rows = k.sbuf("rows", [P, T], BF16)
        k.down_rows = k.sbuf("down_rows", [P, T], BF16)
        k.logT = {n: k.sbuf(n + "_logT", [P, TB]) for n in ("route", "down_route", "wide_route")}
        k.parts = {n: k.sbuf(n + "_parts", [P, TPB, P], BF16) for n in k.logT}
        k.expert_b_parts = k.sbuf("expert_b_parts", [P, 3, D], BF16)
        bias_rest = k.sbuf("bias_rest", [P, D])
        k.loaded = stack.enter_context(nc.semaphore("loaded"))
        k.loads = 4
        cast = stack.enter_context(nc.semaphore("constants_cast"))
        stored = stack.enter_context(nc.semaphore("stored"))
        select = big[:, 12500:12500 + dram["select"].shape[1]]

        with nc.Block() as block:
            @block.sync
            def _(sp):
                for region, array in ((k.x[:, :], x_in), *((resident[g][:, :], dram[g]) for g in ("const", "L0")),
                                      (select, dram["select"])):
                    sp.dma_start(region, array).then_inc(k.loaded, 16)
                for name in k.counters:
                    sp.sem_inc(k.counters[name].sem, LEAD)
                sp.wait_ge(k.loaded, 16 * k.loads)

            @block.gpsimd
            def _(pool):
                for t in (k.rows, k.down_rows, *k.logT.values()):
                    pool.memset(t[:, :], 0.0)
                for t in k.parts.values():
                    pool.memset(t[:, :, :], 0.0)
                pool.drain()

            @block.vector
            def _(dve):
                dve.wait_ge(k.loaded, 16 * k.loads)
                left = piece("L0", "expert_b")
                for part in range(3):
                    dve.tensor_copy(k.expert_b_parts[:, part, :], left)
                    dve.drain()
                    if part < 2:
                        dve.tensor_tensor(bias_rest[:, :], left, k.expert_b_parts[:, part, :], ALU.subtract)
                        dve.drain()
                        left = bias_rest[:, :]
                dve.tensor_copy(k.ident_bf[:, :], k.ident)
                for name, t in (("selector8", sel8), ("selector16", sel16), ("chunk_selector", selc),
                                ("mask", k.mask_bf)):
                    rows, a, b = where["select"][name]
                    dve.tensor_copy(t[:, :], select[0:rows, a:b])
                dve.drain().then_inc(cast, 1)
                dve.wait_ge(cast, 1)

        L0 = {n: piece("L0", n) for n in where["L0"]}
        L0["expert_w"] = L0["expert_w"].rearrange("d (e o) -> d e o", o=D)
        L1 = {n: piece("L1", n) for n in where["L1"]}
        L1["we1"] = L1["we1"].rearrange("d (e c h) -> d e c h", c=4, h=P)
        L1["we2"] = L1["we2"].rearrange("h (e c d) -> h e c d", c=4, d=D)
        L2 = {n: piece("L2", n) for n in where["L2"]}
        L2["gate"] = L2["gate"].rearrange("d (e c h) -> d e c h", c=4, h=P)
        L2["up"] = L2["up"].rearrange("d (e c h) -> d e c h", c=4, h=P)
        L2["down"] = L2["down"].rearrange("h (e c d) -> h e c d", c=4, d=D)
        L2["router_down"] = L2["router_down"].rearrange("h (c e) -> h c e", e=8)
        L3 = {n: piece("L3", n) for n in where["L3"]}
        for n in ("gate", "up", "down"):
            L3[n] = L3[n].rearrange("d (c h) -> d c h", h=P)

        A0 = {n: piece("A0", n) for n in where["A0"]}
        A0["proj"] = A0["proj"].rearrange("d (j c) -> d j c", c=P)
        A0["out"] = A0["out"].rearrange("d (j c) -> d j c", c=D)
        scratch0 = nc.dram_tensor("qkv_chunks", [NCH, P, 12, CH], F32).ap()
        A1 = {n: piece("A1", n) for n in where["A1"]}
        A1["qk"] = A1["qk"].rearrange("d (j c) -> d j c", j=2)
        scratch = nc.dram_tensor("qk_parts", [2, 3, P, T], BF16).ap()
        A3 = {n: piece("A3", n) for n in where["A3"]}
        A2 = {n: piece("A2", n) for n in where["A2"]}
        load = lambda *groups: [(resident[g][:, :], dram[g]) for g in groups]
        run = {
            "L0": lambda loads: top1_ffn(k, L0, loads), "A0": lambda loads: gated_kernel_attention(k, A0, scratch0),
            "L1": lambda loads: top2_silu_ffn(k, L1, loads), "A1": lambda loads: softmax_attention(k, A1, scratch),
            "L2": lambda loads: top2_linear_ffn(k, L2, loads), "A2": lambda loads: window_attention(k, A2),
            "L3": lambda loads: shared_routed_ffn(k, L3, loads), "A3": lambda loads: scan_attention(k, A3),
        }
        for name, groups in stages:
            run[name](load(*groups))

        with nc.Block() as block:
            @block.sync
            def _(sp):
                sp.dma_start(x_out, k.x[:, :]).then_inc(stored, 16)
                sp.wait_ge(stored, 16)



def kernel(**inputs):
    import concourse.bacc as _bacc
    from concourse.bass_utils import run_bass_kernel_spmd as _run

    x = np.ascontiguousarray(inputs["L0_attn_x"][0].T)
    groups = {g: packed(group) for g, group in pieces(**{n: np.asarray(a) for n, a in inputs.items()}).items()}
    arrays = {"in_x": x, **{f"in_{g}": whole for g, (whole, _) in groups.items()}}
    nc = _bacc.Bacc("TRN2", target_bir_lowering=False, num_devices=1)
    args = {n: nc.dram_tensor(n, a.shape, F32, kind="ExternalInput").ap() for n, a in arrays.items()}
    out = nc.dram_tensor("out_0_dram", [P, T], F32, kind="ExternalOutput").ap()
    build(nc, {g: args["in_" + g] for g in groups}, {g: where for g, (_, where) in groups.items()}, args["in_x"], out)
    r = _run(nc, [arrays], core_ids=[0])
    return np.ascontiguousarray(r.results[0]["out_0_dram"].T)[None]
```

```python
import numpy as np
import concourse.bass as bass
from concourse import mybir
from contextlib import ExitStack

F32 = mybir.dt.float32
BF16 = mybir.dt.bfloat16
ACT = mybir.ActivationFunctionType
ALU = mybir.AluOpType
AX = mybir.AxisListType

P = 128
D = 128
T = 2048
TB = 512
NB = T // TB
TPB = TB // P
LN_EPS = 1e-5
LEAD = 4


class Counter:

    def __init__(self, sem):
        self.sem, self.start = sem, LEAD

    def at(self, n):
        return n + (self.start + 1)


class Kit:

    def __init__(self, nc, stack):
        self.nc, self.stack = nc, stack
        self.counters = {n: Counter(stack.enter_context(nc.semaphore(n))) for n in COUNTERS}
        self.stage_tensors = 0
        psum = stack.enter_context(nc.psum_tensor("psum", [P, 8 * TB], F32))
        self.bank = [psum[:, b * TB:(b + 1) * TB] for b in range(8)]
        self.pair = [psum[:, b * TB:(b + 2) * TB] for b in (2, 4)]

    def sbuf(self, name, shape, dtype=F32):
        return self.stack.enter_context(self.nc.sbuf_tensor(name, shape, dtype))

    def counter(self, name):
        return self.counters[name]

    def fresh(self, name):
        self.stage_tensors += 1
        return f"{name}_{self.stage_tensors}"

    def passed(self, counts):
        for name, n in counts.items():
            self.counters[name].start += n


class Carve:

    def __init__(self, region):
        self.region, self.used = region, 0

    def __call__(self, name, shape, dtype=F32):
        n = int(np.prod(shape[1:])) // (1 if dtype == F32 else 2)
        flat = self.region[0:shape[0], self.used:self.used + n]
        self.used += n
        assert self.used <= self.region.shape[1], name
        if dtype != F32:
            flat = flat.bitcast(dtype)
        names = "abcdef"[:len(shape) - 1]
        sizes = dict(zip(names[1:], shape[2:]))
        return flat.rearrange(f"p ({' '.join(names)}) -> p {' '.join(names)}", **sizes) if len(names) > 1 else flat


class Norm:

    def __init__(self, k, st, xn, left=0, block_only=False, variance_bank=1):
        self.k, self.xn, self.left, self.block_only = k, xn, left, block_only
        self.bank1 = k.bank[variance_bank]
        self.square, self.sd = (st(nm, [P, TB]) for nm in ("ln_square", "ln_sd"))
        self.centred = k.counter("ln_centred")
        self.squared = k.counter("ln_squared")
        self.variance = k.counter("ln_variance")
        self.deviation = k.counter("ln_deviation")
        self.normed = k.counter("ln_normed")

    def passed(self):
        self.k.passed({n: NB for n in ("ln_centred", "ln_squared", "ln_variance", "ln_deviation", "ln_normed")})

    def pe_centre(self, pe, n):
        pe.wait_ge(self.normed.sem, self.normed.at(n - 1))
        pe.matmul(self.k.bank[0][:, :], self.k.centre[:, :], self.k.x[:, bass.ts(n, TB)],
                  start=True, stop=True).then_inc(self.centred.sem, 1)

    def act_square(self, act, n):
        act.wait_ge(self.centred.sem, self.centred.at(n))
        act.activation(self.square[:, :], self.k.bank[0][:, :], ACT.Square).then_inc(self.squared.sem, 1)

    def pe_variance(self, pe, n):
        pe.wait_ge(self.squared.sem, self.squared.at(n))
        pe.matmul(self.bank1[:, :], self.k.mean[:, :], self.square[:, :],
                  start=True, stop=True).then_inc(self.variance.sem, 1)

    def act_deviation(self, act, n):
        act.wait_ge(self.variance.sem, self.variance.at(n))
        act.activation(self.sd[:, :], self.bank1[:, :], ACT.Sqrt,
                       bias=self.k.ln_eps[:, :]).then_inc(self.deviation.sem, 1)

    def dve_norm(self, dve, n):
        dve.wait_ge(self.deviation.sem, self.deviation.at(n))
        dve.reciprocal(self.sd[:, :], self.sd[:, :])
        dve.drain()
        here = self.xn[:, :] if self.block_only else self.xn[:, bass.ds(n * TB + self.left, TB)]
        dve.tensor_tensor(here, self.k.bank[0][:, :], self.sd[:, :],
                          ALU.mult).then_inc(self.normed.sem, 1)


    def dve_invert(self, dve, n, quarter):
        if quarter == 0:
            dve.wait_ge(self.deviation.sem, self.deviation.at(n))
        cols = slice(quarter * P, (quarter + 1) * P)
        dve.reciprocal(self.sd[:, cols], self.sd[:, cols])

    def dve_apply(self, dve, n):
        here = self.xn[:, :] if self.block_only else self.xn[:, bass.ds(n * TB + self.left, TB)]
        dve.drain()
        dve.tensor_tensor(here, self.k.bank[0][:, :], self.sd[:, :], ALU.mult).then_inc(self.normed.sem, 1)


class Route:

    def __init__(self, k, st, name, experts, routers, topk, denominator, rows, bias=None):
        self.k, self.E, self.R, self.topk, self.denominator, self.bias = k, experts, routers, topk, denominator, bias
        self.rows = rows
        W = self.W = experts * routers
        G = self.G = TPB * routers
        self.logT = k.logT[name]
        self.tok = st(name + "_tok", [P, TPB, W])
        self.top = st(name + "_top", [P, G])
        self.shift = st(name + "_shift", [P, TPB, W])
        self.expo = st(name + "_expo", [P, TPB, W])
        self.score = st(name + "_score", [P, TPB, W])
        self.best = st(name + "_best", [P, G])
        self.chosen = st(name + "_chosen", [P, TPB, W])
        self.sum = st(name + "_sum", [P, 2, G])
        self.comb = st(name + "_comb", [P, TPB, W])
        self.rest = st(name + "_rest", [P, TPB, W])
        self.parts = k.parts[name]
        self.names = [name + "_" + s for s in ("logits", "logits_out", "by_token", "shifted", "exped", "weighed", "turned", "rows")]
        (self.logits, self.logits_out, self.by_token, self.shifted, self.exped, self.weighed,
         self.turned, self.rows_ready) = (k.counter(s) for s in self.names)

    def passed(self):
        self.k.passed({n: NB for n in self.names})

    def act_logits_out(self, act, n):
        act.wait_ge(self.logits.sem, self.logits.at(n))
        src = self.k.bank[1][0:self.W, :]
        if self.bias is None:
            act.activation(self.logT[0:self.W, :], src, ACT.Copy).then_inc(self.logits_out.sem, 1)
        else:
            act.activation(self.logT[0:self.W, :], src, ACT.Identity, bias=self.bias).then_inc(self.logits_out.sem, 1)

    def pe_by_token(self, pe, n):
        pe.wait_ge(self.logits_out.sem, self.logits_out.at(n))
        for j in range(TPB):
            mm = pe.transpose(self.k.bank[1][:, j * P:(j + 1) * P], self.logT[:, j * P:(j + 1) * P],
                              self.k.ident[:, :])
        mm.then_inc(self.by_token.sem, 1)

    def dve_weights(self, dve, n):
        self.dve_choose(dve, n)
        self.dve_weigh(dve, n)

    def by_group(self, t):
        return t[:, :, :].rearrange("p j (r e) -> p (j r) e", e=self.E)

    def dve_choose(self, dve, n):
        k, E, G, W, g = self.k, self.E, self.G, self.W, self.by_group
        over_e = lambda t: t.unsqueeze(2).to_broadcast([P, G, E])
        tok, shift, score, chosen, rest = map(g, (self.tok, self.shift, self.score, self.chosen, self.rest))
        first_of = k.descending[E].unsqueeze(1).to_broadcast([P, G, E])
        dve.wait_ge(self.by_token.sem, self.by_token.at(n))
        dve.tensor_copy(self.tok[:, :, :], k.bank[1][:, :].rearrange("p (j w) -> p j w", w=P)[:, :, 0:W])
        dve.drain()
        dve.tensor_reduce(self.top[:, :], tok, AX.X, ALU.max)
        dve.drain()
        dve.tensor_tensor(shift, tok, over_e(self.top[:, :]), ALU.subtract).then_inc(self.shifted.sem, 1)
        dve.drain()
        dve.scalar_tensor_tensor(score, shift, 0.0, first_of, ALU.is_equal, ALU.mult)
        dve.drain()
        dve.tensor_reduce(self.best[:, :], score, AX.X, ALU.max)
        dve.drain()
        dve.tensor_tensor(chosen, score, over_e(self.best[:, :]), ALU.is_equal)
        dve.drain()
        if self.topk == 2:
            dve.scalar_tensor_tensor(rest, chosen, -3e38, tok, ALU.mult, ALU.add)
            dve.drain()
            dve.tensor_reduce(self.best[:, :], rest, AX.X, ALU.max)
            dve.drain()
            dve.tensor_tensor(score, rest, over_e(self.best[:, :]), ALU.is_equal)
            dve.drain()
            dve.tensor_tensor(score, score, first_of, ALU.mult)
            dve.drain()
            dve.tensor_reduce(self.best[:, :], score, AX.X, ALU.max)
            dve.drain()
            dve.tensor_tensor(score, score, over_e(self.best[:, :]), ALU.is_equal)
            dve.drain()
            dve.tensor_tensor(chosen, chosen, score, ALU.add)

    def dve_weigh(self, dve, n):
        E, G, W, g = self.E, self.G, self.W, self.by_group
        over_e = lambda t: t.unsqueeze(2).to_broadcast([P, G, E])
        expo, chosen, comb, rest = map(g, (self.expo, self.chosen, self.comb, self.rest))
        dve.drain()
        dve.wait_ge(self.exped.sem, self.exped.at(n))
        if self.denominator != "chosen":
            dve.tensor_reduce(self.sum[:, 1, :], expo, AX.X, ALU.add)
        dve.tensor_tensor(rest, chosen, expo, ALU.mult)
        dve.drain()
        if self.denominator != "all":
            dve.tensor_reduce(self.sum[:, 0, :], rest, AX.X, ALU.add)
            dve.drain()
        total = self.sum[:, 1 if self.denominator == "all" else 0, :]
        if self.denominator == "chosen+1e-9":
            dve.scalar_tensor_tensor(total, self.sum[:, 1, :], 1e-9, total, ALU.mult, ALU.add)
            dve.drain()
        dve.reciprocal(total, total)
        dve.drain()
        dve.tensor_tensor(comb, rest, over_e(total), ALU.mult)
        for part in range(3):
            dve.drain()
            dve_src = self.comb if part == 0 else self.rest
            mine3 = self.parts[:, :, part * W:(part + 1) * W]
            last = dve.tensor_copy(mine3, dve_src[:, :, :])
            if part < 2:
                dve.drain()
                dve.tensor_tensor(self.rest[:, :, :], dve_src[:, :, :], mine3, ALU.subtract)
        last.then_inc(self.weighed.sem, 1)

    def act_exp(self, act, n):
        act.wait_ge(self.shifted.sem, self.shifted.at(n))
        act.activation(self.expo[:, :, :], self.shift[:, :, :], ACT.Exp).then_inc(self.exped.sem, 1)

    def pe_turn_back(self, pe, n):
        pe.wait_ge(self.weighed.sem, self.weighed.at(n))
        turned = self.k.bank[1][:, 0:TB // 2].bitcast(BF16)
        for j in range(TPB):
            mm = pe.transpose(turned[:, j * P:(j + 1) * P], self.parts[:, j, :], self.k.ident_bf[:, :])
        mm.then_inc(self.turned.sem, 1)

    def act_rows(self, act, n):
        act.wait_ge(self.turned.sem, self.turned.at(n))
        act.activation(self.rows[:, bass.ts(n, TB)], self.k.bank[1][:, 0:TB // 2].bitcast(BF16),
                       ACT.Copy).then_inc(self.rows_ready.sem, 1)


def two_ahead(eng, main, steps, route_step, norm_step):
    for step in range(steps):
        norm_step(0, step)
    for step in range(steps):
        route_step(0, step)
        norm_step(1, step)

    def block_of(n, more):
        for step in range(steps):
            main(n, step)
            if more > 0:
                route_step(n + 1, step)
            if more > 1:
                norm_step(n + 2, step)
        main(n, steps)

    with eng.Fori(0, NB - 2) as n:
        block_of(n, 2)
    block_of(NB - 2, 1)
    block_of(NB - 1, 0)


def load_meanwhile(k, block, loads):
    if loads:
        @block.sync
        def _(sp):
            for region, array in loads:
                sp.dma_start(region, array).then_inc(k.loaded, 16)
            k.loads += len(loads)
            sp.wait_ge(k.loaded, 16 * k.loads)


def top1_ffn(k, w, loads=()):
    nc, E = k.nc, 8
    with ExitStack() as s:
        st = lambda name, shape, dt=F32: s.enter_context(nc.sbuf_tensor(k.fresh(name), shape, dt))
        xn = st("xn", [P, T])
        rows = k.rows
        scaled = st("scaled", [P, 2, TB])
        norm = Norm(k, st, xn, variance_bank=5)
        route = Route(k, st, "route", E, 1, 1, "all", rows, bias=w["router_b"])
        spread, scale, used = (k.counter(x) for x in ("spread", "scaled", "expert_used"))
        y_ready, x_done = k.counter("y_ready"), k.counter("x_done")
        bank_y = k.bank[4]
        block = s.enter_context(nc.Block())
        load_meanwhile(k, block, loads)

        @block.tensor
        def _(pe):
            def logits(n):
                pe.wait_ge(norm.normed.sem, norm.normed.at(n))
                pe.matmul(k.bank[1][0:E, :], w["router"], xn[:, bass.ts(n, TB)],
                          start=True, stop=True).then_inc(route.logits.sem, 1)

            def route_step(n, step):
                if step == 0:
                    logits(n)
                elif step == 1:
                    route.pe_by_token(pe, n)
                elif step == 6:
                    route.pe_turn_back(pe, n)

            def norm_step(n, step):
                if step == 0:
                    norm.pe_centre(pe, n)
                elif step == 2:
                    norm.pe_variance(pe, n)

            def put_weights(n, e):
                pe.wait_ge(scale.sem, scale.at(n * E + e - 2))
                if e == 0:
                    pe.wait_ge(route.rows_ready.sem, route.rows_ready.at(n))
                pe.matmul(k.bank[2 + e % 2][:, :], k.selector[E][:, e, :], rows[:, bass.ts(n, TB)],
                          start=True, stop=True).then_inc(spread.sem, 1)

            def expert(n, e):
                if e == E:
                    return
                if e == 0:
                    put_weights(n, 0)
                    pe.wait_ge(x_done.sem, x_done.at(n - 1))
                if e < E - 1:
                    put_weights(n, e + 1)
                pe.wait_ge(scale.sem, scale.at(n * E + e))
                pe.matmul(bank_y[:, :], w["expert_w"][:, e, :], scaled[:, e % 2, :],
                          start=(e == 0), stop=False).then_inc(used.sem, 1)
                if e == E - 1:
                    for part in range(3):
                        mm = pe.matmul(bank_y[:, :], k.expert_b_parts[:, part, :], rows[:, bass.ts(n, TB)],
                                       start=False, stop=(part == 2))
                    mm.then_inc(y_ready.sem, 1)

            two_ahead(pe, expert, E, route_step, norm_step)

        @block.scalar
        def _(act):
            def route_step(n, step):
                if step == 1:
                    route.act_logits_out(act, n)
                elif step == 3:
                    route.act_exp(act, n)
                elif step == 6:
                    route.act_rows(act, n)

            def norm_step(n, step):
                if step == 0:
                    norm.act_square(act, n)
                elif step == 2:
                    norm.act_deviation(act, n)

            two_ahead(act, lambda n, e: None, E, route_step, norm_step)

        @block.vector
        def _(dve):
            def route_step(n, step):
                if step == 2:
                    route.dve_choose(dve, n)
                elif step == 3:
                    route.dve_weigh(dve, n)

            def norm_step(n, step):
                if 3 <= step < 7:
                    norm.dve_invert(dve, n, step - 3)
                elif step == 7:
                    norm.dve_apply(dve, n)

            def expert(n, e):
                if e == E:
                    return add_to_x(n)
                dve.wait_ge(spread.sem, spread.at(n * E + e))
                dve.wait_ge(used.sem, used.at(n * E + e - 2))
                dve.tensor_tensor(scaled[:, e % 2, :], xn[:, bass.ts(n, TB)], k.bank[2 + e % 2][:, :],
                                  ALU.mult).then_inc(scale.sem, 1)

            def add_to_x(n):
                dve.wait_ge(y_ready.sem, y_ready.at(n))
                xb = k.x[:, bass.ts(n, TB)]
                dve.scalar_tensor_tensor(xb, bank_y[:, :], 0.5, xb, ALU.mult, ALU.add).then_inc(x_done.sem, 1)

            two_ahead(dve, expert, E, route_step, norm_step)

    norm.passed()
    route.passed()
    k.passed({"spread": NB * E, "scaled": NB * E, "expert_used": NB * E, "y_ready": NB, "x_done": NB})


def top2_silu_ffn(k, w, loads=()):
    nc, E, C = k.nc, 8, 4
    with ExitStack() as s:
        st = lambda name, shape, dt=F32: s.enter_context(nc.sbuf_tensor(k.fresh(name), shape, dt))
        xn = st("xn", [P, T])
        rows = k.rows
        router_hidden = st("router_hidden", [P, TB])
        hidden = k.probs[:, :].rearrange("p (b c t) -> p b c t", b=2, c=C)
        weight = st("weight", [P, 2, TB])
        weighted = st("weighted", [P, TB])
        norm = Norm(k, st, xn)
        route = Route(k, st, "route", E, 1, 2, "chosen", rows, bias=w["rb2"])
        spread, spread_out = k.counter("spread"), k.counter("spread_out")
        r_pre, r_hid = k.counter("router_pre"), k.counter("router_hidden")
        pre, act_done = k.counter("hidden_pre"), k.counter("hidden_done")
        y_ready, x_done = k.counter("y_ready"), k.counter("x_done")
        block = s.enter_context(nc.Block())
        load_meanwhile(k, block, loads)

        @block.tensor
        def _(pe):
            def prepare(n, step):
                if step == 0:
                    norm.pe_centre(pe, n)
                elif step == 1:
                    norm.pe_variance(pe, n)
                elif step == 2:
                    pe.wait_ge(norm.normed.sem, norm.normed.at(n))
                    pe.matmul(k.bank[1][:, :], w["rw1"], xn[:, bass.ts(n, TB)],
                              start=True, stop=True).then_inc(r_pre.sem, 1)
                elif step == 3:
                    pe.wait_ge(r_hid.sem, r_hid.at(n))
                    pe.matmul(k.bank[1][0:E, :], w["rw2"], router_hidden[:, :],
                              start=True, stop=True).then_inc(route.logits.sem, 1)
                elif step == 4:
                    route.pe_by_token(pe, n)
                elif step == 6:
                    route.pe_turn_back(pe, n)

            def first_layer(n, e):
                for c in range(C):
                    i = n * (E * C) + (e * C + c)
                    pe.wait_ge(act_done.sem, act_done.at(i - 2))
                    pe.matmul(k.bank[4 + c % 2][:, :], w["we1"][:, e, c, :], xn[:, bass.ts(n, TB)],
                              start=True, stop=True).then_inc(pre.sem, 1)

            def second_layer(n, e):
                pe.wait_ge(spread_out.sem, spread_out.at(n * E + e - 1))
                if e == 0:
                    pe.wait_ge(route.rows_ready.sem, route.rows_ready.at(n))
                pe.matmul(k.bank[2][:, :], k.selector[E][:, e, :], rows[:, bass.ts(n, TB)],
                          start=True, stop=True).then_inc(spread.sem, 1)
                pe.wait_ge(x_done.sem, x_done.at(n * E + e - 2))
                for c in range(C):
                    pe.wait_ge(act_done.sem, act_done.at(n * (E * C) + (e * C + c)))
                    mm = pe.matmul(k.bank[6 + e % 2][:, :], w["we2"][:, e, c, :], hidden[:, e % 2, c, :],
                                   start=(c == 0), stop=(c == C - 1))
                mm.then_inc(y_ready.sem, 1)

            def expert(n, e):
                if e == 0:
                    first_layer(n, 0)
                if e < E - 1:
                    first_layer(n, e + 1)
                second_layer(n, e)

            for step in range(8):
                prepare(0, step)
            with pe.Fori(0, NB - 1) as n:
                for e in range(E):
                    expert(n, e)
                    prepare(n + 1, e)
            for e in range(E):
                expert(NB - 1, e)

        @block.scalar
        def _(act):
            def prepare(n, step):
                if step == 0:
                    norm.act_square(act, n)
                elif step == 1:
                    norm.act_deviation(act, n)
                elif step == 2:
                    act.wait_ge(r_pre.sem, r_pre.at(n))
                    act.activation(router_hidden[:, :], k.bank[1][:, :], ACT.Silu,
                                   bias=w["rb1"]).then_inc(r_hid.sem, 1)
                elif step == 3:
                    route.act_logits_out(act, n)
                elif step == 5:
                    route.act_exp(act, n)
                elif step == 6:
                    route.act_rows(act, n)

            def hidden_of(n, e):
                act.wait_ge(y_ready.sem, y_ready.at(n * E + e - 2))
                for c in range(C):
                    act.wait_ge(pre.sem, pre.at(n * (E * C) + (e * C + c)))
                    act.activation(hidden[:, e % 2, c, :], k.bank[4 + c % 2][:, :], ACT.Silu,
                                   bias=w["be1"][:, e * C + c:e * C + c + 1]).then_inc(act_done.sem, 1)

            def expert(n, e):
                if e == 0:
                    hidden_of(n, 0)
                if e < E - 1:
                    hidden_of(n, e + 1)
                act.wait_ge(spread.sem, spread.at(n * E + e))
                act.wait_ge(x_done.sem, x_done.at(n * E + e - 2))
                act.activation(weight[:, e % 2, :], k.bank[2][:, :], ACT.Copy).then_inc(spread_out.sem, 1)

            for step in range(8):
                prepare(0, step)
            with act.Fori(0, NB - 1) as n:
                for e in range(E):
                    expert(n, e)
                    prepare(n + 1, e)
            for e in range(E):
                expert(NB - 1, e)

        @block.vector
        def _(dve):
            def prepare(n, step):
                if step == 1:
                    norm.dve_norm(dve, n)
                elif step == 5:
                    route.dve_weights(dve, n)

            def expert(n, e):
                xb = k.x[:, bass.ts(n, TB)]
                if e == 0:
                    dve.scalar_tensor_tensor(xb, xn[:, bass.ts(n, TB)], 0.5, xb, ALU.mult, ALU.add)
                dve.drain()
                dve.wait_ge(y_ready.sem, y_ready.at(n * E + e))
                dve.wait_ge(spread_out.sem, spread_out.at(n * E + e))
                dve.scalar_tensor_tensor(weighted[:, :], k.bank[6 + e % 2][:, :], w["be2"][:, e:e + 1],
                                         weight[:, e % 2, :], ALU.add, ALU.mult)
                dve.drain()
                dve.scalar_tensor_tensor(xb, weighted[:, :], 0.5, xb, ALU.mult,
                                         ALU.add).then_inc(x_done.sem, 1)

            for step in range(8):
                prepare(0, step)
            with dve.Fori(0, NB - 1) as n:
                for e in range(E):
                    expert(n, e)
                    prepare(n + 1, e)
            for e in range(E):
                expert(NB - 1, e)

    norm.passed()
    route.passed()
    k.passed({"spread": NB * E, "spread_out": NB * E, "router_pre": NB, "router_hidden": NB,
              "hidden_pre": NB * E * C, "hidden_done": NB * E * C, "y_ready": NB * E, "x_done": NB * E})


def top2_linear_ffn(k, w, loads=()):
    nc, E, C = k.nc, 8, 4
    with ExitStack() as s:
        st = lambda name, shape, dt=F32: s.enter_context(nc.sbuf_tensor(k.fresh(name), shape, dt))
        xn = st("xn", [P, T])
        rows = k.rows
        down_rows = k.down_rows
        scaled = k.big_scaled
        gated = st("gated", [P, TB])
        inter = k.probs[:, :].rearrange("p (b c t) -> p b c t", b=2, c=C)
        weight = st("weight", [P, 2, TB])
        weighted = st("weighted", [P, TB])
        norm = Norm(k, st, xn)
        route = Route(k, st, "route", E, 2, 2, "chosen", rows)
        down_route = Route(k, st, "down_route", E, 1, 2, "chosen", down_rows)
        spread, scale = k.counter("spread"), k.counter("scaled")
        gate_ready, up_ready, gate_silu, inter_ready = (
            k.counter(x) for x in ("gate_ready", "up_ready", "gate_silu", "inter_ready"))
        down_spread, down_spread_out = k.counter("down_spread"), k.counter("down_spread_out")
        y_ready, x_done = k.counter("y_ready"), k.counter("x_done")
        block = s.enter_context(nc.Block())
        load_meanwhile(k, block, loads)

        def parity(n):
            return n % 2

        @block.tensor
        def _(pe):
            def prepare(n, step):
                if step == 0:
                    if not isinstance(n, int) or n > 1:
                        pe.wait_ge(down_spread_out.sem, down_spread_out.at(n * E - (2 * E + 1)))
                    norm.pe_centre(pe, n)
                    pe.wait_ge(down_route.rows_ready.sem, down_route.rows_ready.at(n - 2))
                    norm.pe_variance(pe, n)
                elif step == 1:
                    pe.wait_ge(norm.normed.sem, norm.normed.at(n))
                    pe.matmul(k.bank[1][0:2 * E, :], w["router_gate_up"], xn[:, bass.ts(n, TB)],
                              start=True, stop=True).then_inc(route.logits.sem, 1)
                elif step == 2:
                    route.pe_by_token(pe, n)
                elif step == 3:
                    route.pe_turn_back(pe, n)

            def put_weights(n, i):
                pe.wait_ge(scale.sem, scale.at(n * (2 * E) + i - 2))
                if i == 0:
                    pe.wait_ge(route.rows_ready.sem, route.rows_ready.at(n))
                pe.matmul(k.bank[2 + i % 2][:, :], k.selector[2 * E][:, i, :], rows[:, bass.ts(n, TB)],
                          start=True, stop=True).then_inc(spread.sem, 1)

            def gate_up(n, prev, c):
                pe.wait_ge(scale.sem, scale.at(n * (2 * E) + (2 * E - 1)))
                pe.wait_ge(inter_ready.sem, inter_ready.at(n * C + c - 2))
                for e in range(E):
                    mm = pe.matmul(k.bank[4 + c % 2][:, :], w["gate"][:, e, c, :], scaled[:, e, :],
                                   start=(e == 0), stop=(e == E - 1))
                mm.then_inc(gate_ready.sem, 1)
                if c < 2 and prev is not None:
                    pe.wait_ge(x_done.sem, x_done.at(n * E - E - 1))
                for e in range(E):
                    mm = pe.matmul(k.bank[6 + c % 2][:, :], w["up"][:, e, c, :], scaled[:, E + e, :],
                                   start=(e == 0), stop=(e == E - 1))
                mm.then_inc(up_ready.sem, 1)

            def down(n, e, nxt):
                pe.wait_ge(down_spread_out.sem, down_spread_out.at(n * E + e - 1))
                if e == 0:
                    pe.wait_ge(norm.normed.sem, norm.normed.at(nxt if nxt is not None else NB - 1))
                    pe.wait_ge(down_route.rows_ready.sem, down_route.rows_ready.at(n))
                pe.matmul(k.bank[0][:, :], k.selector[E][:, e, :], down_rows[:, bass.ts(n, TB)],
                          start=True, stop=True).then_inc(down_spread.sem, 1)
                pe.wait_ge(x_done.sem, x_done.at(n * E + e - 2))
                for c in range(C):
                    mm = pe.matmul(k.bank[6 + e % 2][:, :], w["down"][:, e, c, :],
                                   inter[:, parity(n), c, :], start=(c == 0), stop=(c == C - 1))
                mm.then_inc(y_ready.sem, 1)

            def down_logits(n):
                pe.wait_ge(inter_ready.sem, inter_ready.at(n * C + (C - 1)))
                for c in range(C):
                    mm = pe.matmul(k.bank[1][0:E, :], w["router_down"][:, c, :], inter[:, parity(n), c, :],
                                   start=(c == 0), stop=(c == C - 1))
                mm.then_inc(down_route.logits.sem, 1)

            def down_prepare(n, step):
                if step == 0:
                    down_logits(n)
                elif step == 2:
                    down_route.pe_by_token(pe, n)
                elif step == 5:
                    down_route.pe_turn_back(pe, n)

            def body(n, prev, nxt):
                for c in range(C):
                    gate_up(n, prev, c)
                    if nxt is not None:
                        prepare(nxt, c)
                if nxt is not None:
                    pe.wait_ge(route.rows_ready.sem, route.rows_ready.at(nxt))
                for e in range(E):
                    if e in (0, 2, 5):
                        down_prepare(n, e)
                    if prev is not None:
                        down(prev, e, nxt)
                    if nxt is not None:
                        put_weights(nxt, 2 * e)
                        put_weights(nxt, 2 * e + 1)

            for step in range(4):
                prepare(0, step)
            for i in range(2 * E):
                put_weights(0, i)
            body(0, None, 1)
            with pe.Fori(1, NB - 1) as n:
                body(n, n - 1, n + 1)
            body(NB - 1, NB - 2, None)
            for e in range(E):
                down(NB - 1, e, None)

        @block.scalar
        def _(act):
            def prepare(n, step):
                if step == 0:
                    norm.act_square(act, n)
                    norm.act_deviation(act, n)
                elif step == 1:
                    route.act_logits_out(act, n)
                elif step == 2:
                    route.act_exp(act, n)
                elif step == 3:
                    route.act_rows(act, n)

            def gate_up(n, c):
                act.wait_ge(gate_ready.sem, gate_ready.at(n * C + c))
                act.wait_ge(inter_ready.sem, inter_ready.at(n * C + c - 1))
                act.activation(gated[:, :], k.bank[4 + c % 2][:, :], ACT.Silu).then_inc(gate_silu.sem, 1)

            def down(n, e):
                act.wait_ge(down_spread.sem, down_spread.at(n * E + e))
                act.wait_ge(x_done.sem, x_done.at(n * E + e - 2))
                act.activation(weight[:, e % 2, :], k.bank[0][:, :], ACT.Copy).then_inc(down_spread_out.sem, 1)

            def body(n, prev, nxt):
                for c in range(C):
                    gate_up(n, c)
                    if nxt is not None:
                        prepare(nxt, c)
                for e in range(E):
                    if e == 0:
                        down_route.act_logits_out(act, n)
                    elif e == 3:
                        down_route.act_exp(act, n)
                    elif e == 5:
                        down_route.act_rows(act, n)
                    if prev is not None:
                        down(prev, e)

            for step in range(4):
                prepare(0, step)
            body(0, None, 1)
            with act.Fori(1, NB - 1) as n:
                body(n, n - 1, n + 1)
            body(NB - 1, NB - 2, None)
            for e in range(E):
                down(NB - 1, e)

        @block.vector
        def _(dve):
            def prepare(n, step):
                if step == 0:
                    norm.dve_norm(dve, n)
                elif step == 2:
                    route.dve_weights(dve, n)

            def scale_inputs(n, these):
                dve.wait_ge(up_ready.sem, up_ready.at(n * C - 1))
                for i in these:
                    dve.wait_ge(spread.sem, spread.at(n * (2 * E) + i))
                    dve.tensor_tensor(scaled[:, i, :], xn[:, bass.ts(n, TB)], k.bank[2 + i % 2][:, :],
                                      ALU.mult).then_inc(scale.sem, 1)

            def gate_up(n, prev, c):
                dve.wait_ge(gate_silu.sem, gate_silu.at(n * C + c))
                dve.wait_ge(up_ready.sem, up_ready.at(n * C + c))
                if prev is not None:
                    dve.wait_ge(y_ready.sem, y_ready.at(n * E - E - 1))
                dve.tensor_tensor(inter[:, parity(n), c, :], gated[:, :], k.bank[6 + c % 2][:, :],
                                  ALU.mult).then_inc(inter_ready.sem, 1)

            def down(n, e):
                xb = k.x[:, bass.ts(n, TB)]
                dve.drain()
                dve.wait_ge(y_ready.sem, y_ready.at(n * E + e))
                dve.wait_ge(down_spread_out.sem, down_spread_out.at(n * E + e))
                dve.tensor_tensor(weighted[:, :], k.bank[6 + e % 2][:, :], weight[:, e % 2, :], ALU.mult)
                dve.drain()
                dve.scalar_tensor_tensor(xb, weighted[:, :], 0.5, xb, ALU.mult, ALU.add).then_inc(x_done.sem, 1)

            def body(n, prev, nxt):
                for c in range(C):
                    gate_up(n, prev, c)
                    if nxt is not None:
                        prepare(nxt, c)
                for e in range(E):
                    if e == 3:
                        down_route.dve_weights(dve, n)
                    if prev is not None:
                        down(prev, e)
                    if nxt is not None:
                        scale_inputs(nxt, (2 * e, 2 * e + 1))

            for step in range(4):
                prepare(0, step)
            scale_inputs(0, range(2 * E))
            body(0, None, 1)
            with dve.Fori(1, NB - 1) as n:
                body(n, n - 1, n + 1)
            body(NB - 1, NB - 2, None)
            for e in range(E):
                down(NB - 1, e)

    norm.passed()
    route.passed()
    down_route.passed()
    k.passed({"spread": NB * 2 * E, "scaled": NB * 2 * E, "gate_ready": NB * C, "up_ready": NB * C,
              "gate_silu": NB * C, "inter_ready": NB * C, "down_spread": NB * E, "down_spread_out": NB * E,
              "y_ready": NB * E, "x_done": NB * E})


def shared_routed_ffn(k, w, loads=()):
    nc, E, C = k.nc, 16, 4
    with ExitStack() as s:
        st = lambda name, shape, dt=F32: s.enter_context(nc.sbuf_tensor(k.fresh(name), shape, dt))
        xn = st("xn", [P, T])
        rows = k.rows
        gated = st("gated", [P, 2, TB])
        product = st("product", [P, TB])
        hidden = st("hidden", [P, 2, TB])
        norm = Norm(k, st, xn, variance_bank=7)
        route = Route(k, st, "wide_route", E, 1, 2, "chosen+1e-9", rows)
        spread = k.counter("spread")
        gate_ready, up_ready, gate_silu, inter_ready = (
            k.counter(x) for x in ("gate_ready", "up_ready", "gate_silu", "inter_ready"))
        used, y_ready, x_done = k.counter("expert_used"), k.counter("y_ready"), k.counter("x_done")
        bank_y = k.bank[3]
        C1 = C + 1
        block = s.enter_context(nc.Block())
        load_meanwhile(k, block, loads)

        @block.tensor
        def _(pe):
            def norm_step(n, step):
                if step == 0:
                    norm.pe_centre(pe, n)
                elif step == 1:
                    norm.pe_variance(pe, n)

            def route_step(n, step):
                if step == 0:
                    pe.wait_ge(norm.normed.sem, norm.normed.at(n))
                    pe.matmul(k.bank[1][0:E, :], w["router"], xn[:, bass.ts(n, TB)],
                              start=True, stop=True).then_inc(route.logits.sem, 1)
                elif step == 1:
                    route.pe_by_token(pe, n)
                elif step == 3:
                    route.pe_turn_back(pe, n)

            def gate_up(n, c):
                i = n * C1 + c
                pe.wait_ge(inter_ready.sem, inter_ready.at(i - (1 if c == 0 else 2)))
                pe.matmul(k.bank[4 + c % 2][:, :], w["gate"][:, c, :], xn[:, bass.ts(n, TB)],
                          start=True, stop=True).then_inc(gate_ready.sem, 1)
                pe.wait_ge(inter_ready.sem, inter_ready.at(i - 1))
                if c == 0:
                    pe.wait_ge(route.rows_ready.sem, route.rows_ready.at(n))
                if c < C:
                    pe.matmul(k.bank[2][:, :], k.chunk_selector[:, c, :], rows[:, bass.ts(n, TB)],
                              start=True, stop=True).then_inc(spread.sem, 1)
                pe.matmul(k.bank[6][:, :], w["up"][:, c, :], xn[:, bass.ts(n, TB)],
                          start=True, stop=True).then_inc(up_ready.sem, 1)

            def down(n, c):
                pe.wait_ge(inter_ready.sem, inter_ready.at(n * C1 + c))
                if c == 0:
                    pe.wait_ge(x_done.sem, x_done.at(n - 1))
                mm = pe.matmul(bank_y[:, :], w["down"][:, c, :], hidden[:, c % 2, :],
                               start=(c == 0), stop=(c == C)).then_inc(used.sem, 1)
                return mm

            def chunk(n, c):
                if c == C1:
                    return
                gate_up(n, c)
                if c > 0:
                    down(n, c - 1)
                if c == C:
                    down(n, C)

            two_ahead(pe, chunk, C1, route_step, norm_step)

        @block.scalar
        def _(act):
            def norm_step(n, step):
                if step == 0:
                    norm.act_square(act, n)
                elif step == 1:
                    norm.act_deviation(act, n)

            def route_step(n, step):
                if step == 0:
                    route.act_logits_out(act, n)
                elif step == 2:
                    route.act_exp(act, n)
                elif step == 4:
                    route.act_rows(act, n)

            def chunk(n, c):
                if c == C1:
                    return
                i = n * C1 + c
                act.wait_ge(gate_ready.sem, gate_ready.at(i))
                act.wait_ge(inter_ready.sem, inter_ready.at(i - (1 if c == 0 else 2)))
                act.activation(gated[:, c % 2, :], k.bank[4 + c % 2][:, :], ACT.Silu).then_inc(gate_silu.sem, 1)

            two_ahead(act, chunk, C1, route_step, norm_step)

        @block.vector
        def _(dve):
            def norm_step(n, step):
                if step in (2, 3):
                    norm.dve_invert(dve, n, 2 * step - 4)
                    norm.dve_invert(dve, n, 2 * step - 3)
                elif step == 4:
                    norm.dve_apply(dve, n)

            def route_step(n, step):
                if step == 1:
                    route.dve_choose(dve, n)
                elif step == 2:
                    route.dve_weigh(dve, n)

            def chunk(n, c):
                if c == C1:
                    return add_to_x(n)
                i = n * C1 + c
                dve.wait_ge(gate_silu.sem, gate_silu.at(i))
                dve.wait_ge(up_ready.sem, up_ready.at(i))
                dve.wait_ge(used.sem, used.at(i - (1 if c == 0 else 2)))
                if c < C:
                    dve.tensor_tensor(product[:, :], gated[:, c % 2, :], k.bank[6][:, :], ALU.mult)
                    dve.drain()
                    dve.wait_ge(spread.sem, spread.at(n * C + c))
                    dve.tensor_tensor(hidden[:, c % 2, :], product[:, :], k.bank[2][:, :],
                                      ALU.mult).then_inc(inter_ready.sem, 1)
                else:
                    dve.tensor_tensor(hidden[:, c % 2, :], gated[:, c % 2, :], k.bank[6][:, :],
                                      ALU.mult).then_inc(inter_ready.sem, 1)

            def add_to_x(n):
                dve.wait_ge(used.sem, used.at(n * C1 + C))
                xb = k.x[:, bass.ts(n, TB)]
                dve.scalar_tensor_tensor(xb, bank_y[:, :], 0.5, xb, ALU.mult, ALU.add).then_inc(x_done.sem, 1)

            two_ahead(dve, chunk, C1, route_step, norm_step)

    norm.passed()
    route.passed()
    k.passed({"spread": NB * C, "gate_ready": NB * C1, "up_ready": NB * C1, "gate_silu": NB * C1,
              "inter_ready": NB * C1, "expert_used": NB * C1, "x_done": NB})


def scan_attention(k, w):
    nc = k.nc
    with ExitStack() as s:
        st = Carve(k.big_upper)
        xn = st("xn", [P, T])
        driven = st("driven", [P, 2, TB])
        y = st("y", [P, T + 1])
        decay = st("decay", [P, 1])
        norm = Norm(k, st, xn)
        tanh_done, scanned = k.counter("scan_input"), k.counter("scanned")
        y_ready, x_done = k.counter("y_ready"), k.counter("x_done")
        block = s.enter_context(nc.Block())

        @block.tensor
        def _(pe):
            def project(n):
                pe.wait_ge(scanned.sem, scanned.at(n))
                pe.wait_ge(x_done.sem, x_done.at(n - 1))
                pe.matmul(k.bank[2][:, :], w["w_out"], y[:, bass.ds(n * TB + 1, TB)],
                          start=True, stop=True).then_inc(y_ready.sem, 1)

            norm.pe_centre(pe, 0)
            norm.pe_variance(pe, 0)
            with pe.Fori(0, NB - 1) as n:
                norm.pe_centre(pe, n + 1)
                norm.pe_variance(pe, n + 1)
                project(n)
            project(NB - 1)

        @block.scalar
        def _(act):
            act.activation(decay[:, :], w["a"], ACT.Tanh).then_inc(tanh_done.sem, 1)
            with act.Fori(0, NB) as n:
                norm.act_square(act, n)
                norm.act_deviation(act, n)

        @block.vector
        def _(dve):
            dve.memset(y[:, 0:1], 0.0)
            dve.wait_ge(tanh_done.sem, tanh_done.at(0))
            norm.dve_norm(dve, 0)

            def scan(n):
                dve.drain()
                dve.tensor_scalar(driven[:, 0, :], xn[:, bass.ts(n, TB)], w["b"], None, ALU.mult)
                dve.drain()
                dve.tensor_tensor_scan(y[:, bass.ds(n * TB + 1, TB)], decay[:, 0:1].to_broadcast([P, TB]),
                                       driven[:, 0, :], y[:, bass.ds(n * TB, 1)],
                                       ALU.mult, ALU.add).then_inc(scanned.sem, 1)

            def add_to_x(n):
                dve.wait_ge(y_ready.sem, y_ready.at(n))
                xb = k.x[:, bass.ts(n, TB)]
                dve.scalar_tensor_tensor(xb, k.bank[2][:, :], w["b_out"], xb, ALU.add,
                                         ALU.add).then_inc(x_done.sem, 1)

            with dve.Fori(0, NB - 1) as n:
                scan(n)
                norm.dve_norm(dve, n + 1)
                add_to_x(n)
            scan(NB - 1)
            add_to_x(NB - 1)

    norm.passed()
    k.passed({"scan_input": 1, "scanned": NB, "y_ready": NB, "x_done": NB})


def window_attention(k, w):
    nc, G = k.nc, 64
    H = WIN
    with ExitStack() as s:
        st = Carve(k.big_upper)
        xn = st("xn", [P, T + 1])
        diff = st("diff", [P, TB])
        square = st("square", [P, TB])
        size = st("size", [P, TB])
        inv = st("inv", [P, TB])
        unit = st("unit", [P, TB])
        unit_size = st("unit_size", [P, TB])
        direction = st("direction", [P, TB])
        expo = st("expo", [P, TB])
        total = st("total", [P, TB])
        value = st("value", [P, H + T])
        weight = st("weight", [P, H + T])
        wsum = st("wsum", [P, TB])
        early = st("early", [P, 2, WIN, WIN])
        early_sum = st("early_sum", [P, 2, WIN])
        gsq = st("gsq", [G, P])
        gscale = st("gscale", [G, 1])
        norm = Norm(k, Carve(k.probs), xn, left=1)
        names = ("win_diff", "win_square", "win_sum", "win_size", "win_unit", "win_weight", "win_dir", "win_dots", "win_exp", "win_mix", "win_value", "win_out", "win_done")
        (s_diff, s_square, s_sum, s_size, s_unit, s_weight, s_dir, s_dots, s_exp,
         s_mix, s_value, s_out, s_done) = (k.counter(x) for x in names)
        block = s.enter_context(nc.Block())

        @block.gpsimd
        def _(pool):
            pool.memset(xn[:, 0:1], 0.0)
            pool.memset(value[:, 0:H], 0.0)
            pool.memset(weight[:, 0:H], 0.0)
            pool.memset(expo[:, :], 0.0)
            pool.drain().then_inc(s_diff.sem, 1)

        @block.tensor
        def _(pe):
            def body(n, nxt):
                pe.wait_ge(s_square.sem, s_square.at(n))
                pe.matmul(k.bank[2][:, :], w["ones"], square[:, :], start=True, stop=True).then_inc(s_sum.sem, 1)
                pe.wait_ge(s_dir.sem, s_dir.at(n))
                pe.matmul(k.bank[4][0:G, :], w["guideT"], direction[:, :], start=True, stop=True).then_inc(s_dots.sem, 1)
                pe.wait_ge(s_exp.sem, s_exp.at(n + 1))
                pe.matmul(k.bank[5][:, :], w["ones"], expo[:, :], start=True, stop=True)
                pe.matmul(k.bank[6][:, :], w["guide"], expo[:, :], start=True, stop=True).then_inc(s_mix.sem, 1)
                if nxt:
                    norm.pe_centre(pe, n + 1)
                    norm.pe_variance(pe, n + 1)
                pe.wait_ge(s_value.sem, s_value.at(n))
                for sh in range(WIN):
                    mm = pe.matmul(k.bank[7][:, :], w["ramp"][:, sh * P:(sh + 1) * P],
                                   value[:, bass.ds(n * TB + (H - sh), TB)],
                                   start=(sh == 0), stop=(sh == WIN - 1))
                mm.then_inc(s_out.sem, 1)

            norm.pe_centre(pe, 0)
            norm.pe_variance(pe, 0)
            with pe.Fori(0, NB - 1) as n:
                body(n, True)
            body(NB - 1, False)

        @block.scalar
        def _(act):
            act.activation(gsq[:, :], w["guide_rows"], ACT.Square, accum_out=gscale[:, :])
            act.drain()
            act.activation(gscale[:, :], gscale[:, :], ACT.Sqrt)
            act.drain().then_inc(s_exp.sem, 1)

            def body(n, nxt):
                act.wait_ge(s_diff.sem, s_diff.at(n + 1))
                act.activation(square[:, :], diff[:, :], ACT.Square).then_inc(s_square.sem, 1)
                act.wait_ge(s_sum.sem, s_sum.at(n))
                act.activation(size[:, :], k.bank[2][:, :], ACT.Sqrt).then_inc(s_size.sem, 1)
                act.drain()
                act.activation(weight[:, bass.ds(n * TB + H, TB)], size[:, :], ACT.Tanh, scale=2.0).then_inc(s_weight.sem, 1)
                act.wait_ge(s_dots.sem, s_dots.at(n))
                act.activation(expo[0:G, :], k.bank[4][0:G, :], ACT.Exp, scale=gscale[:, :]).then_inc(s_exp.sem, 1)
                if nxt:
                    norm.act_square(act, n + 1)
                    norm.act_deviation(act, n + 1)

            norm.act_square(act, 0)
            norm.act_deviation(act, 0)
            with act.Fori(0, NB - 1) as n:
                body(n, True)
            body(NB - 1, False)

        @block.vector
        def _(dve):
            dve.wait_ge(s_exp.sem, s_exp.at(0))
            dve.wait_ge(s_diff.sem, s_diff.at(0))
            dve.tensor_scalar(gscale[:, :], gscale[:, :], 1e-8, None, ALU.max)
            dve.drain()
            dve.reciprocal(gscale[:, :], gscale[:, :])
            dve.drain()
            dve.tensor_scalar(gscale[:, :], gscale[:, :], 2.0, None, ALU.mult)
            dve.drain()

            def body(n, first, nxt):
                here = bass.ds(n * TB + H, TB)
                dve.drain()
                dve.tensor_tensor(diff[:, :], xn[:, bass.ds(n * TB + 1, TB)], xn[:, bass.ds(n * TB, TB)],
                                  ALU.subtract).then_inc(s_diff.sem, 1)
                dve.wait_ge(s_size.sem, s_size.at(n))
                dve.tensor_scalar(inv[:, :], size[:, :], 1e-6, None, ALU.max)
                dve.drain()
                dve.reciprocal(inv[:, :], inv[:, :])
                dve.drain()
                dve.scalar_tensor_tensor(inv[:, :], size[:, :], 1e-6, inv[:, :], ALU.is_gt, ALU.mult)
                dve.drain()
                dve.tensor_tensor(unit[:, :], diff[:, :], inv[:, :], ALU.mult)
                dve.tensor_tensor(unit_size[:, :], size[:, :], inv[:, :], ALU.mult)
                dve.drain()
                dve.tensor_scalar(unit_size[:, :], unit_size[:, :], 1e-8, None, ALU.max)
                dve.drain()
                dve.reciprocal(unit_size[:, :], unit_size[:, :])
                dve.drain()
                dve.tensor_tensor(direction[:, :], unit[:, :], unit_size[:, :], ALU.mult).then_inc(s_dir.sem, 1)
                dve.wait_ge(s_weight.sem, s_weight.at(n))
                dve.tensor_scalar(wsum[:, :], weight[:, here], float(ramp(WIN - 1, WIN)), None, ALU.mult)
                for sh in range(1, WIN):
                    dve.drain()
                    dve.scalar_tensor_tensor(wsum[:, :], weight[:, bass.ds(n * TB + (H - sh), TB)],
                                             float(ramp(WIN - 1 - sh, WIN)), wsum[:, :], ALU.mult, ALU.add)
                dve.tensor_scalar(unit[:, :], unit[:, :], 0.6, None, ALU.mult)
                dve.drain()
                dve.wait_ge(s_mix.sem, s_mix.at(n))
                dve.reciprocal(total[:, :], k.bank[5][:, :])
                dve.drain()
                dve.tensor_tensor(total[:, :], k.bank[6][:, :], total[:, :], ALU.mult)
                dve.drain()
                dve.scalar_tensor_tensor(total[:, :], total[:, :], 0.4, unit[:, :], ALU.mult, ALU.add)
                dve.drain()
                dve.tensor_tensor(value[:, here], total[:, :], weight[:, here], ALU.mult).then_inc(s_value.sem, 1)
                dve.tensor_scalar(wsum[:, :], wsum[:, :], 1e-8, None, ALU.max)
                dve.drain()
                dve.reciprocal(wsum[:, :], wsum[:, :])
                if nxt:
                    norm.dve_norm(dve, n + 1)
                dve.drain()
                dve.wait_ge(s_out.sem, s_out.at(n))
                dve.tensor_tensor(diff[:, :], k.bank[7][:, :], wsum[:, :], ALU.mult)
                dve.drain()
                if first:
                    table = w["first"].rearrange("p (a b) -> p a b", b=WIN)
                    for j, t in enumerate((value, weight)):
                        dve.tensor_tensor(early[:, j, :, :], t[:, H:H + WIN].unsqueeze(1).to_broadcast([P, WIN, WIN]),
                                          table, ALU.mult)
                    dve.drain()
                    dve.tensor_reduce(early_sum[:, :, :].rearrange("p j a -> p (j a)"),
                                      early[:, :, :, :].rearrange("p j a b -> p (j a) b"), AX.X, ALU.add)
                    dve.drain()
                    dve.tensor_scalar(early_sum[:, 1, :], early_sum[:, 1, :], 1e-8, None, ALU.max)
                    dve.drain()
                    dve.reciprocal(early_sum[:, 1, :], early_sum[:, 1, :])
                    dve.drain()
                    dve.tensor_tensor(diff[:, 0:WIN], early_sum[:, 0, :], early_sum[:, 1, :], ALU.mult)
                    dve.drain()
                xb = k.x[:, bass.ts(n, TB)]
                dve.tensor_tensor(xb, xb, diff[:, :], ALU.add).then_inc(s_done.sem, 1)

            norm.dve_norm(dve, 0)
            body(0, True, True)
            with dve.Fori(1, NB - 1) as n:
                body(n, False, True)
            body(NB - 1, False, False)

    norm.passed()
    k.passed({x: NB + (x in ("win_diff", "win_exp")) for x in names})


def softmax_attention(k, w, scratch):
    nc = k.nc
    HEADS, HD, GH = 16, 8, 4
    GROUPS, KT, QB = HEADS // GH, T // P, NB
    STEPS = GROUPS * QB
    SCALE = HD ** -0.5
    STORES = 6
    SHARE = GH * TB // P
    M_ROW = 96

    q_parts, k_parts = scratch
    with ExitStack() as s:
        st = lambda name, shape, dt=F32: s.enter_context(nc.sbuf_tensor(k.fresh(name), shape, dt))
        xn = k.big_tail[:, 0:T]
        q_ops = k.big_low[:, 0:8192].bitcast(BF16).rearrange("p (b q h t) -> p b q h t", b=2, q=QB, h=GH)
        v_group = k.big_low[:, 8192:8192 + KT * GH * 32].rearrange("p (t h m) -> p t h m", h=GH, m=32)
        k_ops = st("k_ops", [P, 2, GH, T], BF16)

        with ExitStack() as s1:
            st1 = Carve(k.probs[:, :])
            norm = Norm(k, st1, xn)
            parts = st1("qk_parts", [P, 2, 3, TB], BF16)
            whole = k.big_low[:, 8192:8192 + 4 * TB].rearrange("p (a t) -> p a t", a=4)
            pre, out, split, kept = (k.counter(x) for x in ("qk_pre", "qk_out", "qk_split", "qk_kept"))
            def each_block(eng, body):
                with eng.Fori(0, NB - 1) as n:
                    body(n, True)
                body(NB - 1, False)

            with nc.Block() as block:
                @block.gpsimd
                def _(pool):
                    pool.memset(q_ops[64:128, :, :, :, :], 0.0)
                    pool.memset(k_ops[64:128, :, :, :], 0.0)
                    pool.drain()
                    pool.memset(k_ops[M_ROW:M_ROW + 3, :, :, :], 1.0)

                @block.tensor
                def _(pe):
                    def body(n, nxt):
                        pe.wait_ge(norm.normed.sem, norm.normed.at(n))
                        if nxt:
                            norm.pe_centre(pe, n + 1)
                        for j in range(2):
                            if j == 1 and nxt:
                                norm.pe_variance(pe, n + 1)
                            pe.wait_ge(out.sem, out.at(n * 2 + j - 2))
                            pe.matmul(k.bank[2 + j][:, :], w["qk"][:, j, :], xn[:, bass.ts(n, TB)],
                                      start=True, stop=True).then_inc(pre.sem, 1)

                    norm.pe_centre(pe, 0)
                    norm.pe_variance(pe, 0)
                    each_block(pe, body)

                @block.scalar
                def _(act):
                    def body(n, nxt):
                        if nxt:
                            norm.act_square(act, n + 1)
                        for j in range(2):
                            if j == 1 and nxt:
                                norm.act_deviation(act, n + 1)
                            act.wait_ge(pre.sem, pre.at(n * 2 + j))
                            act.wait_ge(split.sem, split.at(n * 2 + j - 2))
                            act.activation(whole[:, j, :], k.bank[2 + j][:, :], ACT.Identity,
                                           bias=w["qk_bias"][:, j:j + 1]).then_inc(out.sem, 1)

                    norm.act_square(act, 0)
                    norm.act_deviation(act, 0)
                    each_block(act, body)

                @block.vector
                def _(dve):
                    def body(n, nxt):
                        if nxt:
                            norm.dve_norm(dve, n + 1)
                        for j in range(2):
                            dve.wait_ge(out.sem, out.at(n * 2 + j))
                            dve.wait_ge(kept.sem, n * (16 * STORES) + kept.start)
                            left = whole[:, j, :]
                            for part in range(3):
                                last = dve.tensor_copy(parts[:, j, part, :], left)
                                dve.drain()
                                if part < 2:
                                    dve.tensor_tensor(whole[:, 2 + j, :], left, parts[:, j, part, :], ALU.subtract)
                                    dve.drain()
                                    left = whole[:, 2 + j, :]
                            dve.drain().then_inc(split.sem, 1)

                    norm.dve_norm(dve, 0)
                    each_block(dve, body)

                @block.sync
                def _(sp):
                    with sp.Fori(0, NB) as n:
                        for j in range(2):
                            sp.wait_ge(split.sem, split.at(n * 2 + j))
                            for part in range(3):
                                if j == 0:
                                    dst = q_parts[part, :, bass.ds(n, 1), :, :].rearrange("d q h t -> (q h) d t")
                                else:
                                    dst = k_parts[part, :, :, bass.ts(n, TB)].rearrange("d h t -> h d t")
                                sp.dma_start(dst, parts[:, j, part, :]).then_inc(kept.sem, 16)
                    sp.wait_ge(kept.sem, kept.start + NB * STORES * 16)

            norm.passed()
            k.passed({"qk_pre": 2 * NB, "qk_out": 2 * NB, "qk_split": 2 * NB})

        st = Carve(k.big_low[:, 8192 + KT * GH * 32:12500])
        highest = st("highest", [P, GH * TPB, 4])
        neg_max = st("neg_max", [P, GH * TPB])
        max_rest = st("max_rest", [P, GH * TPB])
        max_parts = st("max_parts", [P, P], BF16)
        max_rows = st("max_rows", [3 * GH * TPB, P], BF16)
        probs = k.probs[:, :].rearrange("p (b h t) -> p b h t", b=2, h=GH)
        sums = st("sums", [P, 2, TB])
        inverse = st("inverse", [P, SHARE])
        w_out = st("w_out", [P, D])
        loaded, max_loaded = k.counter("operands_loaded"), k.counter("max_loaded")
        sums_dealt, inverted, inverse_back = (k.counter(x) for x in ("sums_dealt", "sums_inverted", "inverse_back"))
        (row_scores, row_max, max_split, max_turned, max_out, scores, expd, summed, sums_out,
         spread, normalised, y_ready, x_done, v_pre, v_ready, w_ready) = (k.counter(x) for x in (
            "row_scores", "row_max", "max_split", "max_turned", "max_out", "scores", "exponentials", "summed",
            "sums_out", "sums_spread", "normalised", "y_ready", "x_done", "v_pre", "v_ready",
            "w_out_ready"))
        block = s.enter_context(nc.Block())

        def row_scores_of(kt):
            return range(5 * kt + 2, min(5 * kt + 7, 64))

        IN_THREE = 54
        row_bank = [(0, 1, 7)[m % 3] if m < IN_THREE else m % 2 for m in range(64)]

        ROWS_IN = 16
        LOADS = 12

        q_blocks = q_ops.rearrange("p b q h t -> p (b q) h t")

        @block.sync
        def _(sp):
            def load_group(g, after):
                if after is not None:
                    sp.wait_ge(scores.sem, scores.at(after))
                if g > 0:
                    sp.wait_ge(loaded.sem, g * 16 * LOADS + loaded.start)
                heads = slice(g * GH, (g + 1) * GH)
                for qp in range(3):
                    r = qp * 3 * HD
                    for kp in range(3):
                        sp.dma_start(q_ops[r + kp * HD:r + (kp + 1) * HD, g % 2, :, :, :].rearrange("d q h t -> d q (h t)"),
                                     q_parts[qp, :, :, heads, :].rearrange("d q h t -> d q (h t)")).then_inc(loaded.sem, 16)
                    sp.dma_start(k_ops[r:r + 3 * HD, g % 2, :, :].rearrange("d h t -> d (h t)"),
                                 k_parts[:, :, heads, :].rearrange("k d h t -> (k d) (h t)")).then_inc(loaded.sem, 16)

            def put_max(i):
                sp.wait_ge(max_out.sem, max_out.at(i))
                if i > 0:
                    sp.wait_ge(max_loaded.sem, i * ROWS_IN + max_loaded.start)
                sp.dma_start(q_ops[M_ROW:M_ROW + 3, i // QB % 2, i % QB, :, :].rearrange("p h t -> p (h t)"),
                             max_rows[:, :]).then_inc(max_loaded.sem, 16)

            def invert_sums(i):
                sp.wait_ge(sums_out.sem, sums_out.at(i))
                if i > 0:
                    sp.wait_ge(inverse_back.sem, i * ROWS_IN + inverse_back.start)
                sp.dma_start(inverse[:, :], sums[HD:P:32, i % 2, :]).then_inc(sums_dealt.sem, 16)
                sp.wait_ge(inverted.sem, inverted.at(i))
                sp.dma_start(sums[HD:P:32, i % 2, :], inverse[:, :]).then_inc(inverse_back.sem, 16)

            load_group(0, None)
            put_max(0)
            load_group(1, None)
            for g in range(2, GROUPS):
                for i in range((g - 2) * QB + 1, (g - 1) * QB + 1):
                    if i > 1:
                        invert_sums(i - 2)
                    put_max(i)
                load_group(g, (g - 1) * QB * KT * 2 - 1)
            for i in range((GROUPS - 2) * QB + 1, STEPS):
                invert_sums(i - 2)
                put_max(i)
            invert_sums(STEPS - 2)
            invert_sums(STEPS - 1)

        @block.gpsimd
        def _(pool):
            with pool.Fori(0, GROUPS) as g:
                pool.wait_ge(y_ready.sem, y_ready.at(g * QB - 1))
                pool.tensor_copy(w_out[:, :], w["out"][:, bass.ts(g, D)]).then_inc(w_ready.sem, 1)

        @block.tensor
        def _(pe):
            def row_score(i, g, m):
                h, qt, kb = m // 16, m // 4 % 4, m % 4
                before = [m0 for m0 in range(m) if row_bank[m0] == row_bank[m]]
                if m == 0:
                    pe.wait_ge(max_out.sem, max_out.at(i - 1))
                elif m == 2:
                    pe.wait_ge(v_ready.sem, v_ready.at(g))
                    if not (isinstance(i, int) and i < 3):
                        pe.wait_ge(x_done.sem, x_done.at(i - 3))
                elif before:
                    pe.wait_ge(row_max.sem, row_max.at(i * 64 + before[-1]))
                pe.matmul(k.bank[row_bank[m]][:, :], q_blocks[:, i % (2 * QB), h, qt * P:(qt + 1) * P],
                          k_ops[:, i // QB % 2, h, kb * TB:(kb + 1) * TB],
                          start=True, stop=True).then_inc(row_scores.sem, 1)

            def turn_max(i):
                pe.wait_ge(max_split.sem, max_split.at(i))
                pe.transpose(k.bank[0][:, 0:P // 2].bitcast(BF16), max_parts[:, :],
                             k.ident_bf[:, :]).then_inc(max_turned.sem, 1)

            def score_pair(i, g, kt, hp):
                b = i * (KT * 2) + (kt * 2 + hp)
                pe.wait_ge(expd.sem, expd.at(b - 2))
                for j in range(2):
                    mm = pe.matmul(k.bank[2 + 2 * hp + j][:, :], k_ops[:, g % 2, 2 * hp + j, kt * P:(kt + 1) * P],
                                   q_blocks[:, i % (2 * QB), 2 * hp + j, :], start=True, stop=True)
                mm.then_inc(scores.sem, 1)

            def sum_values(i, kt):
                pe.wait_ge(expd.sem, expd.at(i * (KT * 2) + (kt * 2 + 1)))
                if kt == 0:
                    pe.wait_ge(sums_out.sem, sums_out.at(i - 1))
                for h in range(GH):
                    mm = pe.matmul(k.bank[6][32 * h:32 * h + 32, :], v_group[:, kt, h, :],
                                   probs[:, kt % 2, h, :], start=(kt == 0), stop=(kt == KT - 1))
                mm.then_inc(summed.sem, 1)

            def spread_sums(i, ahead):
                if ahead:
                    pe.wait_ge(row_max.sem, row_max.at((i + 2) * 64 + (IN_THREE - 1)))
                pe.wait_ge(inverse_back.sem, i * ROWS_IN + (ROWS_IN + inverse_back.start))
                pe.wait_ge(x_done.sem, x_done.at(i - 1))
                pe.matmul(k.bank[7][:, :], w["spread"], sums[:, i % 2, :], start=True, stop=True).then_inc(spread.sem, 1)

            def project(i, g):
                pe.wait_ge(normalised.sem, normalised.at(i))
                pe.wait_ge(w_ready.sem, w_ready.at(g))
                pe.matmul(k.bank[7][:, :], w_out[:, :], sums[:, i % 2, :], start=True, stop=True).then_inc(y_ready.sem, 1)

            def values(g):
                pe.wait_ge(x_done.sem, x_done.at(g * QB - 2))
                for kt in range(KT):
                    mm = pe.matmul(k.bank[7][:, kt * 32:(kt + 1) * 32], xn[:, kt * P:(kt + 1) * P],
                                   w["v"][:, bass.ds(g * 32, 32)], start=True, stop=True)
                mm.then_inc(v_pre.sem, 1)

            def wait_operands(g):
                pe.wait_ge(loaded.sem, g * (16 * LOADS) + (16 * LOADS + loaded.start))

            def step(i, g, ahead, tail):
                if ahead:
                    wait_operands((i + 1) // QB)
                    for m in range(2):
                        row_score(i + 1, g, m)
                pe.wait_ge(max_loaded.sem, i * ROWS_IN + (ROWS_IN + max_loaded.start))
                for hp in range(2):
                    score_pair(i, g, 0, hp)
                for kt in range(KT):
                    rows = row_scores_of(kt) if ahead else []
                    if kt == KT - 1 and tail:
                        project(i - 1, (i - 1) // QB)
                    for j in range(6):
                        if j in (1, 2) and kt + 1 < KT:
                            score_pair(i, g, kt + 1, j - 1)
                        if j == 4:
                            if kt == 0:
                                pe.wait_ge(v_ready.sem, v_ready.at(g))
                            sum_values(i, kt)
                        if j < len(rows):
                            row_score(i + 1, g, rows[j])
                    if kt == 11 and tail:
                        spread_sums(i - 1, ahead)
                    if kt == 13 and ahead:
                        turn_max(i + 1)

            wait_operands(0)
            values(0)
            for m in range(64):
                row_score(0, 0, m)
            turn_max(0)
            step(0, 0, True, False)
            with pe.Fori(1, QB) as i:
                step(i, 0, True, True)
            with pe.Fori(1, GROUPS - 1) as g:
                values(g)
                with pe.Fori(0, QB) as qb:
                    step(g * QB + qb, g, True, True)
            g = GROUPS - 1
            values(g)
            with pe.Fori(g * QB, STEPS - 1) as i:
                step(i, g, True, True)
            step(STEPS - 1, g, False, True)
            spread_sums(STEPS - 1, False)
            project(STEPS - 1, GROUPS - 1)

        @block.scalar
        def _(act):
            def max_rows_out(i):
                act.wait_ge(max_turned.sem, max_turned.at(i))
                act.wait_ge(max_loaded.sem, i * ROWS_IN + max_loaded.start)
                act.activation(max_rows[:, :], k.bank[0][0:3 * GH * TPB, 0:P // 2].bitcast(BF16),
                               ACT.Copy).then_inc(max_out.sem, 1)

            def exponentials(i, kt, hp):
                b = i * (KT * 2) + (kt * 2 + hp)
                act.wait_ge(scores.sem, scores.at(b))
                act.wait_ge(summed.sem, summed.at(i * KT + kt - 2))
                both = k.pair[hp]
                act.activation(probs[:, kt % 2, 2 * hp:2 * hp + 2, :].rearrange("p h q -> p (h q)"), both,
                               ACT.Exp, scale=SCALE).then_inc(expd.sem, 1)

            def key_tiles(i, kts, ahead):
                for kt in kts:
                    for hp in range(2):
                        exponentials(i, kt, hp)
                    if kt == 14 and ahead:
                        max_rows_out(i + 1)

            def copy_sums(i):
                act.wait_ge(summed.sem, summed.at(i * KT + (KT - 1)))
                act.wait_ge(y_ready.sem, y_ready.at(i - 2))
                act.activation(sums[:, i % 2, :], k.bank[6][:, :], ACT.Copy).then_inc(sums_out.sem, 1)

            max_rows_out(0)
            key_tiles(0, (0, 1), False)
            with act.Fori(0, STEPS - 1) as i:
                key_tiles(i, range(2, KT), True)
                copy_sums(i)
                key_tiles(i + 1, (0, 1), False)
            key_tiles(STEPS - 1, range(2, KT), False)
            copy_sums(STEPS - 1)

        @block.vector
        def _(dve):
            def row_highest(i, m):
                dve.wait_ge(row_scores.sem, row_scores.at(i * 64 + m))
                dve.tensor_reduce(highest[:, m // 4, m % 4:m % 4 + 1], k.bank[row_bank[m]][:, :], AX.X,
                                  ALU.max).then_inc(row_max.sem, 1)

            def split_max(i):
                dve.drain()
                dve.tensor_reduce(neg_max[:, :], highest[:, :, :], AX.X, ALU.max, negate=True)
                dve.drain()
                n = GH * TPB
                dve.wait_ge(max_turned.sem, max_turned.at(i - 1))
                left = neg_max[:, :]
                for part in range(3):
                    dve.tensor_copy(max_parts[:, part * n:(part + 1) * n], left)
                    dve.drain()
                    if part < 2:
                        dve.tensor_tensor(max_rest[:, :], left, max_parts[:, part * n:(part + 1) * n], ALU.subtract)
                        dve.drain()
                        left = max_rest[:, :]
                dve.drain().then_inc(max_split.sem, 1)

            def values(g):
                dve.wait_ge(v_pre.sem, v_pre.at(g))
                dve.wait_ge(summed.sem, summed.at(g * (QB * KT) - 1))
                dve.tensor_tensor(v_group[:, :, :, 0:HD],
                                  k.bank[7][:, :].rearrange("p (t h d) -> p t h d", h=GH, d=HD),
                                  w["v_bias"][:, bass.ds(g * 32, 32)].rearrange("p (h d) -> p h d", d=HD)
                                  .unsqueeze(1).to_broadcast([P, KT, GH, HD]), ALU.add).then_inc(v_ready.sem, 1)

            def invert(i):
                dve.wait_ge(sums_dealt.sem, i * ROWS_IN + (ROWS_IN + sums_dealt.start))
                dve.reciprocal(inverse[:, :], inverse[:, :]).then_inc(inverted.sem, 1)

            def normalise(i):
                dve.wait_ge(spread.sem, spread.at(i))
                dve.tensor_tensor(sums[:, i % 2, :], sums[:, i % 2, :], k.bank[7][:, :],
                                  ALU.mult).then_inc(normalised.sem, 1)

            def add_to_x(i):
                dve.wait_ge(y_ready.sem, y_ready.at(i))
                xb = k.x[:, bass.ts(i % QB, TB)]
                dve.tensor_tensor(xb, k.bank[7][:, :], xb, ALU.add).then_inc(x_done.sem, 1)

            def step(i, ahead, tail):
                for kt in range(KT):
                    if ahead:
                        for m in (*(range(2) if kt == 0 else ()), *row_scores_of(kt)):
                            row_highest(i + 1, m)
                    if kt == 13 and ahead:
                        split_max(i + 1)
                    if kt == 5 and tail:
                        invert(i - 1)
                    if kt == 13 and tail:
                        normalise(i - 1)
                if tail:
                    add_to_x(i - 1)

            dve.memset(v_group[:, :, :, :], 0.0)
            dve.memset(max_parts[:, :], 0.0)
            dve.drain()
            dve.memset(v_group[:, :, :, HD:HD + 1], 1.0)
            dve.drain()
            values(0)
            for m in range(64):
                row_highest(0, m)
            split_max(0)
            step(0, True, False)
            with dve.Fori(1, QB) as i:
                step(i, True, True)
            with dve.Fori(1, GROUPS - 1) as g:
                values(g)
                with dve.Fori(0, QB) as qb:
                    step(g * QB + qb, True, True)
            g = GROUPS - 1
            values(g)
            with dve.Fori(g * QB, STEPS - 1) as i:
                step(i, True, True)
            step(STEPS - 1, False, True)
            invert(STEPS - 1)
            normalise(STEPS - 1)
            add_to_x(STEPS - 1)
            dve.drain()
            dve.tensor_scalar(k.x[:, :], k.x[:, :], w["out_bias"], None, ALU.add)

    k.counters["qk_kept"].start += NB * STORES * 16
    k.counters["operands_loaded"].start += GROUPS * 16 * LOADS
    for name in ("max_loaded", "sums_dealt", "inverse_back"):
        k.counters[name].start += STEPS * ROWS_IN
    k.passed({"row_scores": STEPS * 64, "row_max": STEPS * 64, "max_split": STEPS, "max_turned": STEPS,
              "max_out": STEPS, "scores": STEPS * KT * 2, "exponentials": STEPS * KT * 2, "summed": STEPS * KT,
              "sums_out": STEPS, "sums_inverted": STEPS, "sums_spread": STEPS, "normalised": STEPS,
              "y_ready": STEPS, "x_done": STEPS, "v_pre": GROUPS, "v_ready": GROUPS, "w_out_ready": GROUPS})


CH = 128
NCH = T // CH


def gated_kernel_attention(k, w, scratch):
    project_and_convolve(k, w, scratch)
    run_chunks(k, w, scratch)


def gate_columns(table):
    return {"g": table[..., 0:16], "alpha": table[..., 16:32], "beta": table[..., 32:36],
            "inv_k": table[..., 36:40], "alpha_sq": table[..., 40:56]}


GATES = 56


def project_and_convolve(k, w, scratch):
    nc = k.nc
    TILES, KTILE = 12, 8
    st = Carve(k.big_high)
    xn = st("xn", [P, 3 + TB])
    norm = Norm(k, st, xn[:, 3:], block_only=True)
    pre = st("pre", [P, 2, 3 + TB])
    acc = st("acc", [P, 2, TB])
    tap_w = st("tap_w", [P, 4, 4, P])
    taps = k.conv_rows
    out = st("out", [P, 4, TB])
    halo = st("halo", [P, TILES, 4])
    nought = st("nought", [P, 4])
    k_sq = st("k_sq", [P, 2, TB])
    z = st("z", [P, NCH, 36])
    k_sum = st("k_sum", [P, NCH, 4])
    tmp = st("tmp", [P, NCH, 16])
    decay_rate = st("decay_rate", [P, 16])
    banks = [k.bank[b] for b in (2, 3)]
    table = k.gates
    made, copied, haloed, convolved, taps_ready = (
        k.counter(n) for n in ("gka_made", "gka_copied", "gka_haloed", "gka_convolved", "gka_taps_ready"))
    kept = [k.counter(f"gka_kept_{b}") for b in range(4)]
    silu, squared, z_made, z_out, sums_made, sums_out = (k.counter(n) for n in (
        "gka_silu", "gka_k_squared", "gka_z_made", "gka_z_out", "gka_sums_made", "gka_sums_out"))
    act_step, dve_step = k.counter("gka_act_step"), k.counter("gka_dve_step")

    def item(n, j):
        return n * 8 + (j // 3 * 2 + j % 3)

    def each_block(eng, block_of):
        block_of(0, True, False)
        with eng.Fori(1, NB - 1) as n:
            block_of(n, True, True)
        block_of(NB - 1, False, True)

    with nc.Block() as block:
        @block.tensor
        def _(pe):
            def key_sums(n):
                pe.wait_ge(squared.sem, squared.at(n * 2 + 1))
                pe.wait_ge(sums_out.sem, sums_out.at(n - 1))
                for j in range(TPB):
                    for p in range(2):
                        mm = pe.matmul(k.bank[5][:, j * 4 + 2 * p:j * 4 + 2 * p + 2], k_sq[:, p, j * P:(j + 1) * P],
                                       w["half"], start=True, stop=True)
                mm.then_inc(sums_made.sem, 1)

            def block_of(n, nxt, prev):
                pe.wait_ge(norm.normed.sem, norm.normed.at(n))
                for j in range(TILES):
                    if j % 3 < 2:
                        pe.wait_ge(copied.sem, copied.at(item(n, j) - 2))
                        pe.matmul(banks[j % 3][:, :], w["proj"][:, j, :], xn[:, 3:],
                                  start=True, stop=True).then_inc(made.sem, 1)
                    else:
                        if j >= 6 or prev:
                            pe.wait_ge(silu.sem, silu.at(n * TILES + j - 6))
                        for i in range(4):
                            mm = pe.matmul(k.bank[6 + j // 3 % 2][:, :], tap_w[:, j // 3, i, :], xn[:, i:i + TB],
                                           start=(i == 0), stop=(i == 3))
                        mm.then_inc(made.sem, 1)
                    if j == 1 and nxt:
                        norm.pe_centre(pe, n + 1)
                    if j == 3 and prev:
                        key_sums(n - 1)
                    if j == 4 and nxt:
                        norm.pe_variance(pe, n + 1)
                pe.wait_ge(z_out.sem, z_out.at(n - 1))
                for j in range(TPB):
                    mm = pe.matmul(k.bank[4][:, j * 36:(j + 1) * 36], xn[:, 3 + j * P:3 + (j + 1) * P], w["gates"],
                                   start=True, stop=True)
                mm.then_inc(z_made.sem, 1)

            norm.pe_centre(pe, 0)
            norm.pe_variance(pe, 0)
            pe.wait_ge(taps_ready.sem, taps_ready.at(0))
            each_block(pe, block_of)
            key_sums(NB - 1)

        @block.scalar
        def _(act):
            def copy(n, j):
                s = j % 3
                if s == 2:
                    return
                act.wait_ge(made.sem, made.at(n * TILES + j))
                act.wait_ge(convolved.sem, convolved.at(item(n, j) - 2))
                act.activation(pre[:, s, 3:3 + TB], banks[s][:, :], ACT.Copy)
                act.wait_ge(silu.sem, silu.at(n * TILES + j - 3))
                act.activation(acc[:, s, :], banks[s][:, :], ACT.Copy,
                               scale=w["conv"][:, 4 * j + 3:4 * j + 4]).then_inc(copied.sem, 1)

            def finish(n, j):
                if j % 3 < 2:
                    act.wait_ge(convolved.sem, convolved.at(item(n, j)))
                    src = acc[:, j % 3, :]
                else:
                    act.wait_ge(made.sem, made.at(n * TILES + j))
                    src = k.bank[6 + j // 3 % 2][:, :]
                act.wait_ge(kept[j % 4].sem, n * (16 * TILES // 4) + (16 * (j // 4) + kept[j % 4].start))
                if j < 2:
                    act.wait_ge(squared.sem, squared.at(n * 2 - 2 + j))
                act.activation(out[:, j % 4, :], src, ACT.Silu).then_inc(silu.sem, 1)

            def block_of(n, nxt, prev):
                for j in range(TILES):
                    copy(n, j)
                    if j > 1:
                        finish(n, j - 2)
                    if j == 2 and nxt:
                        norm.act_square(act, n + 1)
                    if j == 5 and nxt:
                        norm.act_deviation(act, n + 1)
                finish(n, TILES - 2)
                finish(n, TILES - 1)

            norm.act_square(act, 0)
            norm.act_deviation(act, 0)
            each_block(act, block_of)
            act.wait_ge(dve_step.sem, dve_step.at(0))
            act.activation(k_sum[:, :, :], k_sum[:, :, :], ACT.Sqrt).then_inc(act_step.sem, 1)
            act.activation(decay_rate[:, :], w["A_log"], ACT.Exp)
            act.activation(z[:, :, 16:36], z[:, :, 16:36], ACT.Exp, scale=-1.0)
            act.activation(tmp[:, :, :], tmp[:, :, :], ACT.Exp, scale=-1.0)
            act.drain()
            act.activation(tmp[:, :, :], tmp[:, :, :], ACT.Ln, bias=w["one"]).then_inc(act_step.sem, 1)

        @block.gpsimd
        def _(pool):
            pool.memset(halo[:, :, :], 0.0)
            pool.memset(nought[:, :], 0.0)
            for q in range(4):
                for i in range(4):
                    pool.tensor_tensor(tap_w[:, q, i, :], w["proj"][:, 3 * q + 2, :], taps[:, q, i, :], ALU.mult)
            pool.drain().then_inc(taps_ready.sem, 1)

            def block_of(n, nxt, prev):
                for j in range(TILES):
                    s = j % 3
                    if s == 2:
                        continue
                    pool.wait_ge(copied.sem, copied.at(item(n, j)))
                    pool.tensor_tensor(pre[:, s, 0:3], halo[:, j, 0:3], nought[:, 0:3], ALU.add)
                    pool.drain()
                    pool.tensor_tensor(halo[:, j, 0:3], pre[:, s, TB:TB + 3], nought[:, 0:3], ALU.add).then_inc(haloed.sem, 1)
                for p in range(2):
                    j = KTILE + p
                    pool.wait_ge(silu.sem, silu.at(n * TILES + j))
                    pool.wait_ge(sums_made.sem, sums_made.at(n - 1))
                    pool.tensor_tensor(k_sq[:, p, :], out[:, j % 4, :], out[:, j % 4, :],
                                       ALU.mult).then_inc(squared.sem, 1)

            each_block(pool, block_of)

        @block.vector
        def _(dve):
            def sums(n):
                dve.wait_ge(sums_made.sem, sums_made.at(n))
                dve.tensor_scalar(k_sum[:, bass.ts(n, TPB), :], k.bank[5][:, 0:TPB * 4].rearrange("p (c z) -> p c z", z=4),
                                  0.0, None, ALU.add).then_inc(sums_out.sem, 1)

            def block_of(n, nxt, prev):
                for j in range(TILES):
                    s = j % 3
                    if s < 2:
                        dve.wait_ge(haloed.sem, haloed.at(item(n, j)))
                        for i in range(3):
                            dve.scalar_tensor_tensor(acc[:, s, :], pre[:, s, i:i + TB], w["conv"][:, 4 * j + i:4 * j + i + 1],
                                                     acc[:, s, :], ALU.mult, ALU.add)
                            dve.drain()
                        dve.drain().then_inc(convolved.sem, 1)
                    elif j == 5 and prev:
                        sums(n - 1)
                    if 7 <= j < 11 and nxt:
                        norm.dve_invert(dve, n + 1, j - 7)
                dve.wait_ge(z_made.sem, z_made.at(n))
                dve.tensor_scalar(z[:, bass.ts(n, TPB), :], k.bank[4][:, 0:TPB * 36].rearrange("p (c z) -> p c z", z=36),
                                  0.0, None, ALU.add).then_inc(z_out.sem, 1)
                if nxt:
                    dve.tensor_scalar(xn[:, 0:3], xn[:, TB:TB + 3], 0.0, None, ALU.add)
                    norm.dve_apply(dve, n + 1)

            dve.memset(xn[:, 0:3], 0.0)
            norm.dve_norm(dve, 0)
            each_block(dve, block_of)
            sums(NB - 1)
            dve.drain()
            za, t = z[:, :, 0:16], gate_columns(table)
            over = lambda a, m: a.unsqueeze(1).to_broadcast([P, NCH, m])
            dve.tensor_tensor(za, za, over(w["dt_bias"], 16), ALU.add)
            dve.drain()
            dve.scalar_tensor_tensor(tmp[:, :, :], za, -1.0, za, ALU.mult, ALU.max)
            dve.drain().then_inc(dve_step.sem, 1)
            dve.wait_ge(act_step.sem, act_step.at(1))
            dve.scalar_tensor_tensor(tmp[:, :, :], za, 0.0, tmp[:, :, :], ALU.max, ALU.add)
            dve.tensor_scalar(k_sum[:, :, :], k_sum[:, :, :], 1e-6, None, ALU.add)
            dve.tensor_scalar(z[:, :, 16:36], z[:, :, 16:36], 1.0, 1e30, ALU.add, ALU.min)
            dve.drain()
            dve.scalar_tensor_tensor(t["g"], tmp[:, :, :], -1.0, over(decay_rate[:, :], 16), ALU.mult, ALU.mult)
            dve.reciprocal(t["inv_k"], k_sum[:, :, :])
            dve.reciprocal(z[:, :, 16:36], z[:, :, 16:36])
            dve.drain()
            dve.tensor_scalar(t["alpha"], z[:, :, 16:32], 0.125, None, ALU.mult)
            dve.tensor_copy(t["beta"], z[:, :, 32:36])
            dve.drain()
            dve.tensor_tensor(t["alpha_sq"], t["alpha"], t["alpha"], ALU.mult)
            dve.drain()
            dve.tensor_scalar(t["alpha_sq"], t["alpha_sq"], 1.0 / 64, None, ALU.mult)

        @block.sync
        def _(sp):
            with sp.Fori(0, NB) as n:
                for j in range(TILES):
                    sp.wait_ge(silu.sem, silu.at(n * TILES + j))
                    sp.dma_start(scratch[bass.ts(n, TPB), :, j, :].rearrange("c p t -> p c t"),
                                 out[:, j % 4, :].rearrange("p (c t) -> p c t", t=CH)).then_inc(kept[j % 4].sem, 16)
            for b in range(4):
                sp.wait_ge(kept[b].sem, 16 * NB * TILES // 4 + kept[b].start)

    norm.passed()
    k.passed({"gka_made": NB * TILES, "gka_copied": NB * 8, "gka_convolved": NB * 8, "gka_taps_ready": 1, "gka_silu": NB * TILES,
              "gka_haloed": NB * 8,
              **{f"gka_kept_{b}": 16 * NB * TILES // 4 for b in range(4)}, "gka_k_squared": NB * 2, "gka_z_made": NB, "gka_z_out": NB,
              "gka_sums_made": NB, "gka_sums_out": NB,
              "gka_act_step": 2, "gka_dve_step": 1})


def run_chunks(k, w, scratch):
    nc = k.nc
    G, R, HD, PAIRS = 4, 4, 64, 2
    st = Carve(k.big_high)
    qkv = [st(f"qkv{b}", [P, 12, CH]) for b in range(2)]
    gates = [st(f"gates{b}", [P, GATES]) for b in range(2)]
    k_pad = [st(f"k_pad{b}", [P, 2, PAIRS, CH]) for b in range(2)]
    kv = [st(f"kv{b}", [P, PAIRS, 2, 2, HD]) for b in range(2)]
    since = [st(f"since{b}", [P, PAIRS, R, CH]) for b in range(2)]
    decay = [k.probs[:, b * 2048:(b + 1) * 2048].rearrange("p (g r t) -> p g r t", g=G, r=R) for b in range(2)]
    until = [st(f"until{b}", [P, G, R]) for b in range(2)]
    g_masked = st("g_masked", [P, G, R, CH])
    kd = st("kd", [P, PAIRS, R, 2, HD])
    scores = st("scores", [P, G, R, CH])
    x_new = st("x_new", [P, PAIRS, R, CH])
    x_since = st("x_since", [P, PAIRS, R, CH])
    state = st("state", [P, PAIRS, R, 2, 2, HD])
    o = st("o", [P, PAIRS, R, 2, HD])
    o_sq = st("o_sq", [P, PAIRS, R, 2, HD])
    o_sum = st("o_sum", [P, PAIRS, R, 2])
    o_var = st("o_var", [P, PAIRS, R, 2])
    oT = st("oT", [P, PAIRS * R, CH])
    names = ("gka_loaded", "gka_gates", "gka_g_masked", "gka_decay_made", "gka_decay_out", "gka_turned", "gka_kv",
             "gka_k_pad", "gka_kd", "gka_scores", "gka_masked", "gka_u", "gka_x", "gka_x_since", "gka_o_out",
             "gka_state_made", "gka_state", "gka_o_var", "gka_o_sd", "gka_o_scaled", "gka_o_turned",
             "gka_oT", "gka_y", "gka_x_done")
    (loaded, gates_here, g_ready, decay_made, decay_out, turned, kv_ready, k_pad_ready, kd_ready, scored, masked,
     u_made, x_ready, since_ready, o_out, state_made, state_ready, var_ready, sd_ready, o_scaled, o_turned, oT_ready,
     y_ready, x_done) = (k.counter(n) for n in names)
    flat = lambda t: t.rearrange("p r t -> p (r t)")
    PREP = 7

    def reused(c):
        return not isinstance(c, int) or c >= 2

    def each_chunk(eng, prologue, chunk, epilogue):
        prologue()
        chunk(0, 0, True, False)
        with eng.Fori(0, (NCH - 2) // 2) as i:
            chunk(i * 2 + 1, 1, True, True)
            chunk(i * 2 + 2, 0, True, True)
        chunk(NCH - 1, 1, False, True)
        epilogue()

    with nc.Block() as block:
        @block.sync
        def _(sp):
            def load(c, b):
                sp.dma_start(qkv[b][:, :, :], scratch[bass.ds(c, 1), :, :, :].rearrange("c p j t -> p (c j) t")
                             ).then_inc(loaded.sem, 16)

            load(0, 0)

            def chunk(c, b, nxt, prev):
                if nxt:
                    sp.wait_ge(u_made.sem, u_made.at(c * 6 - 1))
                    sp.wait_ge(loaded.sem, c * 16 + (16 + loaded.start))
                    load(c + 1, 1 - b)

            each_chunk(sp, lambda: None, chunk, lambda: None)

        @block.tensor
        def _(pe):
            def made(c, i):
                return decay_made.at(c * PREP + i)

            def prep(c, b, i):
                bank = k.bank[i % 2]
                if i < 4:
                    if i == 0:
                        pe.wait_ge(kv_ready.sem, kv_ready.at(c - 1))
                    pe.wait_ge(decay_out.sem, decay_out.at(c * PREP + i - 2))
                    pe.wait_ge(g_ready.sem, g_ready.at(c * G + i))
                    pe.matmul(bank[:, :], w["later"], flat(g_masked[:, i, :, :]), start=True, stop=False)
                    pe.matmul(bank[:, :], k.ident_bf[:, :], k.mask_bf[:, :], start=False,
                              stop=True).then_inc(decay_made.sem, 1)
                elif i < 6:
                    p = i - 4
                    pe.wait_ge(decay_out.sem, decay_out.at(c * PREP + i - 2))
                    for half in range(2):
                        mm = pe.matmul(bank[64 * half:64 * half + 64, :], w["ones"][:, 0:64],
                                       flat(g_masked[:, 2 * p + half, :, :]), start=True, stop=True)
                    mm.then_inc(decay_made.sem, 1)
                elif i == 6:
                    pe.wait_ge(loaded.sem, c * 16 + (16 + loaded.start))
                    pe.wait_ge(decay_out.sem, decay_out.at(c * PREP + 4))
                    for j in range(4):
                        mm = pe.transpose(bank[:, j * P:(j + 1) * P], qkv[b][:, 8 + j, :], k.ident[:, :])
                    mm.then_inc(turned.sem, 1)
                else:
                    pe.wait_ge(decay_out.sem, decay_out.at(c * PREP + 5))
                    pe.matmul(bank[:, 0:16], w["later"], gates[b][:, 0:16], start=True, stop=True).then_inc(decay_made.sem, 1)

            def score(c, b, u):
                if u == 0:
                    pe.wait_ge(k_pad_ready.sem, k_pad_ready.at(c))
                for g in range(G):
                    p, half = g // 2, g % 2
                    if u > 0 and half == 0:
                        pe.wait_ge(x_ready.sem, x_ready.at(c * 4 + (2 * (u - 1) + p)))
                    pe.wait_ge(masked.sem, masked.at(c * 12 + (u * 4 + g - 2)))
                    x = qkv[b][:, 4 * p:4 * p + 4, :] if u == 0 else x_new[:, p, :, :]
                    pe.matmul(k.bank[2 + half][:, :], k_pad[b][:, half, p, :], flat(x),
                              start=True, stop=True).then_inc(scored.sem, 1)

            def product(c, b, u):
                for p in range(PAIRS):
                    if u == 0:
                        pe.wait_ge(state_ready.sem, state_ready.at(c * 4 - 1))
                        pe.wait_ge(o_out.sem, o_out.at(c * 2 + p - 2))
                        pe.wait_ge(kv_ready.sem, kv_ready.at(c))
                    pe.wait_ge(since_ready.sem, since_ready.at(c * 6 + (2 * u + p)))
                    for r in range(R):
                        pe.matmul(k.bank[4 + p][:, r * CH:(r + 1) * CH], state[:, p, r, 0, :, :].rearrange("p h f -> p (h f)"),
                                  x_since[:, p, r, :], start=(r == 0), stop=False)
                    for half in range(2):
                        g = 2 * p + half
                        pe.wait_ge(masked.sem, masked.at(c * 12 + (u * 4 + g)))
                        mm = pe.matmul(k.bank[4 + p][64 * half:64 * half + 64, :], kv[b][:, p, 0, half, :],
                                       flat(scores[:, g, :, :]), start=False, stop=True)
                    mm.then_inc(u_made.sem, 1)

            def output(c, b, p):
                if True:
                    pe.wait_ge(since_ready.sem, since_ready.at(c * 6 + (4 + p)))
                    pe.wait_ge(masked.sem, masked.at(c * 12 + (8 + 2 * p + 1)))
                    for r in range(R):
                        cols = k.bank[4 + p][:, r * CH:(r + 1) * CH]
                        pe.matmul(cols, x_since[:, p, r, :], state[:, p, r, 1, :, :].rearrange("p h f -> p (h f)"),
                                  start=(r == 0), stop=False)
                        for half in range(2):
                            mm = pe.matmul(cols[:, 64 * half:64 * half + 64], scores[:, 2 * p + half, r, :],
                                           kv[b][:, p, 1, half, :], start=False,
                                           stop=(r == R - 1 and half == 1))
                    mm.then_inc(u_made.sem, 1)

            def new_state(c, b, p):
                for i in (2 * p, 2 * p + 1):
                    if i == 0:
                        pe.wait_ge(kd_ready.sem, kd_ready.at(c * 2))
                        pe.wait_ge(x_done.sem, x_done.at(c - 1))
                    elif i == 2:
                        pe.wait_ge(kd_ready.sem, kd_ready.at(c * 2 + 1))
                    if i == 1:
                        pe.wait_ge(oT_ready.sem, oT_ready.at(c * 2 - 1))
                    if i > 1:
                        pe.wait_ge(state_ready.sem, state_ready.at(c * 4 + (i - 2)))
                    for j in range(2):
                        r = 2 * (i % 2) + j
                        mm = pe.matmul(k.bank[6 + i % 2][:, j * 256:(j + 1) * 256],
                                       kd[:, p, r, :, :].rearrange("p h f -> p (h f)"),
                                       kv[b][:, p, :, :, :].rearrange("p v h f -> p (v h f)"), start=True, stop=True)
                    mm.then_inc(state_made.sem, 1)

            def turn_o(c):
                pe.wait_ge(o_scaled.sem, o_scaled.at(c))
                pe.wait_ge(state_ready.sem, state_ready.at(c * 4 + 3))
                for p in range(PAIRS):
                    for r in range(R):
                        mm = pe.transpose(k.bank[6 + p][:, r * CH:(r + 1) * CH], o[:, p, r, :, :].rearrange("p h f -> p (h f)"),
                                          k.ident[:, :])
                    mm.then_inc(o_turned.sem, 1)

            def project(c):
                pe.wait_ge(oT_ready.sem, oT_ready.at(c * 2 + 1))
                for i in range(8):
                    mm = pe.matmul(k.bank[6][:, 0:CH], w["out"][:, i, :], oT[:, i, :], start=(i == 0), stop=(i == 7))
                mm.then_inc(y_ready.sem, 1)

            def chunk(c, b, nxt, prev):
                score(c, b, 0)
                product(c, b, 0)
                score(c, b, 1)
                if nxt:
                    prep(c + 1, 1 - b, 0)
                    prep(c + 1, 1 - b, 1)
                product(c, b, 1)
                score(c, b, 2)
                if nxt:
                    for i in range(2, 6):
                        prep(c + 1, 1 - b, i)
                if prev:
                    turn_o(c - 1)
                output(c, b, 0)
                if prev:
                    project(c - 1)
                if nxt:
                    prep(c + 1, 1 - b, 6)
                    prep(c + 1, 1 - b, 7)
                new_state(c, b, 0)
                output(c, b, 1)
                new_state(c, b, 1)

            def prologue():
                for i in range(8):
                    prep(0, 0, i)

            def epilogue():
                turn_o(NCH - 1)
                project(NCH - 1)

            each_chunk(pe, prologue, chunk, epilogue)

        @block.scalar
        def _(act):
            def prep_copies(c, b):
                if reused(c):
                    act.wait_ge(u_made.sem, u_made.at(c * 6 - 7))
                    act.wait_ge(decay_made.sem, decay_made.at(c * PREP - PREP - 1))
                act.activation(gates[b][:, :], k.gates[:, bass.ds(c, 1), :].rearrange("p c z -> p (c z)"), ACT.Copy).then_inc(gates_here.sem, 1)
                act.wait_ge(loaded.sem, c * 16 + (16 + loaded.start))
                for half in range(2):
                    last = act.activation(k_pad[b][:, half, :, :], qkv[b][:, 8:10, :], ACT.Copy, scale=w["half"][:, half:half + 1])
                last.then_inc(k_pad_ready.sem, 1)

            def prep(c, b, i):
                act.wait_ge(decay_made.sem, decay_made.at(c * PREP + i))
                if i == 0 and reused(c):
                    act.wait_ge(state_ready.sem, state_ready.at(c * 4 - 5))
                bank = k.bank[i % 2]
                if i < 4:
                    act.activation(flat(decay[b][:, i, :, :]), bank[:, :], ACT.Exp).then_inc(decay_out.sem, 1)
                elif i < 6:
                    act.activation(flat(since[b][:, i - 4, :, :]), bank[:, :], ACT.Exp).then_inc(decay_out.sem, 1)
                else:
                    act.activation(until[b][:, :, :].rearrange("p g r -> p (g r)"), k.bank[1][:, 0:16],
                                   ACT.Exp).then_inc(decay_out.sem, 1)

            def o_copies(c):
                act.wait_ge(o_turned.sem, o_turned.at(c * 2 - 1))
                for p in range(PAIRS):
                    act.wait_ge(u_made.sem, u_made.at(c * 6 + (4 + p)))
                    fl = lambda t: t[:, p, :, :, :].rearrange("p r h f -> p (r h f)")
                    act.activation(fl(o_sq), k.bank[4 + p][:, :], ACT.Square)
                    act.activation(fl(o), k.bank[4 + p][:, :], ACT.Copy).then_inc(o_out.sem, 1)

            def deviation(c):
                act.wait_ge(var_ready.sem, var_ready.at(c))
                act.activation(o_var[:, :, :, :], o_var[:, :, :, :], ACT.Sqrt).then_inc(sd_ready.sem, 1)

            def oT_copies(c):
                act.wait_ge(y_ready.sem, y_ready.at(c - 1))
                for p in range(PAIRS):
                    act.wait_ge(o_turned.sem, o_turned.at(c * 2 + p))
                    act.activation(flat(oT[:, 4 * p:4 * p + 4, :]), k.bank[6 + p][:, :], ACT.Copy,
                                   scale=w["norm_w"]).then_inc(oT_ready.sem, 1)

            def chunk(c, b, nxt, prev):
                if nxt:
                    prep_copies(c + 1, 1 - b)
                if nxt:
                    for i in range(2):
                        prep(c + 1, 1 - b, i)
                if prev:
                    deviation(c - 1)
                if nxt:
                    for i in range(2, 4):
                        prep(c + 1, 1 - b, i)
                if nxt:
                    for i in range(4, 6):
                        prep(c + 1, 1 - b, i)
                if prev:
                    oT_copies(c - 1)
                if nxt:
                    prep(c + 1, 1 - b, 6)
                o_copies(c)

            def prologue():
                prep_copies(0, 0)
                for i in range(7):
                    prep(0, 0, i)

            def epilogue():
                deviation(NCH - 1)
                oT_copies(NCH - 1)

            each_chunk(act, prologue, chunk, epilogue)

        @block.gpsimd
        def _(pool):
            def mask_g(c, b, gs):
                if gs[0] == 0:
                    pool.wait_ge(gates_here.sem, gates_here.at(c))
                for g in gs:
                    pool.wait_ge(decay_made.sem, decay_made.at(c * PREP - 2))
                    pool.tensor_tensor(g_masked[:, g, :, :], gates[b][:, 4 * g:4 * g + 4].unsqueeze(2).to_broadcast([P, R, CH]),
                                       w["upto"].unsqueeze(1).to_broadcast([P, R, CH]), ALU.mult).then_inc(g_ready.sem, 1)

            def scale_x(c, b, u):
                for p in range(PAIRS):
                    if u == 0:
                        pool.wait_ge(decay_out.sem, decay_out.at(c * PREP + 5))
                        pool.wait_ge(loaded.sem, c * 16 + (16 + loaded.start))
                        x = qkv[b][:, 4 * p:4 * p + 4, :]
                    else:
                        pool.wait_ge(x_ready.sem, x_ready.at(c * 4 + (2 * (u - 1) + p)))
                        x = x_new[:, p, :, :]
                    pool.wait_ge(u_made.sem, u_made.at(c * 6 + (2 * u + p - 2)))
                    pool.tensor_tensor(x_since[:, p, :, :], x, since[b][:, p, :, :], ALU.mult).then_inc(since_ready.sem, 1)

            def keys_until(c, b):
                pool.wait_ge(kv_ready.sem, kv_ready.at(c))
                pool.wait_ge(decay_out.sem, decay_out.at(c * PREP + 6))
                for p in range(PAIRS):
                    pool.wait_ge(state_made.sem, state_made.at(c * 4 - 1))
                    keys = kv[b][:, p, 0, :, :].unsqueeze(1).to_broadcast([P, R, 2, HD])
                    by = until[b][:, 2 * p:2 * p + 2, :].rearrange("p h r -> p r h").unsqueeze(3).to_broadcast([P, R, 2, HD])
                    pool.tensor_tensor(kd[:, p, :, :, :], keys, by, ALU.mult).then_inc(kd_ready.sem, 1)

            def chunk(c, b, nxt, prev):
                scale_x(c, b, 0)
                if nxt:
                    mask_g(c + 1, 1 - b, (0, 1))
                scale_x(c, b, 1)
                keys_until(c, b)
                if nxt:
                    mask_g(c + 1, 1 - b, (2, 3))
                scale_x(c, b, 2)

            each_chunk(pool, lambda: mask_g(0, 0, (0, 1, 2, 3)), chunk, lambda: None)

        @block.vector
        def _(dve):
            def mask_scores(c, b, u):
                for g in range(G):
                    dve.wait_ge(scored.sem, scored.at(c * 12 + (u * 4 + g)))
                    if u == 0 and g == 0:
                        dve.wait_ge(decay_out.sem, decay_out.at(c * PREP + 3))
                        dve.wait_ge(gates_here.sem, gates_here.at(c))
                    dve.wait_ge(u_made.sem, u_made.at(c * 6 + (2 * u + g // 2 - 2)))
                    dve.scalar_tensor_tensor(flat(scores[:, g, :, :]), k.bank[2 + g % 2][:, :], gates[b][:, 36 + g:37 + g],
                                             flat(decay[b][:, g, :, :]), ALU.mult, ALU.mult).then_inc(masked.sem, 1)

            def next_x(c, b, u):
                for p in range(PAIRS):
                    dve.wait_ge(u_made.sem, u_made.at(c * 6 + (2 * u + p)))
                    dve.scalar_tensor_tensor(flat(x_new[:, p, :, :]), k.bank[4 + p][:, :], -0.25,
                                             flat(qkv[b][:, 4 * p:4 * p + 4, :]), ALU.mult, ALU.add).then_inc(x_ready.sem, 1)

            def keys_values(c, b):
                dve.wait_ge(turned.sem, turned.at(c))
                dve.wait_ge(gates_here.sem, gates_here.at(c))
                if reused(c):
                    dve.wait_ge(state_made.sem, state_made.at(c * 4 - 5))
                cols = k.bank[0][:, :].rearrange("p (v q f) -> p v q f", v=2, f=HD)
                for v, col in ((0, 36), (1, 32)):
                    for p in range(PAIRS):
                        last = dve.tensor_tensor(kv[b][:, p, v, :, :], cols[:, v, 2 * p:2 * p + 2, :],
                                                 gates[b][:, col + 2 * p:col + 2 * p + 2].unsqueeze(2).to_broadcast([P, 2, HD]),
                                                 ALU.mult)
                last.then_inc(kv_ready.sem, 1)

            def update_state(c, b):
                for i in range(4):
                    dve.wait_ge(state_made.sem, state_made.at(c * 4 + i))
                    for j in range(2):
                        p, r = i // 2, 2 * (i % 2) + j
                        add = k.bank[6 + i % 2][:, j * 256:(j + 1) * 256].rearrange("p (v h f) -> p v h f", v=2, h=2)
                        for half in range(2):
                            rows = slice(64 * half, 64 * half + 64)
                            last = dve.scalar_tensor_tensor(state[rows, p, r, :, half, :], state[rows, p, r, :, half, :],
                                                            since[b][rows, p, r, CH - 1:CH], add[rows, :, half, :],
                                                            ALU.mult, ALU.add)
                    last.then_inc(state_ready.sem, 1)

            def variance(c):
                dve.wait_ge(o_out.sem, o_out.at(c * 2 + 1))
                dve.tensor_reduce(o_sum[:, :, :, :].rearrange("p a r h -> p (a r h)"),
                                  o_sq[:, :, :, :, :].rearrange("p a r h f -> p (a r h) f"), AX.X, ALU.add)
                dve.drain()
                t = gate_columns(k.gates[:, bass.ds(c, 1), :])
                for p in range(PAIRS):
                    a = t["alpha_sq"][:, :, 8 * p:8 * p + 8].rearrange("p c (h r) -> p r (c h)", h=2)
                    dve.tensor_tensor(o_var[:, p, :, :], o_sum[:, p, :, :], a, ALU.mult)
                dve.drain()
                dve.tensor_scalar(o_var[:, :, :, :], o_var[:, :, :, :], 1e-6, None, ALU.add).then_inc(var_ready.sem, 1)

            def scale_o(c):
                dve.wait_ge(sd_ready.sem, sd_ready.at(c))
                dve.reciprocal(o_var[:, :, :, :], o_var[:, :, :, :])
                dve.drain()
                t = gate_columns(k.gates[:, bass.ds(c, 1), :])
                for p in range(PAIRS):
                    a = t["alpha"][:, :, 8 * p:8 * p + 8].rearrange("p c (h r) -> p r (c h)", h=2)
                    dve.tensor_tensor(o_var[:, p, :, :], o_var[:, p, :, :], a, ALU.mult)
                dve.drain()
                every = "p a r h f -> p (a r h) f"
                dve.tensor_tensor(o[:, :, :, :, :].rearrange(every), o[:, :, :, :, :].rearrange(every),
                                  o_var[:, :, :, :].rearrange("p a r h -> p (a r h)").unsqueeze(2).to_broadcast([P, 16, HD]),
                                  ALU.mult).then_inc(o_scaled.sem, 1)

            def add_to_x(c):
                dve.wait_ge(y_ready.sem, y_ready.at(c))
                xb = k.x[:, bass.ts(c, CH)]
                dve.tensor_tensor(xb, k.bank[6][:, 0:CH], xb, ALU.add).then_inc(x_done.sem, 1)

            def chunk(c, b, nxt, prev):
                mask_scores(c, b, 0)
                next_x(c, b, 0)
                mask_scores(c, b, 1)
                if prev:
                    variance(c - 1)
                next_x(c, b, 1)
                mask_scores(c, b, 2)
                if prev:
                    scale_o(c - 1)
                if prev:
                    add_to_x(c - 1)
                if nxt:
                    keys_values(c + 1, 1 - b)
                update_state(c, b)

            def prologue():
                dve.memset(state[:, :, :, :, :, :], 0.0)
                dve.drain()
                keys_values(0, 0)

            def epilogue():
                variance(NCH - 1)
                scale_o(NCH - 1)
                add_to_x(NCH - 1)

            each_chunk(dve, prologue, chunk, epilogue)

    k.passed({"gka_loaded": 16 * NCH, "gka_gates": NCH, "gka_g_masked": NCH * G, "gka_decay_made": NCH * PREP,
              "gka_decay_out": NCH * PREP, "gka_turned": NCH, "gka_kv": NCH, "gka_k_pad": NCH, "gka_kd": NCH * 2,
              "gka_scores": NCH * 12, "gka_masked": NCH * 12, "gka_u": NCH * 6, "gka_x": NCH * 4,
              "gka_x_since": NCH * 6, "gka_o_out": NCH * 2, "gka_state_made": NCH * 4, "gka_state": NCH * 4,
              "gka_o_var": NCH, "gka_o_sd": NCH, "gka_o_scaled": NCH, "gka_o_turned": NCH * 2,
              "gka_oT": NCH * 2, "gka_y": NCH, "gka_x_done": NCH})


ROUTE_STEPS = ("logits", "logits_out", "by_token", "shifted", "exped", "weighed", "turned", "rows")
COUNTERS = (
    ["ln_centred", "ln_squared", "ln_variance", "ln_deviation", "ln_normed"]
    + [f"{r}_{x}" for r in ("route", "down_route", "wide_route") for x in ROUTE_STEPS]
    + ["spread", "spread_out", "scaled", "expert_used", "y_ready", "x_done", "router_pre", "router_hidden",
       "hidden_pre", "hidden_done", "gate_ready", "up_ready", "gate_silu", "inter_ready", "down_spread",
       "down_spread_out", "scan_input", "scanned", "win_diff", "win_square", "win_sum", "win_size", "win_unit",
       "win_weight", "win_dir", "win_dots", "win_exp", "win_mix", "win_value", "win_out",
       "win_done", "qk_pre", "qk_out", "qk_split", "qk_kept", "operands_loaded", "max_loaded", "sums_dealt", "sums_inverted", "inverse_back",
            "row_scores", "row_max", "max_split", "max_turned", "max_out", "scores", "exponentials", "summed",
            "sums_out", "sums_spread", "normalised", "v_pre", "v_ready",
            "w_out_ready"]
    + ["gka_" + x for x in (
        "made", "copied", "convolved", "kept_0", "kept_1", "kept_2", "kept_3", "silu", "k_squared", "haloed", "taps_ready", "z_made", "z_out", "sums_made", "sums_out", "act_step", "dve_step",
        "loaded", "gates", "g_masked", "decay_made", "decay_out", "turned", "kv", "k_pad", "kd", "scores", "masked",
        "u", "x", "x_since", "o_out", "state_made", "state", "o_var", "o_sd", "o_scaled", "o_turned", "oT", "y", "x_done")]
)


WIN = 8


def ramp(j, w):
    return 0.1 + 0.9 * j / (w - 1) if w > 1 else 0.1


def first_weight(p, m):
    return ramp(m - 1, p) if 1 <= m <= p else 0.0


def pieces(**a):
    t = lambda x, *axes: np.transpose(x, axes)
    f = np.float32
    eye = np.eye(P, dtype=f)

    def selector(width, groups, of):
        s = np.zeros((3 * width, groups, P), f)
        for part in range(3):
            for e in range(width):
                for grp in range(groups):
                    for m in range(P):
                        if of(grp, m) == e:
                            s[part * width + e, grp, m] = 1
        return np.concatenate([s.reshape(3 * width, groups * P), np.zeros((P - 3 * width, groups * P), f)], 0)

    out = {
        "const": {
            "centre": eye - f(1 / D), "mean": np.full((P, P), 1 / D, f), "ident": eye,
            "ln_eps": np.full((P, 1), LN_EPS, f),
            "descending8": np.tile(np.arange(8, 0, -1, dtype=f)[None], (P, 1)),
            "descending16": np.tile(np.arange(16, 0, -1, dtype=f)[None], (P, 1)),
        },
        "select": {
            "selector8": selector(8, 8, lambda g, m: g), "selector16": selector(16, 16, lambda g, m: g),
            "chunk_selector": selector(16, 4, lambda g, m: 4 * g + m // 32),
            "mask": np.tile(np.tril(np.full((P, P), -29952, f), -1), (1, 4)),
        },
        "L0": {
            "expert_w": t(a["L0_ffn_expert_w"], 2, 0, 1).reshape(D, -1),
            "router": a["L0_ffn_router_w"].T, "router_b": a["L0_ffn_router_b"][:, None],
            "expert_b": np.concatenate([a["L0_ffn_expert_b"]] * 3 + [np.zeros((P - 24, D), f)], 0),
        },
        "L1": {
            "rw1": a["L1_ffn_rw1"], "rb1": a["L1_ffn_rb1"][:, None], "rw2": a["L1_ffn_rw2"],
            "rb2": a["L1_ffn_rb2"][:, None],
            "be1": t(a["L1_ffn_be1"].reshape(8, 4, P), 2, 0, 1).reshape(P, -1),
            "be2": a["L1_ffn_be2"].T,
            "we1": t(a["L1_ffn_we1"], 1, 0, 2).reshape(D, -1),
            "we2": t(a["L1_ffn_we2"].reshape(8, 4, P, D), 2, 0, 1, 3).reshape(P, -1),
        },
        "L2": {
            "router_gate_up": np.concatenate([a["L2_ffn_router_gate"].T, a["L2_ffn_router_up"].T], 1),
            "router_down": t(a["L2_ffn_router_down"].reshape(8, 4, P), 2, 1, 0).reshape(P, -1),
            "gate": t(a["L2_ffn_w_gate"], 2, 0, 1).reshape(D, -1),
            "up": t(a["L2_ffn_w_up"], 2, 0, 1).reshape(D, -1),
            "down": t(a["L2_ffn_w_down"].reshape(8, D, 4, P), 3, 0, 2, 1).reshape(P, -1),
        },
        "L3": {
            "router": a["L3_ffn_router_w"],
            "gate": np.concatenate([t(a["L3_ffn_wg_r"], 1, 0, 2).reshape(D, -1), t(a["L3_ffn_wg_s"], 1, 0, 2).reshape(D, -1)], 1),
            "up": np.concatenate([t(a["L3_ffn_wu_r"], 1, 0, 2).reshape(D, -1), t(a["L3_ffn_wu_s"], 1, 0, 2).reshape(D, -1)], 1),
            "down": np.concatenate([t(a["L3_ffn_wd_r"].reshape(4, P, D), 1, 0, 2).reshape(P, -1), a["L3_ffn_wd_s"].reshape(P, D)], 1),
        },
        "A3": {
            "w_out": a["L3_attn_w_out"].T, "a": a["L3_attn_a"][:, None], "b": a["L3_attn_b"][:, None],
            "b_out": a["L3_attn_b_out"][:, None],
        },
        "A0": {
            "proj": np.concatenate([a["L0_attn_Wq"][:, tile_features()], a["L0_attn_Wk"], a["L0_attn_Wv"]], 1),
            "conv": t(conv_by_tile(a["L0_attn_Wconv"]), 1, 0, 2).reshape(P, -1),
            "gates": np.concatenate([a["L0_attn_Wa"], a["L0_attn_Walpha"], a["L0_attn_Wb"]], 1),
            "out": t(a["L0_attn_Wo"][tile_features()].reshape(8, P, D), 1, 0, 2).reshape(P, -1),
            "norm_w": np.tile(a["L0_attn_norm_w"], 2)[:, None],
            "A_log": np.tile(a["L0_attn_A_log"][None], (P, 1)), "dt_bias": np.tile(a["L0_attn_dt_bias"][None], (P, 1)),
            "one": np.ones((P, 1), f), "ones": np.ones((P, 64), f),
            "half": np.repeat(np.eye(2, dtype=f), 64, 0),
            "later": np.tril(np.ones((P, P), f), -1), "upto": np.triu(np.ones((P, P), f)),
        },
        "conv_rows": {
            "taps": np.tile(t(conv_by_tile(a["L0_attn_Wconv"])[2::3], 0, 2, 1).reshape(1, -1), (P, 1)),
        },
        "A1": {
            "qk": a["L1_attn_W_in"][:, 0:256],
            "qk_bias": a["L1_attn_b_in"][0:256].reshape(2, P).T,
            "v": a["L1_attn_W_in"][:, 256:384],
            "v_bias": np.tile(a["L1_attn_b_in"][None, 256:384], (P, 1)),
            "out": np.concatenate([np.concatenate([a["L1_attn_W_out"].reshape(4, 4, 8, D), np.zeros((4, 4, 24, D), f)], 2)
                                   .reshape(4, P, D)[g] for g in range(4)], 1),
            "out_bias": a["L1_attn_b_out"][:, None],
            "spread": np.array([[float(r == m // 32 * 32 + 8) for m in range(P)] for r in range(P)], f),
        },
        "A2": {
            "guide": np.concatenate([a["L2_attn_guidance_trajectories"], np.zeros((P - 64, D), f)], 0),
            "guide_rows": a["L2_attn_guidance_trajectories"], "guideT": a["L2_attn_guidance_trajectories"].T,
            "ones": np.ones((P, P), f),
            "ramp": np.concatenate([eye * f(ramp(WIN - 1 - s, WIN)) for s in range(WIN)], 1),
            "first": np.tile(np.array([[first_weight(p, m) for m in range(WIN)] for p in range(WIN)], f).reshape(1, -1), (P, 1)),
        },
    }
    return out


def tile_features():
    return np.concatenate([np.arange(64) + 64 * (8 * p + 4 * half + r)
                           for p in range(2) for r in range(4) for half in range(2)])


def conv_by_tile(w):
    return w[np.concatenate([tile_features(), np.arange(1024, 1536)])].reshape(12, P, 4)


def packed(group):
    where, at = {}, 0
    for name, p in group.items():
        where[name] = (p.shape[0], at, at + p.shape[1])
        at += p.shape[1]
    whole = np.zeros((P, at), np.float32)
    for name, p in group.items():
        rows, a, b = where[name]
        whole[0:rows, a:b] = p
    return whole, where


STAGES = (
    ("L0", ("A0", "conv_rows")), ("A0", ()), ("L0", ("L1", "A1")),
    ("L1", ()), ("A1", ()), ("L1", ("L2", "A2")),
    ("L2", ("L3",)), ("A2", ()), ("L2", ("A3",)),
    ("L3", ()), ("A3", ()), ("L3", ()),
)


def build(nc, dram, where, x_in, x_out, stages=STAGES):
    with ExitStack() as stack:
        k = Kit(nc, stack)
        resident = {g: k.sbuf("w_" + g, list(dram[g].shape)) for g in ("const", "L0")}
        width = {g: dram[g].shape[1] for g in dram}
        first = k.sbuf("w_A0_or_L3_A3", [P, max(width["A0"], width["L3"] + width["A3"])])
        second = k.sbuf("w_gates_or_A1_or_A2", [P, max(NCH * GATES, width["A1"], width["A2"])])
        resident.update(A0=first[:, 0:width["A0"]], L3=first[:, 0:width["L3"]],
                        A3=first[:, width["L3"]:width["L3"] + width["A3"]],
                        A1=second[:, 0:width["A1"]], A2=second[:, 0:width["A2"]])
        big = k.sbuf("big", [P, 24576])
        resident["L2"] = big[:, 0:dram["L2"].shape[1]]
        resident["L1"] = big[:, 12500:12500 + dram["L1"].shape[1]]

        def piece(group, name):
            rows, a, b = where[group][name]
            t = resident[group]
            return t[0:rows, a:b]

        k.big_scaled = big[:, 12500:12500 + 16 * TB].rearrange("p (i t) -> p i t", t=TB)
        k.big_low = big[:, 0:12500]
        resident["conv_rows"] = big[:, 20000:20000 + 2048]
        k.conv_rows = resident["conv_rows"].rearrange("p (q i c) -> p q i c", q=4, i=4)
        k.big_upper = big[:, 12500:24576]
        k.big_high = big[:, 0:24576]
        k.mask_bf = k.sbuf("mask_bf", [P, TB], BF16)
        k.gates = second[:, 0:NCH * GATES].rearrange("p (c z) -> p c z", z=GATES)
        k.big_tail = big[:, 21000:24576]
        k.probs = k.sbuf("probs", [P, 8 * TB])
        k.x = k.sbuf("x", [P, T])
        k.centre, k.mean, k.ident, k.ln_eps = (piece("const", n) for n in ("centre", "mean", "ident", "ln_eps"))
        k.descending = {E: piece("const", f"descending{E}") for E in (8, 16)}
        k.ident_bf = k.sbuf("ident_bf", [P, P], BF16)
        sel8 = k.sbuf("selector8_bf", [P, 8 * P], BF16)
        sel16 = k.sbuf("selector16_bf", [P, 16 * P], BF16)
        selc = k.sbuf("chunk_selector_bf", [P, 4 * P], BF16)
        k.selector = {8: sel8[:, :].rearrange("r (e m) -> r e m", m=P), 16: sel16[:, :].rearrange("r (e m) -> r e m", m=P)}
        k.chunk_selector = selc[:, :].rearrange("r (e m) -> r e m", m=P)
        k.rows = k.sbuf("rows", [P, T], BF16)
        k.down_rows = k.sbuf("down_rows", [P, T], BF16)
        k.logT = {n: k.sbuf(n + "_logT", [P, TB]) for n in ("route", "down_route", "wide_route")}
        k.parts = {n: k.sbuf(n + "_parts", [P, TPB, P], BF16) for n in k.logT}
        k.expert_b_parts = k.sbuf("expert_b_parts", [P, 3, D], BF16)
        bias_rest = k.sbuf("bias_rest", [P, D])
        k.loaded = stack.enter_context(nc.semaphore("loaded"))
        k.loads = 4
        cast = stack.enter_context(nc.semaphore("constants_cast"))
        stored = stack.enter_context(nc.semaphore("stored"))
        select = big[:, 12500:12500 + dram["select"].shape[1]]

        with nc.Block() as block:
            @block.sync
            def _(sp):
                for region, array in ((k.x[:, :], x_in), *((resident[g][:, :], dram[g]) for g in ("const", "L0")),
                                      (select, dram["select"])):
                    sp.dma_start(region, array).then_inc(k.loaded, 16)
                for name in k.counters:
                    sp.sem_inc(k.counters[name].sem, LEAD)
                sp.wait_ge(k.loaded, 16 * k.loads)

            @block.gpsimd
            def _(pool):
                for t in (k.rows, k.down_rows, *k.logT.values()):
                    pool.memset(t[:, :], 0.0)
                for t in k.parts.values():
                    pool.memset(t[:, :, :], 0.0)
                pool.drain()

            @block.vector
            def _(dve):
                dve.wait_ge(k.loaded, 16 * k.loads)
                left = piece("L0", "expert_b")
                for part in range(3):
                    dve.tensor_copy(k.expert_b_parts[:, part, :], left)
                    dve.drain()
                    if part < 2:
                        dve.tensor_tensor(bias_rest[:, :], left, k.expert_b_parts[:, part, :], ALU.subtract)
                        dve.drain()
                        left = bias_rest[:, :]
                dve.tensor_copy(k.ident_bf[:, :], k.ident)
                for name, t in (("selector8", sel8), ("selector16", sel16), ("chunk_selector", selc),
                                ("mask", k.mask_bf)):
                    rows, a, b = where["select"][name]
                    dve.tensor_copy(t[:, :], select[0:rows, a:b])
                dve.drain().then_inc(cast, 1)
                dve.wait_ge(cast, 1)

        L0 = {n: piece("L0", n) for n in where["L0"]}
        L0["expert_w"] = L0["expert_w"].rearrange("d (e o) -> d e o", o=D)
        L1 = {n: piece("L1", n) for n in where["L1"]}
        L1["we1"] = L1["we1"].rearrange("d (e c h) -> d e c h", c=4, h=P)
        L1["we2"] = L1["we2"].rearrange("h (e c d) -> h e c d", c=4, d=D)
        L2 = {n: piece("L2", n) for n in where["L2"]}
        L2["gate"] = L2["gate"].rearrange("d (e c h) -> d e c h", c=4, h=P)
        L2["up"] = L2["up"].rearrange("d (e c h) -> d e c h", c=4, h=P)
        L2["down"] = L2["down"].rearrange("h (e c d) -> h e c d", c=4, d=D)
        L2["router_down"] = L2["router_down"].rearrange("h (c e) -> h c e", e=8)
        L3 = {n: piece("L3", n) for n in where["L3"]}
        for n in ("gate", "up", "down"):
            L3[n] = L3[n].rearrange("d (c h) -> d c h", h=P)

        A0 = {n: piece("A0", n) for n in where["A0"]}
        A0["proj"] = A0["proj"].rearrange("d (j c) -> d j c", c=P)
        A0["out"] = A0["out"].rearrange("d (j c) -> d j c", c=D)
        scratch0 = nc.dram_tensor("qkv_chunks", [NCH, P, 12, CH], F32).ap()
        A1 = {n: piece("A1", n) for n in where["A1"]}
        A1["qk"] = A1["qk"].rearrange("d (j c) -> d j c", j=2)
        scratch = (nc.dram_tensor("q_parts", [3, 8, NB, 16, TB], BF16).ap(), nc.dram_tensor("k_parts", [3, 8, 16, T], BF16).ap())
        A3 = {n: piece("A3", n) for n in where["A3"]}
        A2 = {n: piece("A2", n) for n in where["A2"]}
        load = lambda *groups: [(resident[g][:, :], dram[g]) for g in groups]
        run = {
            "L0": lambda loads: top1_ffn(k, L0, loads), "A0": lambda loads: gated_kernel_attention(k, A0, scratch0),
            "L1": lambda loads: top2_silu_ffn(k, L1, loads), "A1": lambda loads: softmax_attention(k, A1, scratch),
            "L2": lambda loads: top2_linear_ffn(k, L2, loads), "A2": lambda loads: window_attention(k, A2),
            "L3": lambda loads: shared_routed_ffn(k, L3, loads), "A3": lambda loads: scan_attention(k, A3),
        }
        for name, groups in stages:
            run[name](load(*groups))

        with nc.Block() as block:
            @block.sync
            def _(sp):
                sp.dma_start(x_out, k.x[:, :]).then_inc(stored, 16)
                sp.wait_ge(stored, 16)



def kernel(**inputs):
    import concourse.bacc as _bacc
    from concourse.bass_utils import run_bass_kernel_spmd as _run

    x = np.ascontiguousarray(inputs["L0_attn_x"][0].T)
    groups = {g: packed(group) for g, group in pieces(**{n: np.asarray(a) for n, a in inputs.items()}).items()}
    arrays = {"in_x": x, **{f"in_{g}": whole for g, (whole, _) in groups.items()}}
    nc = _bacc.Bacc("TRN2", target_bir_lowering=False, num_devices=1)
    args = {n: nc.dram_tensor(n, a.shape, F32, kind="ExternalInput").ap() for n, a in arrays.items()}
    out = nc.dram_tensor("out_0_dram", [P, T], F32, kind="ExternalOutput").ap()
    build(nc, {g: args["in_" + g] for g in groups}, {g: where for g, (_, where) in groups.items()}, args["in_x"], out)
    r = _run(nc, [arrays], core_ids=[0])
    return np.ascontiguousarray(r.results[0]["out_0_dram"].T)[None]
```
